# Optimizing a Trainium2 kernel written in Bass

```python
import numpy as np
import jax
import jax.numpy as jnp

def _softmax(x, axis=-1):
    return jax.nn.softmax(x, axis=axis)

def _gelu(x):
    return jax.nn.gelu(x, approximate=True)

def _silu(x):
    return jax.nn.silu(x)

def _sigmoid(x):
    return jax.nn.sigmoid(x)

def _layernorm(x, axis=-1, eps=1e-05):
    m = jnp.mean(x, axis=axis, keepdims=True)
    v = jnp.var(x, axis=axis, keepdims=True)
    return (x - m) / jnp.sqrt(v + eps)

def _scatter_add(tgt, idx, src, axis=0):
    return tgt.at[idx].add(src)

def _segment_sum(src, seg, n):
    return jax.ops.segment_sum(src, seg, n)
kernel_name = 'mk_gnn_ffn_d2_gnn_r32_034925'

def setup_inputs(seed: int=0):
    np.random.seed(seed)
    _w = jnp.asarray

    def _rec_inputs():
        import jax
        import jax.numpy as jnp
        _gk = jax.random.key(seed)
        x = -0.0003713 + 1 * jax.random.normal(jax.random.fold_in(_gk, 1), (3125, 256), jnp.float32)
        _s = jax.random.randint(jax.random.fold_in(_gk, 2), (25000,), 0, 3125, jnp.int32)
        _d = jax.random.randint(jax.random.fold_in(_gk, 3), (25000,), 0, 3125, jnp.int32)
        _loop = jnp.arange(3125, dtype=jnp.int32)
        src = jnp.concatenate([_s, _d, _loop])
        dst = jnp.concatenate([_d, _s, _loop])
        _o = jnp.argsort(dst, stable=True)
        src = src[_o]
        dst = dst[_o]
        edge_type_16 = jax.random.randint(jax.random.fold_in(_gk, 14), (53125,), 0, 16, jnp.int32)
        edge_weight1 = jax.random.uniform(jax.random.fold_in(_gk, 15), (53125, 1), jnp.float32, 0.0, 1)
        return (x, src, dst, edge_type_16, edge_weight1)
    x, src, dst, edge_type_16, edge_weight1 = _rec_inputs()

    def _L0_gnn_setup():
        import jax, jax.numpy as jnp
        import numpy as np
        N, E = (50000, 25000)
        IN_C, HID_C, OUT_C = (256, 256, 256)

        def _gcn_prep(edge_index, n_nodes):
            src = jnp.concatenate([edge_index[0], jnp.arange(n_nodes, dtype=edge_index.dtype)])
            dst = jnp.concatenate([edge_index[1], jnp.arange(n_nodes, dtype=edge_index.dtype)])
            deg = jax.ops.segment_sum(jnp.ones_like(dst, dtype=jnp.float32), dst, num_segments=n_nodes)
            deg_inv_sqrt = jnp.where(deg > 0, jax.lax.rsqrt(jnp.maximum(deg, 1.0)), 0.0)
            norm = deg_inv_sqrt[src] * deg_inv_sqrt[dst]
            return (src, dst, norm)

        def _gcn_layer(x, src, dst, norm, W, b, n_nodes):
            h = x @ W
            msg = h[src] * norm[:, None]
            out = jax.ops.segment_sum(msg, dst, num_segments=n_nodes)
            return out + b
        key = jax.random.key(seed)
        ks = jax.random.split(key, 8)
        x_piece = jax.random.normal(ks[0], (N, IN_C), dtype=jnp.float32)
        edge_index_piece = jax.random.randint(ks[1], (2, E), 0, N, dtype=jnp.int64)
        batch = jnp.zeros((N,), dtype=jnp.int64)

        def glorot(k, fan_in, fan_out):
            s = jnp.sqrt(6.0 / (fan_in + fan_out)).astype(jnp.float32)
            return jax.random.uniform(k, (fan_in, fan_out), jnp.float32, -s, s)
        return {'x_piece': x_piece, 'edge_index_piece': edge_index_piece, 'batch': batch, 'W1': glorot(ks[2], IN_C, HID_C), 'b1': jnp.zeros((HID_C,), jnp.float32), 'W2': glorot(ks[3], HID_C, HID_C), 'b2': jnp.zeros((HID_C,), jnp.float32), 'W3': glorot(ks[4], HID_C, OUT_C), 'b3': jnp.zeros((OUT_C,), jnp.float32)}
    _L0_gnn_all = _L0_gnn_setup()
    _L0_gnn_in = {k: v for k, v in _L0_gnn_all.items() if k in ('W1', 'b1', 'W2', 'b2', 'W3', 'b3')}
    del _L0_gnn_all

    def _L0_ffn_setup():
        import jax, jax.numpy as jnp
        import numpy as np
        BN_EPS = 0.001

        def _bn(h, g, b, m, v):
            return g * (h - m) * jax.lax.rsqrt(v + BN_EPS) + b
        key = jax.random.key(seed)
        ks = jax.random.split(key, 8)
        B, F, Df = (256, 64, 256)
        E, H, D = (8, 256, 256)
        s1 = 1.0 / np.sqrt(Df)
        s2 = 1.0 / np.sqrt(H)
        return {'x': jax.random.normal(ks[0], (B, F, Df), jnp.float32), 'Wr': jax.random.normal(ks[1], (Df, E), jnp.float32) * s1, 'br': jnp.zeros((E,), jnp.float32), 'W1': jax.random.normal(ks[2], (E, Df, H), jnp.float32) * s1, 'b1': jnp.zeros((E, H), jnp.float32), 'g1': jnp.ones((E, H), jnp.float32), 'be1': jnp.zeros((E, H), jnp.float32), 'm1': jnp.zeros((E, H), jnp.float32), 'v1': jnp.ones((E, H), jnp.float32), 'W2': jax.random.normal(ks[3], (E, H, H), jnp.float32) * s2, 'b2': jnp.zeros((E, H), jnp.float32), 'g2': jnp.ones((E, H), jnp.float32), 'be2': jnp.zeros((E, H), jnp.float32), 'm2': jnp.zeros((E, H), jnp.float32), 'v2': jnp.ones((E, H), jnp.float32), 'Wo': jax.random.normal(ks[4], (E, H, D), jnp.float32) * s2, 'bo': jnp.zeros((E, D), jnp.float32)}
    _L0_ffn_all = _L0_ffn_setup()
    _L0_ffn_in = {k: v for k, v in _L0_ffn_all.items() if k in ('Wr', 'br', 'W1', 'b1', 'g1', 'be1', 'm1', 'v1', 'W2', 'b2', 'g2', 'be2', 'm2', 'v2', 'Wo', 'bo')}
    del _L0_ffn_all

    def _L1_gnn_setup():
        import jax, jax.numpy as jnp
        import numpy as np
        N_NODES = 50000
        N_EDGES = 25000
        NUM_RELS = 16
        FEAT = 256
        OUT = 256
        key = jax.random.key(seed)
        ks = jax.random.split(key, 7)
        h = jax.random.normal(ks[0], (N_NODES, FEAT), dtype=jnp.float32)
        norm = jax.random.uniform(ks[1], (N_EDGES, 1), dtype=jnp.float32)
        weight = jax.random.normal(ks[2], (NUM_RELS, FEAT, OUT), dtype=jnp.float32) * 0.05
        gate_weight = jax.random.normal(ks[3], (NUM_RELS, FEAT, 1), dtype=jnp.float32) * 0.05
        src = jax.random.randint(ks[4], (N_EDGES,), 0, N_NODES)
        dst = jax.random.randint(ks[5], (N_EDGES,), 0, N_NODES)
        rel_type = jax.random.randint(ks[6], (N_EDGES,), 0, NUM_RELS)
        return {'h': h, 'norm': norm, 'weight': weight, 'gate_weight': gate_weight, 'src': src, 'dst': dst, 'rel_type': rel_type}
    _L1_gnn_all = _L1_gnn_setup()
    _L1_gnn_in = {k: v for k, v in _L1_gnn_all.items() if k in ('weight', 'gate_weight')}
    del _L1_gnn_all

    def _L1_ffn_setup():
        import math
        import jax, jax.numpy as jnp
        import numpy as np
        CAPACITY_FACTOR = 1.25
        TOP_K = 2
        LN_EPS = 1e-05

        def _layer_norm(x, gamma, beta):
            mu = jnp.mean(x, axis=-1, keepdims=True)
            var = jnp.var(x, axis=-1, keepdims=True)
            return (x - mu) * jax.lax.rsqrt(var + LN_EPS) * gamma + beta
        key = jax.random.key(seed)
        ks = jax.random.split(key, 4)
        B, S, D, F, E = (8, 128, 256, 512, 8)
        x = jax.random.normal(ks[0], (B, S, D), dtype=jnp.float32)
        Wr = jax.random.normal(ks[1], (D, E), dtype=jnp.float32) / np.sqrt(D)
        br = jnp.zeros((E,), jnp.float32)
        W1 = jax.random.normal(ks[2], (E, D, F), dtype=jnp.float32) / np.sqrt(D)
        b1 = jnp.zeros((E, F), jnp.float32)
        W2 = jax.random.normal(ks[3], (E, F, D), dtype=jnp.float32) / np.sqrt(F)
        b2 = jnp.zeros((E, D), jnp.float32)
        gamma = jnp.ones((D,), jnp.float32)
        beta = jnp.zeros((D,), jnp.float32)
        return {'x': x, 'Wr': Wr, 'br': br, 'W1': W1, 'b1': b1, 'W2': W2, 'b2': b2, 'gamma': gamma, 'beta': beta}
    _L1_ffn_all = _L1_ffn_setup()
    _L1_ffn_in = {k: v for k, v in _L1_ffn_all.items() if k in ('Wr', 'br', 'W1', 'b1', 'W2', 'b2', 'gamma', 'beta')}
    del _L1_ffn_all
    return {'x': x, 'src': src, 'dst': dst, 'edge_type_16': edge_type_16, 'edge_weight1': edge_weight1, 'L0_gnn_W1': _L0_gnn_in['W1'], 'L0_gnn_b1': _L0_gnn_in['b1'], 'L0_gnn_W2': _L0_gnn_in['W2'], 'L0_gnn_b2': _L0_gnn_in['b2'], 'L0_gnn_W3': _L0_gnn_in['W3'], 'L0_gnn_b3': _L0_gnn_in['b3'], 'L0_ffn_Wr': _L0_ffn_in['Wr'], 'L0_ffn_br': _L0_ffn_in['br'], 'L0_ffn_W1': _L0_ffn_in['W1'], 'L0_ffn_b1': _L0_ffn_in['b1'], 'L0_ffn_g1': _L0_ffn_in['g1'], 'L0_ffn_be1': _L0_ffn_in['be1'], 'L0_ffn_m1': _L0_ffn_in['m1'], 'L0_ffn_v1': _L0_ffn_in['v1'], 'L0_ffn_W2': _L0_ffn_in['W2'], 'L0_ffn_b2': _L0_ffn_in['b2'], 'L0_ffn_g2': _L0_ffn_in['g2'], 'L0_ffn_be2': _L0_ffn_in['be2'], 'L0_ffn_m2': _L0_ffn_in['m2'], 'L0_ffn_v2': _L0_ffn_in['v2'], 'L0_ffn_Wo': _L0_ffn_in['Wo'], 'L0_ffn_bo': _L0_ffn_in['bo'], 'L1_gnn_weight': _L1_gnn_in['weight'], 'L1_gnn_gate_weight': _L1_gnn_in['gate_weight'], 'L1_ffn_Wr': _L1_ffn_in['Wr'], 'L1_ffn_br': _L1_ffn_in['br'], 'L1_ffn_W1': _L1_ffn_in['W1'], 'L1_ffn_b1': _L1_ffn_in['b1'], 'L1_ffn_W2': _L1_ffn_in['W2'], 'L1_ffn_b2': _L1_ffn_in['b2'], 'L1_ffn_gamma': _L1_ffn_in['gamma'], 'L1_ffn_beta': _L1_ffn_in['beta']}

def reference(x, src, dst, edge_type_16, edge_weight1, L0_gnn_W1, L0_gnn_b1, L0_gnn_W2, L0_gnn_b2, L0_gnn_W3, L0_gnn_b3, L0_ffn_Wr, L0_ffn_br, L0_ffn_W1, L0_ffn_b1, L0_ffn_g1, L0_ffn_be1, L0_ffn_m1, L0_ffn_v1, L0_ffn_W2, L0_ffn_b2, L0_ffn_g2, L0_ffn_be2, L0_ffn_m2, L0_ffn_v2, L0_ffn_Wo, L0_ffn_bo, L1_gnn_weight, L1_gnn_gate_weight, L1_ffn_Wr, L1_ffn_br, L1_ffn_W1, L1_ffn_b1, L1_ffn_W2, L1_ffn_b2, L1_ffn_gamma, L1_ffn_beta):
    import jax
    import jax.numpy as jnp

    def _L0_gnn_ref(x_piece, edge_index_piece, batch, W1, b1, W2, b2, W3, b3):
        import jax, jax.numpy as jnp
        import numpy as np
        N, E = (50000, 25000)
        IN_C, HID_C, OUT_C = (256, 256, 256)

        def _gcn_prep(edge_index, n_nodes):
            src = jnp.concatenate([edge_index[0], jnp.arange(n_nodes, dtype=edge_index.dtype)])
            dst = jnp.concatenate([edge_index[1], jnp.arange(n_nodes, dtype=edge_index.dtype)])
            deg = jax.ops.segment_sum(jnp.ones_like(dst, dtype=jnp.float32), dst, num_segments=n_nodes)
            deg_inv_sqrt = jnp.where(deg > 0, jax.lax.rsqrt(jnp.maximum(deg, 1.0)), 0.0)
            norm = deg_inv_sqrt[src] * deg_inv_sqrt[dst]
            return (src, dst, norm)

        def _gcn_layer(x, src, dst, norm, W, b, n_nodes):
            h = x @ W
            msg = h[src] * norm[:, None]
            out = jax.ops.segment_sum(msg, dst, num_segments=n_nodes)
            return out + b
        n_nodes = x_piece.shape[0]
        src, dst, norm = _gcn_prep(edge_index_piece, n_nodes)
        x = _gcn_layer(x_piece, src, dst, norm, W1, b1, n_nodes)
        x = jax.nn.gelu(x)
        x = _gcn_layer(x, src, dst, norm, W2, b2, n_nodes)
        x = jax.nn.gelu(x)
        x = _gcn_layer(x, src, dst, norm, W3, b3, n_nodes)
        return x

    def _L0_ffn_ref(x, Wr, br, W1, b1, g1, be1, m1, v1, W2, b2, g2, be2, m2, v2, Wo, bo):
        import jax, jax.numpy as jnp
        import numpy as np
        BN_EPS = 0.001

        def _bn(h, g, b, m, v):
            return g * (h - m) * jax.lax.rsqrt(v + BN_EPS) + b
        feat = jnp.mean(x, axis=0)
        w = jax.nn.softmax(feat @ Wr + br, axis=-1)
        h = jnp.einsum('bfd,edh->bfeh', x, W1) + b1
        h = jax.nn.relu(_bn(h, g1, be1, m1, v1))
        h = jnp.einsum('bfeh,ehk->bfek', h, W2) + b2
        h = jax.nn.relu(_bn(h, g2, be2, m2, v2))
        y = jnp.einsum('bfeh,ehd->bfed', h, Wo) + bo
        return jnp.einsum('bfed,fe->bfd', y, w)

    def _L1_gnn_ref(h, norm, weight, gate_weight, src, dst, rel_type):
        import jax, jax.numpy as jnp
        import numpy as np
        N_NODES = 50000
        N_EDGES = 25000
        NUM_RELS = 16
        FEAT = 256
        OUT = 256
        n_nodes = h.shape[0]
        all_msg = jnp.einsum('nf,rfo->rno', h, weight)
        msg = all_msg[rel_type, src] * norm
        all_gate = jnp.einsum('nf,rf->rn', h, gate_weight[..., 0])
        gate = jax.nn.sigmoid(all_gate[rel_type, src])[:, None]
        msg = msg * gate
        agg = jax.ops.segment_sum(msg, dst, num_segments=n_nodes)
        return jax.nn.relu(agg)

    def _L1_ffn_ref(x, Wr, br, W1, b1, W2, b2, gamma, beta):
        import math
        import jax, jax.numpy as jnp
        import numpy as np
        CAPACITY_FACTOR = 1.25
        TOP_K = 2
        LN_EPS = 1e-05

        def _layer_norm(x, gamma, beta):
            mu = jnp.mean(x, axis=-1, keepdims=True)
            var = jnp.var(x, axis=-1, keepdims=True)
            return (x - mu) * jax.lax.rsqrt(var + LN_EPS) * gamma + beta
        B, S, D = x.shape
        E = Wr.shape[1]
        N = B * S
        K = TOP_K
        logits = jnp.mean(x, axis=1) @ Wr + br
        routing_weights = jax.nn.softmax(logits, axis=-1)
        capacity = float(math.ceil(N * CAPACITY_FACTOR / E))
        expected_loads = routing_weights.sum(axis=0) * (N / B)
        scale = jnp.where(expected_loads > capacity, capacity / expected_loads, 1.0)
        routing_weights = jax.nn.softmax(routing_weights * scale, axis=-1)
        rw_tok = jnp.broadcast_to(routing_weights[:, None, :], (B, S, E)).reshape(N, E)
        top_w, top_i = jax.lax.top_k(rw_tok, K)
        top_w = jax.nn.softmax(top_w, axis=-1)
        xf = x.reshape(N, D)
        h = jax.nn.gelu(jnp.einsum('nd,edf->enf', xf, W1) + b1[:, None, :], approximate=False)
        y = jnp.einsum('enf,efd->end', h, W2) + b2[:, None, :]
        w_dense = jnp.zeros((N, E), x.dtype).at[jnp.arange(N)[:, None], top_i].add(top_w)
        out = jnp.einsum('ne,end->nd', w_dense, y).reshape(B, S, D)
        out = _layer_norm(out + x, gamma, beta)
        return out
    edge_index = jnp.stack([src, dst])
    batch0 = jnp.zeros((3125,), jnp.int32)
    x = x + _L0_gnn_ref(_layernorm(x, axis=-1), edge_index, batch0, L0_gnn_W1, L0_gnn_b1, L0_gnn_W2, L0_gnn_b2, L0_gnn_W3, L0_gnn_b3)
    x = x + _L0_ffn_ref(_layernorm(x, axis=-1)[None], L0_ffn_Wr, L0_ffn_br, L0_ffn_W1, L0_ffn_b1, L0_ffn_g1, L0_ffn_be1, L0_ffn_m1, L0_ffn_v1, L0_ffn_W2, L0_ffn_b2, L0_ffn_g2, L0_ffn_be2, L0_ffn_m2, L0_ffn_v2, L0_ffn_Wo, L0_ffn_bo)[0]
    x = x + _L1_gnn_ref(_layernorm(x, axis=-1), edge_weight1, L1_gnn_weight, L1_gnn_gate_weight, src, dst, edge_type_16)
    x = x + _L1_ffn_ref(_layernorm(x, axis=-1)[None], L1_ffn_Wr, L1_ffn_br, L1_ffn_W1, L1_ffn_b1, L1_ffn_W2, L1_ffn_b2, L1_ffn_gamma, L1_ffn_beta)[0]
    return x

_drawn_inputs = setup_inputs


def setup_inputs(seed=0):
    import zlib

    import numpy as np

    out = dict(_drawn_inputs(seed))
    spreads = {'L0_gnn_b1': (0.0, 0.277),
     'L0_gnn_b2': (0.0, 0.1),
     'L0_gnn_b3': (0.0, 0.1),
     'L0_ffn_br': (0.0, 0.1),
     'L0_ffn_b1': (0.0, 0.303),
     'L0_ffn_g1': (1.0, 0.2),
     'L0_ffn_be1': (0.0, 0.309),
     'L0_ffn_m1': (0.0, 0.3),
     'L0_ffn_v1': (1.0, 0.585),
     'L0_ffn_b2': (0.0, 0.1),
     'L0_ffn_g2': (1.0, 0.2),
     'L0_ffn_be2': (0.0, 0.1),
     'L0_ffn_m2': (0.0, 0.1),
     'L0_ffn_v2': (1.0, 0.2),
     'L0_ffn_bo': (0.0, 0.1),
     'L1_ffn_br': (0.0, 0.8),
     'L1_ffn_b1': (0.0, 0.404),
     'L1_ffn_b2': (0.0, 0.293),
     'L1_ffn_gamma': (1.0, 0.2),
     'L1_ffn_beta': (0.0, 0.1)}
    factors = {'L0_gnn_W1': 4.424}
    for name, (base, spread) in spreads.items():
        noise = np.random.default_rng([zlib.crc32(name.encode()), seed]).standard_normal(out[name].shape)
        drawn = base * np.exp(spread * noise) if base else spread * noise
        out[name] = jnp.asarray(drawn.astype(out[name].dtype))
    for name, factor in factors.items():
        out[name] = (out[name] * factor).astype(out[name].dtype)
    return out
```

```python
from contextlib import ExitStack

import concourse.bass as bass
from concourse import mybir
from concourse.alu_op_type import AluOpType as ALU

F32 = mybir.dt.float32
BF16 = mybir.dt.bfloat16
I32 = mybir.dt.int32
ACT = mybir.ActivationFunctionType
AX_X = mybir.AxisListType.X

P = 128
N_NODES = 3125
N_EDGES = 53125
D = 256
HALVES = D // P
TILES = -(-N_NODES // P)
ROWS = TILES * P
TAIL = N_NODES - (TILES - 1) * P
CHUNK = 5
CHUNKS = TILES // CHUNK
UNITS = -(-CHUNK // 2)
CROWS = CHUNK * P
NH = CROWS // 2
GE = 8
GROUP = GE * P
GROUPS = -(-N_EDGES // GROUP)
GTAIL = N_EDGES - (GROUPS - 1) * GROUP
RING = 4
RELS = 16
E0 = 8
F1 = 512
FT = F1 // P
TOP_K = 2
LN_EPS = 1e-5
BN_EPS = 1e-3
AGGS = 4
BIG = 4096.0
CAPACITY = float(-(-(N_NODES * 5) // (4 * E0)))


class Chain:

    def __init__(self, eng, sem):
        self.eng, self.sem, self.n, self.base = eng, sem, 0, 0

    def done(self, ins):
        ins.then_inc(self.sem, 1)
        self.n += 1
        self.eng.wait_ge(self.sem, self.base + self.n)

    def loop(self, turn, per_turn):
        self.base = turn * per_turn

    def end(self, turns, per_turn):
        self.base = 0
        self.n += (turns - 1) * per_turn


def build(nc, a, out):
    with ExitStack() as ctx:
        _build(nc, a, out, ctx)


def _build(nc, a, out, ctx):
    def sb(name, shape, dt=F32):
        return ctx.enter_context(nc.sbuf_tensor(name, shape, dt))

    def sem(name):
        return ctx.enter_context(nc.semaphore(name))

    gcn_table = [nc.dram_tensor(f"gcn_table{l}", (ROWS, D), F32).ap() for l in range(3)]
    rel_table = nc.dram_tensor("rel_table", (ROWS * RELS, D), F32).ap()

    x_res = sb("x_res", [P, TILES, D])
    xn = sb("xn", [P, TILES, D])
    xt = sb("xt", [P, HALVES, ROWS + P])
    union = sb("union", [P, 10240])
    ring = union[:, 0:8192].rearrange("p (s j f) -> p s j f", s=RING, j=GE)
    onehot = union[:, 8192:10240].rearrange("p (s j w) -> p s j w", s=2, j=GE)
    h1 = union[:, 0:1280].rearrange("p (m n) -> p m n", m=2)
    h2 = union[:, 1280:2560].rearrange("p (m n) -> p m n", m=2)
    bob = union[:, 2560:4608].rearrange("p (e f) -> p e f", e=E0)
    stage = union[:, 0:8192].rearrange("p (s r f) -> p s r f", s=2, r=RELS)
    hh = union[:, 0:5120].rearrange("p (s m n) -> p s m n", s=2, m=FT)
    lo1h = union[:, 0:1024].bitcast(BF16).rearrange("p (s j w) -> p s j w", s=2, j=GE)
    hi1h = union[:, 1024:1024 + 256].bitcast(BF16)[:, 0:2 * GE * TILES].rearrange("p (s j w) -> p s j w", s=2, j=GE)
    edge_i = union[:, 2048:6144].bitcast(I32).rearrange("p (k e) -> p k e", k=4)
    edge_f = union[:, 6144:10240].rearrange("p (k e) -> p k e", k=4)

    gw = sb("gw", [P, 3, HALVES, D])
    gb = sb("gb", [P, 3, D])
    weights = sb("weights", [P, 3, E0 * HALVES * D])
    wa, wb, wc = (weights[:, i, :].rearrange("p (e k f) -> p e k f", e=E0, k=HALVES) for i in range(3))
    rw = weights[:, 0:2, :].rearrange("p k (r f) -> p k r f", r=RELS)
    rg = sb("rg", [P, HALVES, RELS])
    s1 = weights[:, 2, 0:2048].rearrange("p (s k f) -> p s k f", s=TOP_K, k=HALVES)
    s2 = weights[:, 2, 2048:4096].rearrange("p (s k f) -> p s k f", s=TOP_K, k=FT)

    ident = sb("ident", [P, P])
    ones = sb("ones", [P, P])
    iota_w = sb("iota_w", [P, P])
    zero_bf = sb("zero_bf", [P, P], BF16)
    tail_one = sb("tail_one", [P, 2])
    dstc = sb("dstc", [P, GROUPS, GE])
    wgtc = sb("wgtc", [P, GROUPS, GE])
    scratch = xn[:, :, :].rearrange("p t f -> p (t f)")
    tmpc = scratch[:, 0:4 * GROUPS * GE].rearrange("p (k g j) -> p k g j", k=4, j=GE)
    tmpci = scratch[:, 1664:1664 + 3 * GROUPS * GE].bitcast(I32).rearrange("p (k g j) -> p k g j", k=3, j=GE)
    tmpe = scratch[:, 4096:6144].rearrange("p (k e) -> p k e", k=2)
    rel_dst = sb("rel_dst", [P, GROUPS, GE])
    idx_src = sb("idx_src", [P, GROUPS + 1, GE], I32)
    idx_rel = sb("idx_rel", [P, GROUPS + 1, GE], I32)
    idx_ring = sb("idx_ring", [P, AGGS, RING, GE], I32)
    base0 = sb("base0", [P, GROUPS])
    base_f = sb("base_f", [P, GROUPS])
    base_i = sb("base_i", [P, GROUPS], I32)
    gstat = sb("gstat", [P, 4])
    gspread = sb("gspread", [P, 2, P])
    span_i = sb("span_i", [P, GROUPS], I32)
    npass_f = sb("npass_f", [P, 2])
    npass = sb("npass", [P, 2], I32)
    dinv = sb("dinv", [P, TILES])
    xr = sb("xr", [P, 2, HALVES, P])
    stats = sb("stats", [P, TILES, 6])
    mean = sb("mean", [P, TILES])
    rstd = sb("rstd", [P, TILES])
    rscale = sb("rscale", [P, TILES])
    wr0 = sb("wr0", [P, HALVES, E0])
    br0 = sb("br0", [1, E0])
    rout = sb("rout", [P, TILES, E0])
    rtmp = sb("rtmp", [P, TILES])
    bnp = sb("bnp", [80, 2, P])
    bnc = sb("bnc", [P, 2, 5, 16])
    bn_s = sb("bn_s", [P, 2, 16])
    bn_t = sb("bn_t", [P, 2, 16])
    gates = sb("gates", [P, TILES, RELS])
    wr1 = sb("wr1", [P, HALVES, E0])
    small = sb("small", [1, 12, E0])
    iota8 = sb("iota8", [1, E0])
    sel_i = sb("sel_i", [1, 4], I32)
    mean_t = sb("mean_t", [P, HALVES])
    b1s = sb("b1s", [FT, TOP_K, P])
    b1c = sb("b1c", [P, TOP_K, FT])
    b2s = sb("b2s", [1, TOP_K, D])
    wsel = sb("wsel", [P, TOP_K])
    b2m = sb("b2m", [1, 2, D])
    gam = sb("gam", [P, D])
    bet = sb("bet", [P, D])

    ps = ctx.enter_context(nc.psum_tensor("ps", [P, 8, 512], F32))

    ld_edges, ld_x, ld_gcn, ld_mix, ld_rel, ld_mix2 = (sem("ld_" + n) for n in ("edges", "x", "gcn", "mix", "rel", "mix2"))
    consts = sem("consts")
    dve_chain, act_chain = sem("dve_chain"), sem("act_chain")
    edges_f = sem("edges_f")
    edges_tr = sem("edges_tr")
    edges_ev = sem("edges_ev")
    gstat_ready = sem("gstat_ready")
    gspread_mm = sem("gspread_mm")
    plan_ready = sem("plan_ready")
    deg_in, deg_sd, gcn_added, bo_added = sem("deg_in"), sem("deg_sd"), sem("gcn_added"), sem("bo_added")
    hist_1h, hist_mm, hist_done = sem("hist_1h"), sem("hist_mm"), sem("hist_done")
    ln_stats = [sem(f"ln_stats{i}") for i in range(5)]
    ln_var = [sem(f"ln_var{i}") for i in range(5)]
    ln_sd = [sem(f"ln_sd{i}") for i in range(5)]
    ln_row = [sem(f"ln_row{i}") for i in range(4)]
    tr_mm = [sem(f"tr_mm{i}") for i in range(6)]
    tr_ev = [sem(f"tr_ev{i}") for i in range(6)]
    table_out = [sem(f"table_out{i}") for i in range(4)]
    idx_copied = [sem(f"idx_copied{i}") for i in range(AGGS)]
    gathered = [[sem(f"gathered{i}_{s}") for s in range(RING)] for i in range(AGGS)]
    onehot_ready = [sem(f"onehot_ready{i}") for i in range(AGGS)]
    group_mm = [sem(f"group_mm{i}") for i in range(AGGS)]
    agg_added = [sem(f"agg_added{i}") for i in range(AGGS)]
    pass_base = [sem(f"pass_base{i}") for i in range(AGGS)]
    agg_done = [sem(f"agg_done{i}") for i in range(AGGS)]
    y_mm = [sem(f"y_mm{i}") for i in range(3)]
    y_ev = [sem(f"y_ev{i}") for i in range(3)]
    row_ready = [sem(f"row_ready{i}") for i in range(2)]
    gelu_done = [sem(f"gelu_done{i}") for i in range(2)]
    rout_mm, rout_max, rout_exp, rout_ready = (sem("rout_" + n) for n in ("mm", "max", "exp", "ready"))
    ld_bo = sem("ld_bo")
    bn_tr, bn_ev, bn_var, bn_sd, bn_ready = (sem("bn_" + n) for n in ("tr", "ev", "var", "sd", "ready"))
    l1_mm, l1_ev, l2_mm, l2_ev, yo_mm, yo_ev = (sem(n) for n in ("l1_mm", "l1_ev", "l2_mm", "l2_ev", "yo_mm", "yo_ev"))
    xr_copied = sem("xr_copied")
    gate_mm, gate_ready = sem("gate_mm"), sem("gate_ready")
    rel_mm, rel_ev_a, rel_ev_v, rel_out = sem("rel_mm"), sem("rel_ev_a"), sem("rel_ev_v"), [sem("rel_out0"), sem("rel_out1")]
    back_mm, back_ev = sem("back_mm"), sem("back_ev")
    mean_mm, mean_ev, log_mm, exp_in, exp_out = (sem(n) for n in ("mean_mm", "mean_ev", "log_mm", "exp_in", "exp_out"))
    sel_ready, sel_ld, sel_tr, sel_ev, wsel_in, wsel_mm, wsel_ev = (
        sem(n) for n in ("sel_ready", "sel_ld", "sel_tr", "sel_ev", "wsel_in", "wsel_mm", "wsel_ev"))
    b2_ready, w2_scaled = sem("b2_ready"), sem("w2_scaled")
    hid_mm, hid_ev, fo_mm, fo_ev, fin_ready, out_done = (
        sem(n) for n in ("hid_mm", "hid_ev", "fo_mm", "fo_ev", "fin_ready", "out_done"))

    block = ctx.enter_context(nc.Block())

    @block.sync
    def _(sp):
        for k, name in enumerate(("dst", "src", "edge_type_16")):
            sp.wait_ge(consts, 4)
            sp.dma_start(edge_i[0:GROUPS - 1, k, :],
                         a[name][0:(GROUPS - 1) * GROUP].rearrange("(g e) -> g e", g=GROUPS - 1)).then_inc(ld_edges, 16)
            sp.dma_start(edge_i[GROUPS - 1:GROUPS, k, 0:GTAIL],
                         a[name][(GROUPS - 1) * GROUP:N_EDGES].rearrange("(g e) -> g e", g=1)).then_inc(ld_edges, 16)
        sp.dma_start(edge_f[0:GROUPS - 1, 3, :], a["edge_weight1"][0:(GROUPS - 1) * GROUP, :]
                     .rearrange("(g e) o -> g (e o)", g=GROUPS - 1)).then_inc(ld_edges, 16)
        sp.dma_start(edge_f[GROUPS - 1:GROUPS, 3, 0:GTAIL], a["edge_weight1"][(GROUPS - 1) * GROUP:N_EDGES, :]
                     .rearrange("(g e) o -> g (e o)", g=1)).then_inc(ld_edges, 16)
        sp.dma_start(x_res[:, 0:TILES - 1, :],
                     a["x"][0:(TILES - 1) * P, :].rearrange("(t p) f -> p t f", p=P)).then_inc(ld_x, 16)
        sp.dma_start(x_res[0:TAIL, TILES - 1, :], a["x"][(TILES - 1) * P:N_NODES, :]).then_inc(ld_x, 16)
        for l in range(3):
            sp.dma_start(gw[:, l, :, :], a[f"L0_gnn_W{l + 1}"].rearrange("(k p) f -> p k f", p=P)).then_inc(ld_gcn, 16)
            sp.dma_start(gb[:, l, :], a[f"L0_gnn_b{l + 1}"].partition_broadcast(P)).then_inc(ld_gcn, 16)
        for w, name in ((wa, "L0_ffn_W1"), (wb, "L0_ffn_W2"), (wc, "L0_ffn_Wo")):
            for e in range(E0):
                sp.dma_start(w[:, e, :, :], a[name][e].rearrange("(k p) f -> p k f", p=P)).then_inc(ld_mix, 16)
        for q, names in enumerate((("b1", "g1", "be1", "m1", "v1"), ("b2", "g2", "be2", "m2", "v2"))):
            for n, name in enumerate(names):
                sp.dma_start(bnp[n * 16:(n + 1) * 16, q, :],
                             a["L0_ffn_" + name].rearrange("e (h p) -> (e h) p", p=P)).then_inc(ld_mix, 16)
        sp.dma_start(wr0[:, :, :], a["L0_ffn_Wr"].rearrange("(k p) e -> p k e", p=P)).then_inc(ld_mix, 16)
        sp.dma_start(br0[:, :], a["L0_ffn_br"].rearrange("(o e) -> o e", o=1)).then_inc(ld_mix, 16)
        for k in range(HALVES):
            sp.dma_start(rg[:, k, :], a["L1_gnn_gate_weight"][:, k * P:(k + 1) * P, :].rearrange("r p o -> p (r o)"),
                         allow_slow_non_contiguous=True).then_inc(ld_rel, 16)
        sp.dma_start(wr1[:, :, :], a["L1_ffn_Wr"].rearrange("(k p) e -> p k e", p=P)).then_inc(ld_mix2, 16)
        sp.dma_start(small[:, 0, :], a["L1_ffn_br"].rearrange("(o e) -> o e", o=1)).then_inc(ld_mix2, 16)
        sp.dma_start(gam[:, :], a["L1_ffn_gamma"].partition_broadcast(P)).then_inc(ld_mix2, 16)
        sp.dma_start(bet[:, :], a["L1_ffn_beta"].partition_broadcast(P)).then_inc(ld_mix2, 16)

        for l in range(3):
            ready = ln_row[0] if l == 0 else row_ready[l - 1]
            with sp.Fori(0, TILES) as k:
                sp.wait_ge(ready, k + 1)
                sp.dma_start(gcn_table[l][bass.ds(k * P, P), :], xn[:, k, :]).then_inc(table_out[l], 16)
        sp.wait_ge(agg_done[2], 1)
        sp.dma_start(bob[:, :, :], a["L0_ffn_bo"].partition_broadcast(P)).then_inc(ld_bo, 16)
        sp.wait_ge(l2_mm, CHUNKS * E0 * 2)
        for r in range(RELS):
            sp.dma_start(rw[:, :, r, :], a["L1_gnn_weight"][r].rearrange("(k p) f -> p k f", p=P)).then_inc(ld_rel, 16)
        def rel_rows(k, s, n):
            sp.wait_ge(rel_ev_a, k * 4 + 8)
            sp.wait_ge(rel_ev_v, k * 4 + 8)
            sp.dma_start(rel_table[bass.ds(k * P * RELS, P * RELS), :].rearrange("(p r) f -> p r f", r=RELS),
                         stage[:, s, :, :]).then_inc(rel_out[s], 16)
        with sp.Fori(0, TILES // 2) as k2:
            rel_rows(k2 * 2, 0, k2)
            rel_rows(k2 * 2 + 1, 1, k2)
        rel_rows(TILES - 1, 0, TILES // 2)

        sp.wait_ge(sel_ready, 1)
        for s in range(TOP_K):
            e = sp.value_load(sel_i[0:1, s:s + 1], min_val=0, max_val=E0 - 1)
            sp.dma_start(s1[:, s, :, :], a["L1_ffn_W1"][bass.ds(e, 1), :, :]
                         .rearrange("o (k p) f -> p (o k) f", p=P)).then_inc(sel_ld, 16)
            sp.dma_start(s2[:, s, :, :], a["L1_ffn_W2"][bass.ds(e, 1), :, :]
                         .rearrange("o (k p) f -> p (o k) f", p=P)).then_inc(sel_ld, 16)
            sp.dma_start(b1s[:, s, :], a["L1_ffn_b1"][bass.ds(e, 1), :]
                         .rearrange("o (k p) -> (o k) p", p=P)).then_inc(sel_ld, 16)
            sp.dma_start(b2s[:, s, :], a["L1_ffn_b2"][bass.ds(e, 1), :]).then_inc(sel_ld, 16)
        with sp.Fori(0, TILES - 1) as k:
            sp.wait_ge(fin_ready, k + 1)
            sp.dma_start(out[bass.ds(k * P, P), :], x_res[:, k, :]).then_inc(out_done, 16)
        sp.wait_ge(fin_ready, TILES)
        sp.dma_start(out[(TILES - 1) * P:N_NODES, :], x_res[0:TAIL, TILES - 1, :]).then_inc(out_done, 16)
        sp.wait_ge(out_done, 16 * TILES)

    @block.gpsimd
    def _(g):
        g.memset(edge_i[:, 0, :], -1).then_inc(consts, 1)
        g.memset(edge_i[:, 1:4, :], 0).then_inc(consts, 1)
        g.memset(edge_f[:, 3, :], 0.0).then_inc(consts, 1)
        g.memset(x_res[:, TILES - 1, :], 0.0).then_inc(consts, 1)
        g.memset(xt[:, :, ROWS:], 0.0).then_inc(consts, 1)
        g.iota(iota_w[:, :], [[1, P]], base=0, channel_multiplier=0,
               allow_small_or_imprecise_dtypes=True).then_inc(consts, 1)
        g.iota(iota8[:, :], [[1, E0]], base=0, channel_multiplier=0,
               allow_small_or_imprecise_dtypes=True).then_inc(consts, 1)
        g.memset(ones[:, :], 1.0).then_inc(consts, 1)
        g.memset(zero_bf[:, :], 0.0).then_inc(consts, 1)
        g.wait_ge(consts, 8)
        g.affine_select(out=ident[:, :], in_=ones[:, :], compare_op=ALU.is_equal, fill=0.0,
                        base=0, pattern=[[-1, P]], channel_multiplier=1).then_inc(consts, 1)
        g.affine_select(out=tail_one[:, :], in_=ones[:, 0:2], compare_op=ALU.is_ge, fill=0.0,
                        base=TAIL - 1, pattern=[[0, 2]], channel_multiplier=-1).then_inc(consts, 1)

        for l in range(AGGS):
            table = gcn_table[l] if l < 3 else rel_table
            idx = idx_src if l < 3 else idx_rel
            if l == 0:
                g.wait_ge(plan_ready, 1)
                passes = g.value_load(npass[0:1, 0:1], min_val=1, max_val=26)
            if l < 3:
                g.wait_ge(table_out[l], 16 * TILES)
            else:
                g.wait_ge(tr_ev[4], CHUNK + TILES)
                for s in range(2):
                    g.tensor_copy(xr[:, s, :, :], xt[:, :, s * P:(s + 1) * P]).then_inc(xr_copied, 1)
                with g.Fori(1, TILES // 2) as k2:
                    for s in range(2):
                        k = k2 * 2 + s
                        g.wait_ge(rel_mm, (k - 1) * 8)
                        g.tensor_copy(xr[:, s, :, :], xt[:, :, bass.ds(k * P, P)]).then_inc(xr_copied, 1)
                g.wait_ge(rel_mm, (TILES - 2) * 8)
                g.tensor_copy(xr[:, 0, :, :], xt[:, :, ROWS - P:ROWS]).then_inc(xr_copied, 1)
                g.wait_ge(rel_out[0], 16 * (TILES // 2 + 1))
                g.wait_ge(rel_out[1], 16 * (TILES // 2))
            if l > 0:
                g.wait_ge(agg_done[l - 1], 1)
            g.tensor_copy(idx_ring[:, l, 0, :], idx[:, 0, :]).then_inc(idx_copied[l], 1)
            with g.Fori(0, passes) as m:
                with g.Fori(0, GROUPS // RING) as i:
                    for s in range(RING):
                        t = m * GROUPS + i * RING + s
                        g.wait_ge(idx_copied[l], t + 1)
                        g.wait_ge(group_mm[l], t + 1)
                        g.tensor_copy(idx_ring[:, l, (s + 1) % RING, :],
                                      idx[:, i * RING + (s + 1), :]).then_inc(idx_copied[l], 1)
                        for j in range(GE):
                            g.indirect_dma_start(
                                out=ring[:, s, j, :], out_offset=None, in_=table[:, :],
                                in_offset=bass.IndirectOffsetOnAxis(ap=idx_ring[:, l, s, j:j + 1], axis=0),
                            ).then_inc(gathered[l][s], 16)

    @block.tensor
    def _(pe):
        pe.wait_ge(consts, 11)
        for l in range(AGGS):
            pe.sem_inc(group_mm[l], 3)
        for k in range(4):
            pe.wait_ge(edges_f, min(k + 1, 3))
            if k == 3:
                pe.wait_ge(ld_edges, 16 * 8)
            for j in range(GE):
                mm = pe.transpose(ps[:, k, j * GROUPS:(j + 1) * GROUPS],
                                  edge_f[0:GROUPS, k, j * P:(j + 1) * P], ident[0:GROUPS, 0:GROUPS])
            mm.then_inc(edges_tr, 1)
        pe.wait_ge(gstat_ready, 1)
        pe.matmul(ps[:, 4, 0:GROUPS], gspread[0:GROUPS, 0, :], ident[0:GROUPS, 0:GROUPS], start=True, stop=True)
        pe.matmul(ps[:, 5, 0:GROUPS], gspread[0:GROUPS, 1, :], ident[0:GROUPS, 0:GROUPS],
                  start=True, stop=True).then_inc(gspread_mm, 1)
        deg = ps[:, 6, 0:TILES]
        pe.sem_inc(hist_mm, 2)
        pe.matmul(deg, zero_bf[:, :], zero_bf[:, 0:TILES], start=True, stop=False, skip_group_check=True)
        with pe.Fori(0, GROUPS // 2) as i:
            for s in range(2):
                pe.wait_ge(hist_1h, i * 2 + s + 1)
                for j in range(GE):
                    mm = pe.matmul(deg, lo1h[:, s, j, :], hi1h[:, s, j, :], start=False, stop=False,
                                   skip_group_check=True)
                mm.then_inc(hist_mm, 1)
        pe.matmul(deg, zero_bf[:, :], zero_bf[:, 0:TILES], start=False, stop=True,
                  skip_group_check=True).then_inc(hist_done, 1)

        def transposes(src_rows, ready, which, c):
            for u in range(CHUNK):
                k = c * CHUNK + u
                pe.wait_ge(ready, k + 1)
                pe.wait_ge(tr_ev[which], k + 1)
                for h in range(HALVES):
                    mm = pe.transpose(ps[:, u, h * P:(h + 1) * P], src_rows[:, k, h * P:(h + 1) * P], ident[:, :])
                mm.then_inc(tr_mm[which], 1)

        def aggregate(l):
            with pe.Fori(0, passes) as m:
                with pe.Fori(0, GROUPS // RING) as i:
                    for s in range(RING):
                        t = m * GROUPS + i * RING + s
                        pe.wait_ge(gathered[l][s], (m * (GROUPS // RING) + i + 1) * (16 * GE))
                        pe.wait_ge(onehot_ready[l], t + 1)
                        pe.wait_ge(agg_added[l], t + 1)
                        for h in range(HALVES):
                            for j in range(GE):
                                mm = pe.matmul(ps[:, 6 + s % 2, h * P:(h + 1) * P], ring[:, s, j, h * P:(h + 1) * P],
                                               onehot[:, s % 2, j, :], start=(j == 0), stop=(j == GE - 1))
                        mm.then_inc(group_mm[l], 1)

        for c in range(CHUNKS):
            transposes(xn, ln_row[0], 0, c)
        pe.wait_ge(plan_ready, 1)
        passes = pe.value_load(npass[0:1, 0:1], min_val=1, max_val=26)
        for l in range(3):
            aggregate(l)
            pe.wait_ge(agg_done[l], 1)
            pe.wait_ge(ld_gcn, 16 * 6)
            for c in range(CHUNKS):
                for u in range(CHUNK):
                    k = c * CHUNK + u
                    if u % 2 == 0:
                        pe.wait_ge(y_ev[l], c * CHUNK + min(u + 2, CHUNK))
                    for h in range(HALVES):
                        mm = pe.matmul(ps[:, 5 + u // 2, (u % 2) * D:(u % 2 + 1) * D], xt[:, h, k * P:(k + 1) * P],
                                       gw[:, l, h, :], start=(h == 0), stop=(h == 1))
                    if u % 2 == 1 or u == CHUNK - 1:
                        mm.then_inc(y_mm[l], 1)
                if l < 2:
                    transposes(xn, row_ready[l], l + 1, c)

        for c in range(CHUNKS):
            transposes(xn, ln_row[1], 3, c)
        pe.wait_ge(ld_mix, 16 * (3 * E0 + 12))
        for q in range(2):
            mm = pe.transpose(ps[:, 5, q * 80:(q + 1) * 80], bnp[:, q, :], ident[0:80, 0:80])
        mm.then_inc(bn_tr, 1)
        pe.wait_ge(tr_ev[3], CHUNK + TILES)
        for k in range(TILES):
            pe.matmul(ps[:, 6, k * E0:(k + 1) * E0], ones[0:1, :], br0[:, :], start=True, stop=False)
            for h in range(HALVES):
                mm = pe.matmul(ps[:, 6, k * E0:(k + 1) * E0], xt[:, h, k * P:(k + 1) * P], wr0[:, h, :],
                               start=False, stop=(h == 1))
        mm.then_inc(rout_mm, 1)
        pe.wait_ge(rout_ready, 1)
        pe.wait_ge(bn_ready, 1)

        def experts_out(t, e):
            pe.wait_ge(l2_ev, t * 2 + 4)
            for u in range(CHUNK):
                if u % 2 == 0:
                    pe.wait_ge(yo_ev, t * CHUNK + min(u + 2, CHUNK))
                for h in range(HALVES):
                    mm = pe.matmul(ps[:, 4 + u // 2, (u % 2) * D:(u % 2 + 1) * D], h2[:, h, u * P:(u + 1) * P],
                                   wc[:, e, h, :], start=(h == 0), stop=(h == 1))
                if u % 2 == 1 or u == CHUNK - 1:
                    mm.then_inc(yo_mm, 1)

        with pe.Fori(0, CHUNKS) as c:
            for e in range(E0):
                t = c * E0 + e
                for m in range(2):
                    pe.wait_ge(l2_ev, t * 2 + m + 1)
                    for n in range(2):
                        for h in range(HALVES):
                            mm = pe.matmul(ps[:, 2 * m + n, 0:NH], wa[:, e, h, m * P:(m + 1) * P],
                                           xt[:, h, bass.ds(c * CROWS + n * NH, NH)], start=(h == 0), stop=(h == 1))
                    mm.then_inc(l1_mm, 1)
                if e > 0:
                    experts_out(t - 1, e - 1)
                pe.wait_ge(l1_ev, t * 2 + 2)
                for m in range(2):
                    for n in range(2):
                        for h in range(HALVES):
                            mm = pe.matmul(ps[:, 2 * m + n, 0:NH], wb[:, e, h, m * P:(m + 1) * P],
                                           h1[:, h, n * NH:(n + 1) * NH], start=(h == 0), stop=(h == 1))
                    mm.then_inc(l2_mm, 1)
            experts_out(c * E0 + (E0 - 1), E0 - 1)

        for c in range(CHUNKS):
            transposes(xn, ln_row[2], 4, c)
        pe.wait_ge(ld_rel, 16 * (RELS + HALVES))
        pe.wait_ge(tr_ev[4], CHUNK + TILES)
        for k in range(TILES):
            for h in range(HALVES):
                mm = pe.matmul(ps[:, 7, k * RELS:(k + 1) * RELS], xt[:, h, k * P:(k + 1) * P], rg[:, h, :],
                               start=(h == 0), stop=(h == 1))
        mm.then_inc(gate_mm, 1)
        pe.wait_ge(gate_ready, 1)

        def rel_products(k, s):
            pe.wait_ge(xr_copied, k + 1)
            for r in range(RELS // 2):
                pe.wait_ge(rel_ev_v if r % 2 else rel_ev_a, k * 4 + r // 2 + 1)
                for h in range(HALVES):
                    mm = pe.matmul(ps[:, (r % 2) * 4 + r // 2, :], xr[:, s, h, :],
                                   rw[:, h, 2 * r:2 * r + 2, :].rearrange("p r f -> p (r f)"),
                                   start=(h == 0), stop=(h == 1))
                mm.then_inc(rel_mm, 1)

        with pe.Fori(0, TILES // 2) as k2:
            for s in range(2):
                rel_products(k2 * 2 + s, s)
        rel_products(TILES - 1, 0)
        aggregate(3)
        pe.wait_ge(agg_done[3], 1)
        for c in range(CHUNKS):
            for u in range(CHUNK):
                k = c * CHUNK + u
                pe.wait_ge(back_ev, k + 1)
                for h in range(HALVES):
                    mm = pe.transpose(ps[:, u, h * P:(h + 1) * P], xt[:, h, k * P:(k + 1) * P], ident[:, :])
                mm.then_inc(back_mm, 1)

        for c in range(CHUNKS):
            transposes(xn, ln_row[3], 5, c)
        for h in range(HALVES):
            for k in range(TILES):
                mm = pe.matmul(ps[:, 5, h:h + 1], xn[:, k, h * P:(h + 1) * P],
                               ones[:, 0:1] if k < TILES - 1 else tail_one[:, 0:1],
                               start=(k == 0), stop=(k == TILES - 1))
        mm.then_inc(mean_mm, 1)
        pe.wait_ge(mean_ev, 1)
        pe.wait_ge(ld_mix2, 64)
        for h in range(HALVES):
            mm = pe.matmul(ps[0:1, 6, 0:E0], mean_t[:, h:h + 1], wr1[:, h, :], start=(h == 0), stop=(h == 1))
        mm.then_inc(log_mm, 1)
        pe.wait_ge(wsel_in, 1)
        pe.matmul(ps[:, 6, 16:16 + TOP_K], ones[0:1, :], small[:, 8, 0:TOP_K], start=True, stop=True).then_inc(wsel_mm, 1)
        pe.wait_ge(sel_ld, 16 * 4 * TOP_K)
        for s in range(TOP_K):
            mm = pe.transpose(ps[:, 7, s * FT:(s + 1) * FT], b1s[:, s, :], ident[0:FT, 0:FT])
        mm.then_inc(sel_tr, 1)
        pe.wait_ge(sel_ev, 1)
        pe.wait_ge(w2_scaled, TOP_K)
        pe.wait_ge(b2_ready, 1)
        pe.wait_ge(tr_ev[5], CHUNK + TILES)
        with pe.Fori(0, CHUNKS) as c:
            for s in range(TOP_K):
                for f in range(FT):
                    q = s * FT + f
                    pe.wait_ge(hid_ev, (c * TOP_K * FT) + q + 1)
                    for n in range(2):
                        for h in range(HALVES):
                            mm = pe.matmul(ps[:, 2 * (q % 2) + n, 0:NH], s1[:, s, h, f * P:(f + 1) * P],
                                           xt[:, h, bass.ds(c * CROWS + n * NH, NH)], start=(h == 0), stop=(h == 1))
                    mm.then_inc(hid_mm, 1)
            pe.wait_ge(hid_ev, (c + 1) * TOP_K * FT + 2)
            for u in range(CHUNK):
                k = c * CHUNK + u
                if u % 2 == 0:
                    pe.wait_ge(fo_ev, c * CHUNK + min(u + 2, CHUNK))
                acc = ps[:, 4 + u // 2, (u % 2) * D:(u % 2 + 1) * D]
                pe.matmul(acc, ones[0:1, :], b2m[:, 1, :], start=True, stop=False)
                for s in range(TOP_K):
                    for f in range(FT):
                        mm = pe.matmul(acc, hh[:, s, f, u * P:(u + 1) * P], s2[:, s, f, :], start=False,
                                       stop=(s == TOP_K - 1 and f == FT - 1))
                if u % 2 == 1 or u == CHUNK - 1:
                    mm.then_inc(fo_mm, 1)

    @block.scalar
    def _(act):
        for i in range(6):
            act.sem_inc(tr_ev[i], CHUNK)
        act.sem_inc(l2_ev, 2)
        act.sem_inc(hid_ev, 2)
        act.sem_inc(rel_ev_a, 4)

        def evacuate(which, c):
            for u in range(CHUNK):
                k = c * CHUNK + u
                act.wait_ge(tr_mm[which], k + 1)
                act.activation(xt[:, :, bass.ds(k * P, P)], ps[:, u, 0:D].rearrange("p (h n) -> p h n", h=HALVES),
                               ACT.Copy).then_inc(tr_ev[which], 1)

        def ln_sqrt(i):
            act.wait_ge(ln_var[i], 1)
            act.activation(rstd[:, :], rstd[:, :], ACT.Sqrt).then_inc(ln_sd[i], 1)

        ln_sqrt(0)
        act.wait_ge(deg_in, 1)
        act.activation(dinv[:, :], dinv[:, :], ACT.Sqrt).then_inc(deg_sd, 1)
        with act.Fori(0, CHUNKS) as c:
            evacuate(0, c)
        for l in range(2):
            with act.Fori(0, CHUNKS) as c:
                for u in range(CHUNK):
                    k = c * CHUNK + u
                    act.wait_ge(y_ev[l], k + CHUNK + 1)
                    act.activation(xn[:, k, :], xn[:, k, :], ACT.Gelu_apprx_tanh).then_inc(gelu_done[l], 1)
                    act.wait_ge(gelu_done[l], k + 1)
                    act.activation(xn[:, k, :], xn[:, k, :], ACT.Copy, scale=dinv[:, bass.ds(k, 1)]).then_inc(row_ready[l], 1)
                evacuate(l + 1, c)
        ln_sqrt(1)
        with act.Fori(0, CHUNKS) as c:
            evacuate(3, c)
        act.wait_ge(bn_var, 1)
        act.activation(bn_s[:, :, :], bn_s[:, :, :], ACT.Sqrt).then_inc(bn_sd, 1)
        act.wait_ge(rout_max, 1)
        act.activation(rout[:, :, :], rout[:, :, :], ACT.Exp).then_inc(rout_exp, 1)
        act.wait_ge(bn_ready, 1)
        with act.Fori(0, CHUNKS) as c:
            for e in range(E0):
                t = c * E0 + e
                for layer, (mm, ev, h) in enumerate(((l1_mm, l1_ev, h1), (l2_mm, l2_ev, h2))):
                    for m in range(2):
                        act.wait_ge(mm, t * 2 + m + 1)
                        col = 2 * e + m
                        act.activation(h[:, m, :].rearrange("p (n w) -> p n w", n=2), ps[:, 2 * m:2 * m + 2, 0:NH],
                                       ACT.Relu, bias=bn_t[:, layer, col:col + 1],
                                       scale=bn_s[:, layer, col:col + 1]).then_inc(ev, 1)
        ln_sqrt(2)
        with act.Fori(0, CHUNKS) as c:
            evacuate(4, c)
        act.wait_ge(gate_mm, 1)
        act.activation(gates[:, :, :].rearrange("p t r -> p (t r)"), ps[:, 7, 0:TILES * RELS],
                       ACT.Sigmoid).then_inc(gate_ready, 1)
        act.wait_ge(gate_ready, 1)

        def rel_evac(k, s):
            for r in range(0, RELS // 2, 2):
                act.wait_ge(rel_mm, k * 8 + r + 1)
                for q in range(2):
                    rel = 2 * r + q
                    ins = act.activation(stage[:, s, rel, :], ps[:, r // 2, q * D:(q + 1) * D], ACT.Copy,
                                         scale=gates[:, k, rel:rel + 1])
                ins.then_inc(rel_ev_a, 1)

        rel_evac(0, 0)
        rel_evac(1, 1)
        with act.Fori(1, TILES // 2) as k2:
            for s in range(2):
                act.wait_ge(rel_out[s], k2 * 16)
                rel_evac(k2 * 2 + s, s)
        act.wait_ge(rel_out[0], (TILES // 2) * 16)
        rel_evac(TILES - 1, 0)
        ln_sqrt(3)
        with act.Fori(0, CHUNKS) as c:
            evacuate(5, c)
        for i in range(2):
            act.wait_ge(exp_in, i + 1)
            act.activation(small[:, 1, :], small[:, 1, :], ACT.Exp).then_inc(exp_out, 1)
        act.wait_ge(exp_in, 3)
        act.activation(small[:, 9, 0:1], small[:, 9, 0:1], ACT.Exp).then_inc(exp_out, 1)
        act.wait_ge(sel_ev, 1)
        with act.Fori(0, CHUNKS) as c:
            for s in range(TOP_K):
                for f in range(FT):
                    q = s * FT + f
                    act.wait_ge(hid_mm, c * (TOP_K * FT) + q + 1)
                    act.activation(hh[:, s, f, :].rearrange("p (n w) -> p n w", n=2),
                                   ps[:, 2 * (q % 2):2 * (q % 2) + 2, 0:NH], ACT.Gelu,
                                   bias=b1c[:, s, f:f + 1]).then_inc(hid_ev, 1)
        act.wait_ge(ln_var[4], 1)
        act.activation(rstd[:, :], rstd[:, :], ACT.Sqrt).then_inc(ln_sd[4], 1)

    @block.vector
    def _(v):
        ch = Chain(v, dve_chain)
        for i in range(3):
            v.sem_inc(y_ev[i], CHUNK)
        for i in range(AGGS):
            v.sem_inc(agg_added[i], 2)
        v.sem_inc(yo_ev, CHUNK)
        v.sem_inc(rel_ev_v, 4)
        v.sem_inc(fo_ev, CHUNK)
        v.sem_inc(back_ev, CHUNK)

        v.wait_ge(consts, 11)
        v.wait_ge(ld_edges, 16 * 8)
        for k in range(3):
            v.tensor_copy(edge_f[0:GROUPS, k, :], edge_i[0:GROUPS, k, :]).then_inc(edges_f, 1)
        v.wait_ge(edges_f, 3)
        dst_rows = edge_f[0:GROUPS, 0, :]
        ch.done(v.tensor_scalar(tmpe[0:GROUPS, 0, :], dst_rows, 0.0, BIG, ALU.is_lt, ALU.mult))
        ch.done(v.tensor_tensor(tmpe[0:GROUPS, 1, :], tmpe[0:GROUPS, 0, :], dst_rows, ALU.add))
        ch.done(v.tensor_reduce(gstat[0:GROUPS, 0:1], tmpe[0:GROUPS, 1, :], AX_X, ALU.min))
        ch.done(v.tensor_reduce(gstat[0:GROUPS, 1:2], dst_rows, AX_X, ALU.max))
        ch.done(v.tensor_tensor(gstat[0:GROUPS, 2:3], gstat[0:GROUPS, 1:2], gstat[0:GROUPS, 0:1], ALU.subtract))
        v.tensor_scalar(gspread[0:GROUPS, 0, :], ones[0:GROUPS, :], gstat[0:GROUPS, 0:1], None, ALU.mult)
        v.tensor_scalar(gspread[0:GROUPS, 1, :], ones[0:GROUPS, :], gstat[0:GROUPS, 2:3], None,
                        ALU.mult).then_inc(gstat_ready, 1)

        def column(k):
            return ps[:, k, 0:GROUPS * GE].rearrange("p (j g) -> p g j", j=GE)

        v.wait_ge(edges_tr, 4)
        v.tensor_copy(dstc[:, :, :], column(0))
        v.tensor_copy(tmpc[:, 0, :, :], column(1))
        v.tensor_copy(tmpc[:, 1, :, :], column(2))
        ch.done(v.tensor_copy(wgtc[:, :, :], column(3)))
        ch.done(v.tensor_copy(idx_src[:, 0:GROUPS, :], tmpc[:, 0, :, :]))
        ch.done(v.scalar_tensor_tensor(out=idx_rel[:, 0:GROUPS, :], in0=tmpc[:, 0, :, :], scalar=float(RELS),
                                       in1=tmpc[:, 1, :, :], op0=ALU.mult, op1=ALU.add))
        v.tensor_copy(idx_src[:, GROUPS, :], idx_src[:, 0, :])
        v.tensor_copy(idx_rel[:, GROUPS, :], idx_rel[:, 0, :])
        ch.done(v.tensor_copy(tmpci[:, 2, :, :], dstc[:, :, :]))
        v.tensor_scalar(tmpci[:, 0, :, :], tmpci[:, 2, :, :], P - 1, None, ALU.bitwise_and)
        ch.done(v.tensor_scalar(tmpci[:, 1, :, :], tmpci[:, 2, :, :], 7, None, ALU.arith_shift_right))
        v.tensor_copy(tmpc[:, 0, :, :], tmpci[:, 0, :, :])
        ch.done(v.tensor_copy(tmpc[:, 1, :, :], tmpci[:, 1, :, :]))
        v.wait_ge(gspread_mm, 1)
        v.tensor_copy(base0[:, :], ps[:, 4, 0:GROUPS])
        ch.done(v.tensor_copy(span_i[:, :], ps[:, 5, 0:GROUPS]))
        ch.done(v.tensor_scalar(base_i[:, :], span_i[:, :], 7, None, ALU.arith_shift_right))
        ch.done(v.tensor_copy(base_f[:, :], base_i[:, :]))
        ch.done(v.tensor_reduce(npass_f[:, 0:1], base_f[:, :], AX_X, ALU.max))
        ch.done(v.tensor_scalar(npass[:, 0:1], npass_f[:, 0:1], 1.0, None, ALU.add))
        v.sem_inc(plan_ready, 1)

        def row_stats(src, i):
            with v.Fori(0, TILES) as k:
                v.bn_stats(stats[:, k, :], src[:, k, :]).then_inc(ln_stats[i], 1)
            v.wait_ge(ln_stats[i], TILES)
            v.tensor_tensor(mean[:, :], stats[:, :, 1], stats[:, :, 4], ALU.add)
            v.tensor_tensor(rstd[:, :], stats[:, :, 2], stats[:, :, 5], ALU.add)
            ch.done(v.tensor_tensor(rscale[:, :], stats[:, :, 1], stats[:, :, 4], ALU.subtract))
            v.tensor_scalar(mean[:, :], mean[:, :], 0.5, None, ALU.mult)
            v.tensor_scalar(rstd[:, :], rstd[:, :], 1.0 / D, LN_EPS, ALU.mult, ALU.add)
            ch.done(v.scalar_tensor_tensor(out=rscale[:, :], in0=rscale[:, :], scalar=0.25, in1=rscale[:, :],
                                           op0=ALU.mult, op1=ALU.mult))
            v.tensor_tensor(rstd[:, :], rstd[:, :], rscale[:, :], ALU.add).then_inc(ln_var[i], 1)

        def normalise(i, scale):
            with v.Fori(0, TILES) as k:
                v.tensor_scalar(xn[:, k, :], x_res[:, k, :], mean[:, bass.ds(k, 1)], scale[:, bass.ds(k, 1)],
                                ALU.subtract, ALU.mult).then_inc(ln_row[i], 1)

        v.wait_ge(ld_x, 32)
        row_stats(x_res, 0)

        with v.Fori(0, GROUPS // 2) as i:
            for s in range(2):
                n = i * 2 + s
                v.wait_ge(hist_mm, n + 1)
                v.tensor_tensor(hi1h[:, s, :, :], tmpc[:, 1, n, :].unsqueeze(2).to_broadcast([P, GE, TILES]),
                                iota_w[:, 0:TILES].unsqueeze(1).to_broadcast([P, GE, TILES]), ALU.is_equal)
                v.tensor_tensor(lo1h[:, s, :, :], tmpc[:, 0, n, :].unsqueeze(2).to_broadcast([P, GE, P]),
                                iota_w[:, :].unsqueeze(1).to_broadcast([P, GE, P]), ALU.is_equal).then_inc(hist_1h, 1)
        v.wait_ge(hist_done, 1)
        v.tensor_scalar(dinv[:, :], ps[:, 6, 0:TILES], 1.0, None, ALU.add).then_inc(deg_in, 1)
        v.wait_ge(deg_sd, 1)
        ch.done(v.reciprocal(dinv[:, :], dinv[:, :]))
        v.wait_ge(ln_sd[0], 1)
        ch.done(v.reciprocal(rstd[:, :], rstd[:, :]))
        ch.done(v.tensor_tensor(rscale[:, :], rstd[:, :], dinv[:, :], ALU.mult))
        normalise(0, rscale)

        passes = v.value_load(npass[0:1, 0:1], min_val=1, max_val=26)

        def aggregate(l):
            v.tensor_copy(base_f[:, :], base0[:, :]).then_inc(pass_base[l], 1)
            with v.Fori(0, passes) as m:
                v.wait_ge(pass_base[l], m * 3 + 1)
                v.tensor_copy(base_i[:, :], base_f[:, :]).then_inc(pass_base[l], 1)
                v.tensor_tensor(rel_dst[:, :, :], dstc[:, :, :],
                                base_f[:, :].unsqueeze(2).to_broadcast([P, GROUPS, GE]),
                                ALU.subtract).then_inc(pass_base[l], 1)
                with v.Fori(0, GROUPS // RING) as i:
                    for s in range(RING):
                        n = i * RING + s
                        t = m * GROUPS + n
                        v.wait_ge(pass_base[l], m * 3 + 3)
                        v.wait_ge(group_mm[l], t + 2)
                        for j in range(GE):
                            scalar = rel_dst[:, n, j:j + 1]
                            if l < 3:
                                ins = v.tensor_scalar(onehot[:, s % 2, j, :], iota_w[:, :], scalar, None, ALU.is_equal)
                            else:
                                ins = v.tensor_scalar(onehot[:, s % 2, j, :], iota_w[:, :], scalar,
                                                      wgtc[:, n, j:j + 1], ALU.is_equal, ALU.mult)
                        ins.then_inc(onehot_ready[l], 1)
                        first = v.value_load(base_i[0:1, bass.ds(n, 1)], min_val=0, max_val=ROWS)
                        v.wait_ge(group_mm[l], t + 4)
                        v.wait_ge(agg_added[l], t + 2)
                        window = xt[:, :, bass.ds(first, P)]
                        v.tensor_tensor(window, ps[:, 6 + s % 2, 0:D].rearrange("p (h n) -> p h n", h=HALVES),
                                        window, ALU.add).then_inc(agg_added[l], 1)
                v.tensor_scalar(base_f[:, :], base_f[:, :], float(P), float(ROWS), ALU.add,
                                ALU.min).then_inc(pass_base[l], 1)
            v.wait_ge(pass_base[l], passes * 3 + 1)
            v.wait_ge(agg_added[l], passes * GROUPS + 2)
            v.sem_inc(agg_done[l], 1)

        for l in range(3):
            v.wait_ge(tr_ev[l], CHUNK + TILES)
            aggregate(l)
            v.wait_ge(ld_gcn, 16 * 6)
            with v.Fori(0, CHUNKS) as c:
                for u in range(CHUNK):
                    k = c * CHUNK + u
                    v.wait_ge(y_mm[l], c * UNITS + u // 2 + 1)
                    v.scalar_tensor_tensor(out=xn[:, k, :], in0=ps[:, 5 + u // 2, (u % 2) * D:(u % 2 + 1) * D],
                                           scalar=dinv[:, bass.ds(k, 1)], in1=gb[:, l, :],
                                           op0=ALU.mult, op1=ALU.add).then_inc(y_ev[l], 1)
                    if l == 2:
                        v.wait_ge(y_ev[l], k + CHUNK + 1)
                        v.tensor_tensor(x_res[:, k, :], x_res[:, k, :], xn[:, k, :], ALU.add).then_inc(gcn_added, 1)
        v.wait_ge(gcn_added, TILES)
        row_stats(x_res, 1)
        v.wait_ge(ln_sd[1], 1)
        ch.done(v.reciprocal(rstd[:, :], rstd[:, :]))
        normalise(1, rstd)

        v.wait_ge(bn_tr, 1)
        ch.done(v.tensor_copy(bnc[:, :, :, :].rearrange("p q n e -> p (q n e)"), ps[:, 5, 0:160]))
        v.tensor_scalar(bn_s[:, :, :], bnc[:, :, 4, :], BN_EPS, None, ALU.add).then_inc(bn_var, 1)
        v.wait_ge(bn_sd, 1)
        ch.done(v.reciprocal(bn_s[:, :, :], bn_s[:, :, :]))
        ch.done(v.tensor_tensor(bn_s[:, :, :], bn_s[:, :, :], bnc[:, :, 1, :], ALU.mult))
        ch.done(v.tensor_tensor(bn_t[:, :, :], bnc[:, :, 0, :], bnc[:, :, 3, :], ALU.subtract))
        ch.done(v.tensor_tensor(bn_t[:, :, :], bn_t[:, :, :], bn_s[:, :, :], ALU.mult))
        v.tensor_tensor(bn_t[:, :, :], bn_t[:, :, :], bnc[:, :, 2, :], ALU.add).then_inc(bn_ready, 1)
        v.wait_ge(rout_mm, 1)
        logits = ps[:, 6, 0:TILES * E0].rearrange("p (t e) -> p t e", e=E0)

        def over_experts():
            return rtmp[:, :].unsqueeze(2).to_broadcast([P, TILES, E0])

        ch.done(v.tensor_reduce(rtmp[:, :], logits, AX_X, ALU.max))
        v.tensor_tensor(rout[:, :, :], logits, over_experts(), ALU.subtract).then_inc(rout_max, 1)
        v.wait_ge(rout_exp, 1)
        ch.done(v.tensor_reduce(rtmp[:, :], rout[:, :, :], AX_X, ALU.add))
        ch.done(v.reciprocal(rtmp[:, :], rtmp[:, :]))
        v.tensor_tensor(rout[:, :, :], rout[:, :, :], over_experts(), ALU.mult).then_inc(rout_ready, 1)
        v.wait_ge(rout_ready, 1)
        v.wait_ge(ld_bo, 16)
        with v.Fori(0, CHUNKS) as c:
            for e in range(E0):
                t = c * E0 + e
                for u in range(CHUNK):
                    k = c * CHUNK + u
                    v.wait_ge(yo_ev, t * CHUNK + u + 1)
                    v.scalar_tensor_tensor(out=x_res[:, k, :], in0=bob[:, e, :], scalar=rout[:, k, e:e + 1],
                                           in1=x_res[:, k, :], op0=ALU.mult, op1=ALU.add).then_inc(bo_added, 1)
                for u in range(CHUNK):
                    k = c * CHUNK + u
                    v.wait_ge(bo_added, t * CHUNK + u + 1)
                    v.wait_ge(yo_mm, t * UNITS + u // 2 + 1)
                    v.scalar_tensor_tensor(out=x_res[:, k, :], in0=ps[:, 4 + u // 2, (u % 2) * D:(u % 2 + 1) * D],
                                           scalar=rout[:, k, e:e + 1], in1=x_res[:, k, :],
                                           op0=ALU.mult, op1=ALU.add).then_inc(yo_ev, 1)
        v.wait_ge(yo_ev, CHUNK + TILES * E0)

        row_stats(x_res, 2)
        v.wait_ge(ln_sd[2], 1)
        ch.done(v.reciprocal(rstd[:, :], rstd[:, :]))
        normalise(2, rstd)
        v.wait_ge(gate_ready, 1)

        def rel_evac(k, s):
            for r in range(1, RELS // 2, 2):
                v.wait_ge(rel_mm, k * 8 + r + 1)
                for q in range(2):
                    rel = 2 * r + q
                    ins = v.tensor_scalar(stage[:, s, rel, :], ps[:, 4 + r // 2, q * D:(q + 1) * D],
                                          gates[:, k, rel:rel + 1], None, ALU.mult)
                ins.then_inc(rel_ev_v, 1)

        rel_evac(0, 0)
        rel_evac(1, 1)
        with v.Fori(1, TILES // 2) as k2:
            for s in range(2):
                v.wait_ge(rel_out[s], k2 * 16)
                rel_evac(k2 * 2 + s, s)
        v.wait_ge(rel_out[0], (TILES // 2) * 16)
        rel_evac(TILES - 1, 0)
        v.wait_ge(xr_copied, TILES)
        ch.done(v.memset(xt[:, :, :], 0.0))
        v.wait_ge(rel_out[0], 16 * (TILES // 2 + 1))
        v.wait_ge(rel_out[1], 16 * (TILES // 2))
        aggregate(3)
        with v.Fori(0, CHUNKS) as c:
            for u in range(CHUNK):
                k = c * CHUNK + u
                v.wait_ge(back_mm, k + 1)
                v.scalar_tensor_tensor(out=x_res[:, k, :], in0=ps[:, u, 0:D], scalar=0.0, in1=x_res[:, k, :],
                                       op0=ALU.max, op1=ALU.add).then_inc(back_ev, 1)
        v.wait_ge(back_ev, CHUNK + TILES)
        row_stats(x_res, 3)
        v.wait_ge(ln_sd[3], 1)
        ch.done(v.reciprocal(rstd[:, :], rstd[:, :]))
        normalise(3, rstd)

        v.wait_ge(mean_mm, 1)
        v.tensor_scalar(mean_t[:, :], ps[:, 5, 0:HALVES], 1.0 / N_NODES, None, ALU.mult).then_inc(mean_ev, 1)
        v.wait_ge(log_mm, 1)

        def row(i, n=E0, at=0):
            return small[:, i, at:at + n]

        def softmax(i):
            ch.done(v.tensor_reduce(row(2, 1), row(1), AX_X, ALU.max))
            v.tensor_scalar(row(1), row(1), row(2, 1), None, ALU.subtract).then_inc(exp_in, 1)
            v.wait_ge(exp_out, i + 1)
            ch.done(v.tensor_reduce(row(2, 1), row(1), AX_X, ALU.add))
            ch.done(v.reciprocal(row(2, 1), row(2, 1)))
            ch.done(v.tensor_scalar(row(1), row(1), row(2, 1), None, ALU.mult))

        ch.done(v.tensor_tensor(row(1), ps[0:1, 6, 0:E0], row(0), ALU.add))
        softmax(0)
        ch.done(v.tensor_scalar(row(3), row(1), float(N_NODES), CAPACITY, ALU.mult, ALU.max))
        ch.done(v.reciprocal(row(3), row(3)))
        ch.done(v.tensor_scalar(row(3), row(3), CAPACITY, None, ALU.mult))
        ch.done(v.tensor_tensor(row(1), row(1), row(3), ALU.mult))
        softmax(1)
        for s in range(TOP_K):
            ch.done(v.tensor_reduce(row(4, 1, s), row(1), AX_X, ALU.max))
            ch.done(v.tensor_scalar(row(5), row(1), row(4, 1, s), None, ALU.is_equal))
            ch.done(v.tensor_scalar(row(6), iota8[:, :], -1.0, float(E0), ALU.mult, ALU.add))
            ch.done(v.tensor_tensor(row(5), row(5), row(6), ALU.mult))
            ch.done(v.tensor_reduce(row(7, 1), row(5), AX_X, ALU.max))
            ch.done(v.tensor_scalar(row(7, 1, 1 + s), row(7, 1), -1.0, float(E0), ALU.mult, ALU.add))
            ch.done(v.tensor_scalar(row(5), iota8[:, :], row(7, 1, 1 + s), -2.0, ALU.is_equal, ALU.mult))
            ch.done(v.tensor_tensor(row(1), row(1), row(5), ALU.add))
        v.tensor_copy(sel_i[:, 0:TOP_K], row(7, TOP_K, 1)).then_inc(sel_ready, 1)
        v.tensor_tensor(row(9, 1), row(4, 1, 1), row(4, 1, 0), ALU.subtract).then_inc(exp_in, 1)
        v.wait_ge(exp_out, 3)
        ch.done(v.tensor_scalar(row(10, 1), row(9, 1), 1.0, None, ALU.add))
        ch.done(v.reciprocal(row(8, 1), row(10, 1)))
        v.tensor_tensor(row(8, 1, 1), row(8, 1), row(9, 1), ALU.mult).then_inc(wsel_in, 1)
        v.wait_ge(wsel_in, 1)
        v.wait_ge(wsel_mm, 1)
        ch.done(v.tensor_copy(wsel[:, :], ps[:, 6, 16:16 + TOP_K]))
        v.wait_ge(sel_ld, 16 * 4 * TOP_K)
        v.wait_ge(sel_tr, 1)
        v.tensor_copy(b1c[:, :, :].rearrange("p s f -> p (s f)"), ps[:, 7, 0:TOP_K * FT]).then_inc(sel_ev, 1)
        for s in range(TOP_K):
            w = s2[:, s, :, :].rearrange("p k f -> p (k f)")
            v.tensor_scalar(w, w, wsel[:, s:s + 1], None, ALU.mult).then_inc(w2_scaled, 1)
        ch.done(v.tensor_scalar(b2m[:, 0, :], b2s[:, 0, :], wsel[0:1, 0:1], None, ALU.mult))
        v.scalar_tensor_tensor(out=b2m[:, 1, :], in0=b2s[:, 1, :], scalar=wsel[0:1, 1:2], in1=b2m[:, 0, :],
                               op0=ALU.mult, op1=ALU.add).then_inc(b2_ready, 1)
        with v.Fori(0, CHUNKS) as c:
            for u in range(CHUNK):
                k = c * CHUNK + u
                v.wait_ge(fo_mm, c * UNITS + u // 2 + 1)
                v.tensor_tensor(xn[:, k, :], ps[:, 4 + u // 2, (u % 2) * D:(u % 2 + 1) * D], xn[:, k, :],
                                ALU.add).then_inc(fo_ev, 1)
        v.wait_ge(fo_ev, CHUNK + TILES)
        row_stats(xn, 4)
        v.wait_ge(ln_sd[4], 1)
        ch.done(v.reciprocal(rstd[:, :], rstd[:, :]))
        with v.Fori(0, TILES) as k:
            ch.loop(k, 3)
            ch.done(v.tensor_scalar(xn[:, k, :], xn[:, k, :], mean[:, bass.ds(k, 1)], rstd[:, bass.ds(k, 1)],
                                    ALU.subtract, ALU.mult))
            ch.done(v.tensor_tensor(xn[:, k, :], xn[:, k, :], gam[:, :], ALU.mult))
            ch.done(v.tensor_tensor(xn[:, k, :], xn[:, k, :], bet[:, :], ALU.add))
            v.tensor_tensor(x_res[:, k, :], x_res[:, k, :], xn[:, k, :], ALU.add).then_inc(fin_ready, 1)
        ch.end(TILES, 3)


_INS = ["x", "src", "dst", "edge_type_16", "edge_weight1",
        "L0_gnn_W1", "L0_gnn_b1", "L0_gnn_W2", "L0_gnn_b2", "L0_gnn_W3", "L0_gnn_b3",
        "L0_ffn_Wr", "L0_ffn_br", "L0_ffn_W1", "L0_ffn_b1", "L0_ffn_g1", "L0_ffn_be1", "L0_ffn_m1", "L0_ffn_v1",
        "L0_ffn_W2", "L0_ffn_b2", "L0_ffn_g2", "L0_ffn_be2", "L0_ffn_m2", "L0_ffn_v2", "L0_ffn_Wo", "L0_ffn_bo",
        "L1_gnn_weight", "L1_gnn_gate_weight",
        "L1_ffn_Wr", "L1_ffn_br", "L1_ffn_W1", "L1_ffn_b1", "L1_ffn_W2", "L1_ffn_b2", "L1_ffn_gamma", "L1_ffn_beta"]


def kernel(**inputs):
    import numpy as np
    import concourse.bacc as bacc
    from concourse.bass_utils import run_bass_kernel_spmd

    nc = bacc.Bacc("TRN2", target_bir_lowering=False, num_devices=1)
    arrays, aps = {}, {}
    for name in _INS:
        arr = np.ascontiguousarray(inputs[name])
        arrays["in_" + name] = arr
        aps[name] = nc.dram_tensor("in_" + name, arr.shape, mybir.dt.from_np(arr.dtype), kind="ExternalInput").ap()
    result = nc.dram_tensor("result", (N_NODES, D), F32, kind="ExternalOutput").ap()
    build(nc, aps, result)
    r = run_bass_kernel_spmd(nc, [arrays], core_ids=[0])
    return r.results[0]["result"]
```

```python
from contextlib import ExitStack

import concourse.bass as bass
from concourse import mybir
from concourse.alu_op_type import AluOpType as ALU

F32 = mybir.dt.float32
BF16 = mybir.dt.bfloat16
I32 = mybir.dt.int32
ACT = mybir.ActivationFunctionType
AX_X = mybir.AxisListType.X

P = 128
N_NODES = 3125
N_EDGES = 53125
D = 256
HALVES = D // P
TILES = -(-N_NODES // P)
ROWS = TILES * P
TAIL = N_NODES - (TILES - 1) * P
CHUNK = 5
CHUNKS = TILES // CHUNK
UNITS = -(-CHUNK // 2)
CROWS = CHUNK * P
NH = CROWS // 2
GE = 8
GROUP = GE * P
GROUPS = -(-N_EDGES // GROUP)
GTAIL = N_EDGES - (GROUPS - 1) * GROUP
RING = 4
RELS = 16
E0 = 8
F1 = 512
FT = F1 // P
TOP_K = 2
LN_EPS = 1e-5
BN_EPS = 1e-3
PROLOGUE = 12
FOLLOW = [12, 12, 12, 4, 0]
AGGS = 4
BIG = 4096.0
CAPACITY = float(-(-(N_NODES * 5) // (4 * E0)))


class Steps:

    def __init__(self, eng, sem, turn=0, per_turn=0):
        self.eng, self.sem, self.n, self.base, self.per_turn = eng, sem, 0, turn * per_turn, per_turn

    def done(self, ins):
        ins.then_inc(self.sem, 1)
        self.n += 1
        self.eng.wait_ge(self.sem, self.base + self.n)

    def end(self):
        assert self.n == self.per_turn, self.n


def mix_plan(t0):
    follow = t0[2]
    if follow > E0:
        return 2, E0 - 1, follow - 2 - (E0 - 1)
    return follow // 2, 0, follow - follow // 2


def build(nc, a, out):
    with ExitStack() as ctx:
        _build(nc, a, out, ctx)


def _build(nc, a, out, ctx):
    def sb(name, shape, dt=F32):
        return ctx.enter_context(nc.sbuf_tensor(name, shape, dt))

    def sem(name):
        return ctx.enter_context(nc.semaphore(name))

    gcn_table = [nc.dram_tensor(f"gcn_table{l}", (ROWS, D), F32).ap() for l in range(3)]
    rel_table = nc.dram_tensor("rel_table", (ROWS * RELS, D), F32).ap()

    x_res = sb("x_res", [P, TILES, D])
    xn = sb("xn", [P, TILES, D])
    xt = sb("xt", [P, HALVES, ROWS + P])
    union = sb("union", [P, 10240])
    ring = union[:, 0:8192].rearrange("p (s j f) -> p s j f", s=RING, j=GE)
    onehot = union[:, 8192:10240].rearrange("p (s j w) -> p s j w", s=2, j=GE)
    rows = sb("rows", [P, CHUNK, D])
    xs = sb("xs", [P, HALVES, CROWS])
    stage = union[:, 0:8192].rearrange("p (s r f) -> p s r f", s=2, r=RELS)
    hh = union[:, 0:5120].rearrange("p (s m n) -> p s m n", s=2, m=FT)
    lo1h = union[:, 0:1024].bitcast(BF16).rearrange("p (s j w) -> p s j w", s=2, j=GE)
    hi1h = union[:, 1024:1024 + 256].bitcast(BF16)[:, 0:2 * GE * TILES].rearrange("p (s j w) -> p s j w", s=2, j=GE)
    gspread = union[:, 1280:1536].rearrange("p (k q) -> p k q", k=2)
    edge_i = union[:, 2048:6144].bitcast(I32).rearrange("p (k e) -> p k e", k=4)
    edge_f = union[:, 6144:10240].rearrange("p (k e) -> p k e", k=4)

    gw = sb("gw", [P, 3, HALVES, D])
    gb = sb("gb", [P, 3, D])
    weights = sb("weights", [P, 3, E0 * HALVES * D])
    wa, wb, wc = (weights[:, i, :].rearrange("p (e k f) -> p e k f", e=E0, k=HALVES) for i in range(3))
    rw = weights[:, 0:2, :].rearrange("p k (r f) -> p k r f", r=RELS)
    rg = sb("rg", [P, HALVES, RELS])
    s1 = weights[:, 2, 0:2048].rearrange("p (s k f) -> p s k f", s=TOP_K, k=HALVES)
    s2 = weights[:, 2, 2048:4096].rearrange("p (s k f) -> p s k f", s=TOP_K, k=FT)

    ident = sb("ident", [P, P])
    ones = sb("ones", [P, P])
    iota_w = sb("iota_w", [P, P])
    iota_bf = sb("iota_bf", [P, P], BF16)
    zero_bf = sb("zero_bf", [P, P], BF16)
    row_mask = sb("row_mask", [P, TILES])
    zero_f = sb("zero_f", [P, 2])
    dstc = sb("dstc", [P, GROUPS, GE])
    wgtc = sb("wgtc", [P, GROUPS, GE])
    scratch = xn[:, :, :].rearrange("p t f -> p (t f)")
    tmpc = scratch[:, 0:4 * GROUPS * GE].rearrange("p (k g j) -> p k g j", k=4, j=GE)
    tmpci = scratch[:, 1664:1664 + 3 * GROUPS * GE].bitcast(I32).rearrange("p (k g j) -> p k g j", k=3, j=GE)
    h1 = scratch[:, 0:1280].rearrange("p (m n) -> p m n", m=2)
    h2 = scratch[:, 1280:2560].rearrange("p (m n) -> p m n", m=2)
    bob = scratch[:, 2560:4608].rearrange("p (e f) -> p e f", e=E0)
    tmpe = scratch[:, 4096:6144].rearrange("p (k e) -> p k e", k=2)
    rel_dst = sb("rel_dst", [P, GROUPS, GE])
    idx_src = sb("idx_src", [P, GROUPS + 1, GE], I32)
    idx_rel = sb("idx_rel", [P, GROUPS + 1, GE], I32)
    idx_ring = sb("idx_ring", [P, AGGS, RING, GE], I32)
    base0 = sb("base0", [P, GROUPS])
    base_f = sb("base_f", [P, GROUPS])
    base_i = sb("base_i", [P, GROUPS], I32)
    gstat = sb("gstat", [P, 4])
    span_i = sb("span_i", [P, GROUPS], I32)
    npass_f = sb("npass_f", [P, 3])
    npass = sb("npass", [P, 2], I32)
    dinv = sb("dinv", [P, TILES])
    xr = sb("xr", [P, 2, HALVES, P])
    stats0 = sb("stats0", [P, TILES, 6])
    mean0, rstd0, half0 = (sb(n, [P, TILES]) for n in ("mean0", "rstd0", "half0"))
    stats = sb("stats", [P, CHUNK, 6])
    mean, rstd, half = (sb(n, [P, CHUNK]) for n in ("mean", "rstd", "half"))
    wr0 = sb("wr0", [P, HALVES, E0])
    br0 = sb("br0", [1, E0])
    rout = sb("rout", [P, CHUNK, E0])
    rtmp = sb("rtmp", [P, CHUNK])
    bnp = sb("bnp", [80, 2, P])
    bnc = sb("bnc", [P, 2, 5, 16])
    bn_s = sb("bn_s", [P, 2, 16])
    bn_t = sb("bn_t", [P, 2, 16])
    gates = sb("gates", [P, TILES, RELS])
    wr1 = sb("wr1", [P, HALVES, E0])
    small = sb("small", [1, 12, E0])
    iota8 = sb("iota8", [1, E0])
    sel_i = sb("sel_i", [1, 4], I32)
    mean_t = sb("mean_t", [P, HALVES])
    b1s = union[0:FT, 5120:5376].rearrange("p (s f) -> p s f", s=TOP_K)
    b1c = sb("b1c", [P, TOP_K, FT])
    b2s = union[0:1, 5376:5888].rearrange("p (s f) -> p s f", s=TOP_K)
    wsel = sb("wsel", [P, TOP_K])
    b2m = union[0:1, 5888:6400].rearrange("p (s f) -> p s f", s=2)
    gam = sb("gam", [P, D])
    bet = sb("bet", [P, D])

    ps = ctx.enter_context(nc.psum_tensor("ps", [P, 8, 512], F32))

    ld_edges, ld_x, ld_gcn, ld_mix, ld_rel, ld_mix2 = (sem("ld_" + n) for n in ("edges", "x", "gcn", "mix", "rel", "mix2"))
    consts = sem("consts")
    once_steps, mix_steps, back_steps, out_steps = (
        sem(n) for n in ("once_steps", "mix_steps", "back_steps", "out_steps"))
    edges_f = sem("edges_f")
    edges_tr = sem("edges_tr")
    gstat_ready = sem("gstat_ready")
    gspread_mm = sem("gspread_mm")
    plan_ready = sem("plan_ready")
    deg_in, deg_sd, gcn_added, bo_added = sem("deg_in"), sem("deg_sd"), sem("gcn_added"), sem("bo_added")
    lo_1h, hi_1h, hist_mm, hist_done = sem("lo_1h"), sem("hi_1h"), sem("hist_mm"), sem("hist_done")
    digits_ready = sem("digits_ready")
    ln_var = [sem(f"ln_var{i}") for i in range(5)]
    ln_sd = [sem(f"ln_sd{i}") for i in range(5)]
    ln_row = [sem(f"ln_row{i}") for i in range(4)]
    tr_mm = [sem(f"tr_mm{i}") for i in range(6)]
    tr_ev = [sem(f"tr_ev{i}") for i in range(6)]
    table_out = [sem(f"table_out{i}") for i in range(4)]
    idx_copied = [sem(f"idx_copied{i}") for i in range(AGGS)]
    gathered = [[sem(f"gathered{i}_{s}") for s in range(RING)] for i in range(AGGS)]
    onehot_ready = [sem(f"onehot_ready{i}") for i in range(AGGS)]
    group_mm = [sem(f"group_mm{i}") for i in range(AGGS)]
    agg_added = [sem(f"agg_added{i}") for i in range(AGGS)]
    pass_base = [sem(f"pass_base{i}") for i in range(AGGS)]
    chunk_summed, xs_copied, agg_done = sem("chunk_summed"), sem("xs_copied"), sem("agg_done")
    y_mm, y_ev = sem("y_mm"), sem("y_ev")
    gelu_done, row_ready, rows_free = sem("gelu_done"), sem("row_ready"), sem("rows_free")
    rout_mm, rout_max, rout_exp, rout_ready = (sem("rout_" + n) for n in ("mm", "max", "exp", "ready"))
    ld_bo = sem("ld_bo")
    bn_tr, bn_var, bn_sd, bn_ready = (sem("bn_" + n) for n in ("tr", "var", "sd", "ready"))
    l1_mm, l1_ev, l2_mm, l2_ev, yo_mm, yo_ev = (sem(n) for n in ("l1_mm", "l1_ev", "l2_mm", "l2_ev", "yo_mm", "yo_ev"))
    xr_copied = sem("xr_copied")
    gate_mm, gate_ready = sem("gate_mm"), sem("gate_ready")
    rel_mm, rel_ev_a, rel_ev_v, rel_out = sem("rel_mm"), sem("rel_ev_a"), sem("rel_ev_v"), [sem("rel_out0"), sem("rel_out1")]
    back_mm, back_ev = sem("back_mm"), sem("back_ev")
    rows_copied, beta_added, fin_scaled = sem("rows_copied"), sem("beta_added"), sem("fin_scaled")
    mean_mm, mean_ev, log_mm, exp_in, exp_out = (sem(n) for n in ("mean_mm", "mean_ev", "log_mm", "exp_in", "exp_out"))
    sel_ready, sel_ld, sel_tr, sel_ev, wsel_in, wsel_mm = (
        sem(n) for n in ("sel_ready", "sel_ld", "sel_tr", "sel_ev", "wsel_in", "wsel_mm"))
    b2_ready, w2_scaled = sem("b2_ready"), sem("w2_scaled")
    hid_mm, hid_ev, fo_mm, fo_ev, fin_ready, out_done = (
        sem(n) for n in ("hid_mm", "hid_ev", "fo_mm", "fo_ev", "fin_ready", "out_done"))

    block = ctx.enter_context(nc.Block())

    @block.sync
    def _(sp):
        for k, name in enumerate(("dst", "src", "edge_type_16")):
            sp.wait_ge(consts, 4)
            sp.dma_start(edge_i[0:GROUPS - 1, k, :],
                         a[name][0:(GROUPS - 1) * GROUP].rearrange("(g e) -> g e", g=GROUPS - 1)).then_inc(ld_edges, 16)
            sp.dma_start(edge_i[GROUPS - 1:GROUPS, k, 0:GTAIL],
                         a[name][(GROUPS - 1) * GROUP:N_EDGES].rearrange("(g e) -> g e", g=1)).then_inc(ld_edges, 16)
        sp.dma_start(edge_f[0:GROUPS - 1, 3, :], a["edge_weight1"][0:(GROUPS - 1) * GROUP, :]
                     .rearrange("(g e) o -> g (e o)", g=GROUPS - 1)).then_inc(ld_edges, 16)
        sp.dma_start(edge_f[GROUPS - 1:GROUPS, 3, 0:GTAIL], a["edge_weight1"][(GROUPS - 1) * GROUP:N_EDGES, :]
                     .rearrange("(g e) o -> g (e o)", g=1)).then_inc(ld_edges, 16)
        sp.dma_start(x_res[:, 0:TILES - 1, :],
                     a["x"][0:(TILES - 1) * P, :].rearrange("(t p) f -> p t f", p=P)).then_inc(ld_x, 16)
        sp.dma_start(x_res[0:TAIL, TILES - 1, :], a["x"][(TILES - 1) * P:N_NODES, :]).then_inc(ld_x, 16)
        for l in range(3):
            sp.dma_start(gw[:, l, :, :], a[f"L0_gnn_W{l + 1}"].rearrange("(k p) f -> p k f", p=P)).then_inc(ld_gcn, 16)
            sp.dma_start(gb[:, l, :], a[f"L0_gnn_b{l + 1}"].partition_broadcast(P)).then_inc(ld_gcn, 16)
        for w, name in ((wa, "L0_ffn_W1"), (wb, "L0_ffn_W2"), (wc, "L0_ffn_Wo")):
            for e in range(E0):
                sp.dma_start(w[:, e, :, :], a[name][e].rearrange("(k p) f -> p k f", p=P)).then_inc(ld_mix, 16)
        for q, names in enumerate((("b1", "g1", "be1", "m1", "v1"), ("b2", "g2", "be2", "m2", "v2"))):
            for n, name in enumerate(names):
                sp.dma_start(bnp[n * 16:(n + 1) * 16, q, :],
                             a["L0_ffn_" + name].rearrange("e (h p) -> (e h) p", p=P)).then_inc(ld_mix, 16)
        sp.dma_start(wr0[:, :, :], a["L0_ffn_Wr"].rearrange("(k p) e -> p k e", p=P)).then_inc(ld_mix, 16)
        sp.dma_start(br0[:, :], a["L0_ffn_br"].rearrange("(o e) -> o e", o=1)).then_inc(ld_mix, 16)
        for k in range(HALVES):
            sp.dma_start(rg[:, k, :], a["L1_gnn_gate_weight"][:, k * P:(k + 1) * P, :].rearrange("r p o -> p (r o)"),
                         allow_slow_non_contiguous=True).then_inc(ld_rel, 16)
        sp.dma_start(wr1[:, :, :], a["L1_ffn_Wr"].rearrange("(k p) e -> p k e", p=P)).then_inc(ld_mix2, 16)
        sp.dma_start(small[:, 0, :], a["L1_ffn_br"].rearrange("(o e) -> o e", o=1)).then_inc(ld_mix2, 16)
        sp.dma_start(gam[:, :], a["L1_ffn_gamma"].partition_broadcast(P)).then_inc(ld_mix2, 16)
        sp.dma_start(bet[:, :], a["L1_ffn_beta"].partition_broadcast(P)).then_inc(ld_mix2, 16)

        with sp.Fori(0, TILES) as k:
            sp.wait_ge(ln_row[0], k + 1)
            sp.dma_start(gcn_table[0][bass.ds(k * P, P), :], xn[:, k, :]).then_inc(table_out[0], 16)
        sp.wait_ge(table_out[0], 16 * TILES)
        sp.wait_ge(tr_mm[0], TILES)
        sp.dma_start(bob[:, :, :], a["L0_ffn_bo"].partition_broadcast(P)).then_inc(ld_bo, 16)
        sp.sem_inc(rows_free, 1)
        for l in range(2):
            with sp.Fori(0, CHUNKS) as c:
                for u in range(CHUNK):
                    k = c * CHUNK + u
                    sp.wait_ge(row_ready, k + (l * TILES + 1))
                    sp.dma_start(gcn_table[l + 1][bass.ds(k * P, P), :], rows[:, u, :]).then_inc(table_out[l + 1], 16)
                sp.wait_ge(table_out[l + 1], c * (16 * CHUNK) + 16 * CHUNK)
                sp.sem_inc(rows_free, 1)
        last = (CHUNKS - 1) * E0
        for e in range(E0):
            for i, used in enumerate((l1_mm, l2_mm)):
                sp.wait_ge(used, (last + e + 1) * 2)
                sp.dma_start(rw[:, i, 2 * e:2 * e + 2, :], a["L1_gnn_weight"][2 * e:2 * e + 2, i * P:(i + 1) * P, :]
                             .rearrange("r p f -> p r f")).then_inc(ld_rel, 16)
        def rel_rows(k, s, n):
            sp.wait_ge(rel_ev_a, k * 4 + 8)
            sp.wait_ge(rel_ev_v, k * 4 + 8)
            sp.dma_start(rel_table[bass.ds(k * P * RELS, P * RELS), :].rearrange("(p r) f -> p r f", r=RELS),
                         stage[:, s, :, :]).then_inc(rel_out[s], 16)
        with sp.Fori(0, TILES // 2) as k2:
            rel_rows(k2 * 2, 0, k2)
            rel_rows(k2 * 2 + 1, 1, k2)
        rel_rows(TILES - 1, 0, TILES // 2)

        sp.wait_ge(sel_ready, 1)
        for s in range(TOP_K):
            e = sp.value_load(sel_i[0:1, s:s + 1], min_val=0, max_val=E0 - 1)
            sp.dma_start(s1[:, s, :, :], a["L1_ffn_W1"][bass.ds(e, 1), :, :]
                         .rearrange("o (k p) f -> p (o k) f", p=P)).then_inc(sel_ld, 16)
            sp.dma_start(s2[:, s, :, :], a["L1_ffn_W2"][bass.ds(e, 1), :, :]
                         .rearrange("o (k p) f -> p (o k) f", p=P)).then_inc(sel_ld, 16)
            sp.dma_start(b1s[:, s, :], a["L1_ffn_b1"][bass.ds(e, 1), :]
                         .rearrange("o (k p) -> (o k) p", p=P)).then_inc(sel_ld, 16)
            sp.dma_start(b2s[:, s, :], a["L1_ffn_b2"][bass.ds(e, 1), :]).then_inc(sel_ld, 16)
        with sp.Fori(0, TILES - 1) as k:
            sp.wait_ge(fin_ready, k + 1)
            sp.dma_start(out[bass.ds(k * P, P), :], x_res[:, k, :]).then_inc(out_done, 16)
        sp.wait_ge(fin_ready, TILES)
        sp.dma_start(out[(TILES - 1) * P:N_NODES, :], x_res[0:TAIL, TILES - 1, :]).then_inc(out_done, 16)
        sp.wait_ge(out_done, 16 * TILES)

    @block.gpsimd
    def _(g):
        g.memset(edge_i[:, 0, :], -1).then_inc(consts, 1)
        g.memset(edge_i[:, 1:4, :], 0).then_inc(consts, 1)
        g.memset(edge_f[:, 3, :], 0.0).then_inc(consts, 1)
        g.memset(x_res[:, TILES - 1, :], 0.0).then_inc(consts, 1)
        g.memset(xt[:, :, ROWS:], 0.0).then_inc(consts, 1)
        g.iota(iota_w[:, :], [[1, P]], base=0, channel_multiplier=0,
               allow_small_or_imprecise_dtypes=True).then_inc(consts, 1)
        g.iota(iota8[:, :], [[1, E0]], base=0, channel_multiplier=0,
               allow_small_or_imprecise_dtypes=True).then_inc(consts, 1)
        g.memset(ones[:, :], 1.0).then_inc(consts, 1)
        g.memset(zero_bf[:, :], 0.0).then_inc(consts, 1)
        g.wait_ge(consts, 8)
        g.affine_select(out=ident[:, :], in_=ones[:, :], compare_op=ALU.is_equal, fill=0.0,
                        base=0, pattern=[[-1, P]], channel_multiplier=1).then_inc(consts, 1)
        g.affine_select(out=row_mask[:, :], in_=ones[:, 0:TILES], compare_op=ALU.is_ge, fill=0.0,
                        base=N_NODES - 1, pattern=[[-P, TILES]], channel_multiplier=-1).then_inc(consts, 1)
        g.memset(zero_f[:, :], 0.0).then_inc(consts, 1)
        for l in range(AGGS):
            table = gcn_table[l] if l < 3 else rel_table
            idx = idx_src if l < 3 else idx_rel
            if l == 0:
                g.wait_ge(plan_ready, 1)
                passes = g.value_load(npass[0:1, 0:1], min_val=1, max_val=26)
            if l < 3:
                g.wait_ge(table_out[l], 16 * TILES)
            else:
                g.wait_ge(tr_ev[4], CHUNK + TILES)
                for s in range(2):
                    g.tensor_copy(xr[:, s, :, :], xt[:, :, s * P:(s + 1) * P]).then_inc(xr_copied, 1)
                with g.Fori(1, TILES // 2) as k2:
                    for s in range(2):
                        k = k2 * 2 + s
                        g.wait_ge(rel_mm, (k - 1) * 8)
                        g.tensor_copy(xr[:, s, :, :], xt[:, :, bass.ds(k * P, P)]).then_inc(xr_copied, 1)
                g.wait_ge(rel_mm, (TILES - 2) * 8)
                g.tensor_copy(xr[:, 0, :, :], xt[:, :, ROWS - P:ROWS]).then_inc(xr_copied, 1)
                g.wait_ge(rel_out[0], 16 * (TILES // 2 + 1))
                g.wait_ge(rel_out[1], 16 * (TILES // 2))
            if l > 0:
                g.wait_ge(agg_done, l)
            g.tensor_copy(idx_ring[:, l, 0, :], idx[:, 0, :]).then_inc(idx_copied[l], 1)
            with g.Fori(0, passes) as m:
                with g.Fori(0, GROUPS // RING) as i:
                    for s in range(RING):
                        t = m * GROUPS + i * RING + s
                        g.wait_ge(idx_copied[l], t + 1)
                        g.wait_ge(group_mm[l], t + 1)
                        g.tensor_copy(idx_ring[:, l, (s + 1) % RING, :],
                                      idx[:, i * RING + (s + 1), :]).then_inc(idx_copied[l], 1)
                        for j in range(GE):
                            g.indirect_dma_start(
                                out=ring[:, s, j, :], out_offset=None, in_=table[:, :],
                                in_offset=bass.IndirectOffsetOnAxis(ap=idx_ring[:, l, s, j:j + 1], axis=0),
                            ).then_inc(gathered[l][s], 16)
        g.wait_ge(ld_mix2, 64)
        with g.Fori(0, CHUNKS) as c:
            for u in range(CHUNK):
                k = c * CHUNK + u
                g.wait_ge(ln_row[3], k + 1)
                g.tensor_tensor(x_res[:, k, :], x_res[:, k, :], bet[:, :], ALU.add).then_inc(beta_added, 1)

    @block.tensor
    def _(pe):
        pe.wait_ge(consts, 12)
        for l in range(AGGS):
            pe.sem_inc(group_mm[l], 3)
        for k in range(4):
            pe.wait_ge(edges_f, min(k + 1, 3))
            if k == 3:
                pe.wait_ge(ld_edges, 16 * 8)
            for j in range(GE):
                mm = pe.transpose(ps[:, k, j * GROUPS:(j + 1) * GROUPS],
                                  edge_f[0:GROUPS, k, j * P:(j + 1) * P], ident[0:GROUPS, 0:GROUPS])
            mm.then_inc(edges_tr, 1)
        pe.wait_ge(gstat_ready, 1)
        pe.matmul(ps[:, 4, 0:GROUPS], gspread[0:GROUPS, 0, :], ident[0:GROUPS, 0:GROUPS], start=True, stop=True)
        pe.matmul(ps[:, 5, 0:GROUPS], gspread[0:GROUPS, 1, :], ident[0:GROUPS, 0:GROUPS],
                  start=True, stop=True).then_inc(gspread_mm, 1)
        deg = ps[:, 6, 0:TILES]
        pe.sem_inc(hist_mm, 2)
        pe.matmul(deg, zero_bf[:, :], zero_bf[:, 0:TILES], start=True, stop=False, skip_group_check=True)
        with pe.Fori(0, GROUPS // 2) as i:
            for s in range(2):
                pe.wait_ge(lo_1h, i * 2 + s + 1)
                pe.wait_ge(hi_1h, i * 2 + s + 1)
                for j in range(GE):
                    mm = pe.matmul(deg, lo1h[:, s, j, :], hi1h[:, s, j, :], start=False, stop=False,
                                   skip_group_check=True)
                mm.then_inc(hist_mm, 1)
        pe.matmul(deg, zero_bf[:, :], zero_bf[:, 0:TILES], start=False, stop=True,
                  skip_group_check=True).then_inc(hist_done, 1)

        def transposes(tile, ready, which, c, first=0):
            for u in range(CHUNK):
                k = c * CHUNK + u
                pe.wait_ge(ready, k + (first + 1))
                pe.wait_ge(tr_ev[which], k + 1)
                for h in range(HALVES):
                    mm = pe.transpose(ps[:, u, h * P:(h + 1) * P], tile(u)[:, h * P:(h + 1) * P], ident[:, :])
                mm.then_inc(tr_mm[which], 1)

        def chunk_row(u):
            return rows[:, u, :]

        for c in range(CHUNKS):
            transposes(lambda u: xn[:, c * CHUNK + u, :], ln_row[0], 0, c)
        pe.wait_ge(ld_mix, 16 * (3 * E0 + 12))
        for q in range(2):
            mm = pe.transpose(ps[:, 5, q * 80:(q + 1) * 80], bnp[:, q, :], ident[0:80, 0:80])
        mm.then_inc(bn_tr, 1)
        pe.wait_ge(plan_ready, 1)
        passes = pe.value_load(npass[0:1, 0:1], min_val=1, max_val=26)
        ordered = pe.value_load(npass[0:1, 1:2], min_val=0, max_val=1)
        pe.wait_ge(ld_gcn, 16 * 6)
        pe.wait_ge(bn_ready, 1)

        def group(l, t, turn, s):
            pe.wait_ge(gathered[l][s], (turn + 1) * (16 * GE))
            pe.wait_ge(onehot_ready[l], t + 1)
            pe.wait_ge(agg_added[l], t + 2)
            for h in range(HALVES):
                for j in range(GE):
                    mm = pe.matmul(ps[:, 7, h * P:(h + 1) * P], ring[:, s, j, h * P:(h + 1) * P],
                                   onehot[:, s % 2, j, :], start=(j == 0), stop=(j == GE - 1))
            mm.then_inc(group_mm[l], 1)

        def groups(l, t0, n):
            with pe.Fori(0, n // RING) as i:
                for s in range(RING):
                    group(l, t0 + i * RING + s, t0 // RING + i, s)

        def y_products(l, c):
            pe.wait_ge(xs_copied, l * CHUNKS + 1 + c)
            pe.wait_ge(tr_ev[l + 1 if l < 2 else 4], c * CHUNK + CHUNK)
            for u in range(CHUNK):
                if u % 2 == 0:
                    pe.wait_ge(y_ev, c * CHUNK + (l * TILES + min(u + 2, CHUNK)))
                for h in range(HALVES):
                    mm = pe.matmul(ps[:, 4 + u // 2, (u % 2) * D:(u % 2 + 1) * D], xs[:, h, u * P:(u + 1) * P],
                                   gw[:, l, h, :], start=(h == 0), stop=(h == 1))
                if u % 2 == 1 or u == CHUNK - 1:
                    mm.then_inc(y_mm, 1)

        def gcn_chunk(l, c, _):
            y_products(l, c)
            transposes(chunk_row, row_ready, l + 1, c, l * TILES)

        def experts_out(t, e):
            pe.wait_ge(l2_ev, t * 2 + 4)
            for u in range(CHUNK):
                if u % 2 == 0:
                    pe.wait_ge(yo_ev, t * CHUNK + min(u + 2, CHUNK))
                for h in range(HALVES):
                    mm = pe.matmul(ps[:, 4 + u // 2, (u % 2) * D:(u % 2 + 1) * D], h2[:, h, u * P:(u + 1) * P],
                                   wc[:, e, h, :], start=(h == 0), stop=(h == 1))
                if u % 2 == 1 or u == CHUNK - 1:
                    mm.then_inc(yo_mm, 1)

        def mix_chunk(l, c, t0):
            before, between, after = mix_plan(t0)
            y_products(l, c)
            for n in range(before):
                group(l, t0[0] + n, t0[1], n % RING)
            transposes(chunk_row, ln_row[1], 3, c)
            pe.wait_ge(tr_ev[3], c * CHUNK + 2 * CHUNK)
            for u in range(CHUNK):
                at = ps[:, 5, u * E0:(u + 1) * E0]
                pe.matmul(at, ones[0:1, :], br0[:, :], start=True, stop=False)
                for h in range(HALVES):
                    mm = pe.matmul(at, xs[:, h, u * P:(u + 1) * P], wr0[:, h, :], start=False, stop=(h == 1))
            mm.then_inc(rout_mm, 1)
            for e in range(E0):
                t = c * E0 + e
                for m in range(2):
                    pe.wait_ge(l2_ev, t * 2 + m + 1)
                    for n in range(2):
                        for h in range(HALVES):
                            mm = pe.matmul(ps[:, 2 * m + n, 0:NH], wa[:, e, h, m * P:(m + 1) * P],
                                           xs[:, h, n * NH:(n + 1) * NH], start=(h == 0), stop=(h == 1))
                    mm.then_inc(l1_mm, 1)
                if e == 1:
                    pe.wait_ge(rout_max, c + 1)
                if e > 0:
                    experts_out(t - 1, e - 1)
                    if between:
                        n = before + e - 1
                        group(l, t0[0] + n, t0[1] + n // RING, n % RING)
                pe.wait_ge(l1_ev, t * 2 + 2)
                for m in range(2):
                    for n in range(2):
                        for h in range(HALVES):
                            mm = pe.matmul(ps[:, 2 * m + n, 0:NH], wb[:, e, h, m * P:(m + 1) * P],
                                           h1[:, h, n * NH:(n + 1) * NH], start=(h == 0), stop=(h == 1))
                    mm.then_inc(l2_mm, 1)
            experts_out(c * E0 + (E0 - 1), E0 - 1)
            for n in range(before + between, before + between + after):
                group(l, t0[0] + n, t0[1] + n // RING, n % RING)
            transposes(chunk_row, ln_row[2], 4, c)

        def back_chunk(l, c, _):
            pe.wait_ge(xs_copied, l * CHUNKS + 1 + c)
            for u in range(CHUNK):
                pe.wait_ge(tr_ev[5], c * CHUNK + u + 1)
                for h in range(HALVES):
                    mm = pe.transpose(ps[:, u, h * P:(h + 1) * P], xs[:, h, u * P:(u + 1) * P], ident[:, :])
                mm.then_inc(back_mm, 1)
            transposes(chunk_row, rows_copied, 5, c)
            for u in range(CHUNK):
                for h in range(HALVES):
                    mm = pe.matmul(ps[:, 5 + h, 0:1], rows[:, u, h * P:(h + 1) * P],
                                   row_mask[:, bass.ds(c * CHUNK + u, 1)], start=False, stop=False,
                                   skip_group_check=True)
            mm.then_inc(mean_mm, 1)

        def stage_of(l, chunk):
            with pe.If_eq(pe.to_reg(ordered), 1):
                groups(l, 0, PROLOGUE)
                with pe.Fori(0, 3) as c:
                    t0 = c * PROLOGUE + PROLOGUE
                    chunk(l, c, (t0, c * (PROLOGUE // RING) + PROLOGUE // RING, FOLLOW[0]))
                    if chunk is not mix_chunk:
                        with pe.Fori(0, FOLLOW[0] // RING) as i:
                            for s in range(RING):
                                group(l, t0 + i * RING + s, (c + 1) * (PROLOGUE // RING) + i, s)
                for c in (3, 4):
                    t0 = PROLOGUE * (c + 1) if c == 3 else GROUPS
                    chunk(l, c, (t0, t0 // RING, FOLLOW[c]))
                    if chunk is not mix_chunk and FOLLOW[c]:
                        groups(l, t0, FOLLOW[c])
            with pe.Else():
                with pe.Fori(0, passes) as m:
                    with pe.Fori(0, GROUPS // RING) as i:
                        for s in range(RING):
                            group(l, m * GROUPS + i * RING + s, m * (GROUPS // RING) + i, s)
                with pe.Fori(0, CHUNKS) as c:
                    chunk(l, c, (0, 0, 0))

        stage_of(0, gcn_chunk)
        stage_of(1, gcn_chunk)
        stage_of(2, mix_chunk)

        pe.wait_ge(ld_rel, 16 * (2 * E0 + HALVES))
        pe.wait_ge(tr_ev[4], CHUNK + TILES)
        for k in range(TILES):
            for h in range(HALVES):
                mm = pe.matmul(ps[:, 7, k * RELS:(k + 1) * RELS], xt[:, h, k * P:(k + 1) * P], rg[:, h, :],
                               start=(h == 0), stop=(h == 1))
        mm.then_inc(gate_mm, 1)
        pe.wait_ge(gate_ready, 1)

        def rel_products(k, s):
            pe.wait_ge(xr_copied, k + 1)
            for r in range(RELS // 2):
                pe.wait_ge(rel_ev_v if r % 2 else rel_ev_a, k * 4 + r // 2 + 1)
                for h in range(HALVES):
                    mm = pe.matmul(ps[:, (r % 2) * 4 + r // 2, :], xr[:, s, h, :],
                                   rw[:, h, 2 * r:2 * r + 2, :].rearrange("p r f -> p (r f)"),
                                   start=(h == 0), stop=(h == 1))
                mm.then_inc(rel_mm, 1)

        with pe.Fori(0, TILES // 2) as k2:
            for s in range(2):
                rel_products(k2 * 2 + s, s)
        rel_products(TILES - 1, 0)

        pe.wait_ge(rel_ev_v, 4 * TILES + 4)
        for h in range(HALVES):
            pe.matmul(ps[:, 5 + h, 0:1], ident[:, :], zero_f[:, 0:1], start=True, stop=False, skip_group_check=True)
        stage_of(3, back_chunk)
        for h in range(HALVES):
            mm = pe.matmul(ps[:, 5 + h, 0:1], ident[:, :], zero_f[:, 0:1], start=False, stop=True,
                           skip_group_check=True)
        mm.then_inc(mean_mm, 1)

        pe.wait_ge(mean_ev, 1)
        pe.wait_ge(ld_mix2, 64)
        for h in range(HALVES):
            mm = pe.matmul(ps[0:1, 6, 0:E0], mean_t[:, h:h + 1], wr1[:, h, :], start=(h == 0), stop=(h == 1))
        mm.then_inc(log_mm, 1)
        pe.wait_ge(wsel_in, 1)
        pe.matmul(ps[:, 6, 16:16 + TOP_K], ones[0:1, :], small[:, 8, 0:TOP_K], start=True, stop=True).then_inc(wsel_mm, 1)
        pe.wait_ge(sel_ld, 16 * 4 * TOP_K)
        for s in range(TOP_K):
            mm = pe.transpose(ps[:, 7, s * FT:(s + 1) * FT], b1s[:, s, :], ident[0:FT, 0:FT])
        mm.then_inc(sel_tr, 1)
        pe.wait_ge(sel_ev, 1)
        pe.wait_ge(w2_scaled, TOP_K)
        pe.wait_ge(b2_ready, 1)
        pe.wait_ge(tr_ev[5], CHUNK + TILES)
        with pe.Fori(0, CHUNKS) as c:
            for s in range(TOP_K):
                for f in range(FT):
                    q = s * FT + f
                    pe.wait_ge(hid_ev, (c * TOP_K * FT) + q + 1)
                    for n in range(2):
                        for h in range(HALVES):
                            mm = pe.matmul(ps[:, 2 * (q % 2) + n, 0:NH], s1[:, s, h, f * P:(f + 1) * P],
                                           xt[:, h, bass.ds(c * CROWS + n * NH, NH)], start=(h == 0), stop=(h == 1))
                    mm.then_inc(hid_mm, 1)
            pe.wait_ge(hid_ev, (c + 1) * TOP_K * FT + 2)
            for u in range(CHUNK):
                if u % 2 == 0:
                    pe.wait_ge(fo_ev, c * CHUNK + min(u + 2, CHUNK))
                acc = ps[:, 4 + u // 2, (u % 2) * D:(u % 2 + 1) * D]
                pe.matmul(acc, ones[0:1, :], b2m[:, 1, :], start=True, stop=False)
                for s in range(TOP_K):
                    for f in range(FT):
                        mm = pe.matmul(acc, hh[:, s, f, u * P:(u + 1) * P], s2[:, s, f, :], start=False,
                                       stop=(s == TOP_K - 1 and f == FT - 1))
                if u % 2 == 1 or u == CHUNK - 1:
                    mm.then_inc(fo_mm, 1)

    @block.scalar
    def _(act):
        for i in range(6):
            act.sem_inc(tr_ev[i], CHUNK)
        act.sem_inc(l2_ev, 2)
        act.sem_inc(hid_ev, 2)
        act.sem_inc(rel_ev_a, 4)

        def evacuate(which, c, dst):
            for u in range(CHUNK):
                k = c * CHUNK + u
                act.wait_ge(tr_mm[which], k + 1)
                act.activation(dst(k, u), ps[:, u, 0:D].rearrange("p (h n) -> p h n", h=HALVES),
                               ACT.Copy).then_inc(tr_ev[which], 1)

        def into_xt(k, u):
            return xt[:, :, bass.ds(k * P, P)]

        def into_xs(k, u):
            return xs[:, :, u * P:(u + 1) * P]

        def ln_sqrt(i, c):
            act.wait_ge(ln_var[i], c + 1)
            act.activation(rstd[:, :], rstd[:, :], ACT.Sqrt).then_inc(ln_sd[i], 1)

        def copy_sums(l, c):
            act.wait_ge(chunk_summed, l * CHUNKS + 1 + c)
            act.activation(xs[:, :, :], xt[:, :, bass.ds(c * CROWS, CROWS)], ACT.Copy).then_inc(xs_copied, 1)

        act.wait_ge(deg_in, 1)
        act.activation(dinv[:, :], dinv[:, :], ACT.Sqrt).then_inc(deg_sd, 1)
        act.wait_ge(ln_var[0], CHUNKS)
        act.activation(rstd0[:, :], rstd0[:, :], ACT.Sqrt).then_inc(ln_sd[0], 1)
        with act.Fori(0, CHUNKS) as c:
            evacuate(0, c, into_xt)
        act.wait_ge(bn_var, 1)
        act.activation(bn_s[:, :, :], bn_s[:, :, :], ACT.Sqrt).then_inc(bn_sd, 1)
        for l in range(2):
            with act.Fori(0, CHUNKS) as c:
                copy_sums(l, c)
                for u in range(CHUNK):
                    k = c * CHUNK + u
                    act.wait_ge(y_ev, k + (l * TILES + CHUNK + 1))
                    act.activation(rows[:, u, :], rows[:, u, :], ACT.Gelu_apprx_tanh).then_inc(gelu_done, 1)
                for u in range(CHUNK):
                    k = c * CHUNK + u
                    act.wait_ge(gelu_done, k + (l * TILES + 1))
                    act.activation(rows[:, u, :], rows[:, u, :], ACT.Copy,
                                   scale=dinv[:, bass.ds(k, 1)]).then_inc(row_ready, 1)
                evacuate(l + 1, c, into_xt)
        with act.Fori(0, CHUNKS) as c:
            copy_sums(2, c)
            ln_sqrt(1, c)
            evacuate(3, c, into_xs)
            act.wait_ge(rout_max, c + 1)
            act.activation(rout[:, :, :], rout[:, :, :], ACT.Exp).then_inc(rout_exp, 1)
            for e in range(E0):
                t = c * E0 + e
                for layer, (mm, ev, h) in enumerate(((l1_mm, l1_ev, h1), (l2_mm, l2_ev, h2))):
                    for m in range(2):
                        act.wait_ge(mm, t * 2 + m + 1)
                        col = 2 * e + m
                        act.activation(h[:, m, :].rearrange("p (n w) -> p n w", n=2), ps[:, 2 * m:2 * m + 2, 0:NH],
                                       ACT.Relu, bias=bn_t[:, layer, col:col + 1],
                                       scale=bn_s[:, layer, col:col + 1]).then_inc(ev, 1)
            ln_sqrt(2, c)
            evacuate(4, c, into_xt)
        act.wait_ge(gate_mm, 1)
        act.activation(gates[:, :, :].rearrange("p t r -> p (t r)"), ps[:, 7, 0:TILES * RELS],
                       ACT.Sigmoid).then_inc(gate_ready, 1)
        act.wait_ge(gate_ready, 1)

        def rel_evac(k, s):
            for r in range(0, RELS // 2, 2):
                act.wait_ge(rel_mm, k * 8 + r + 1)
                for q in range(2):
                    rel = 2 * r + q
                    ins = act.activation(stage[:, s, rel, :], ps[:, r // 2, q * D:(q + 1) * D], ACT.Copy,
                                         scale=gates[:, k, rel:rel + 1])
                ins.then_inc(rel_ev_a, 1)

        rel_evac(0, 0)
        rel_evac(1, 1)
        with act.Fori(1, TILES // 2) as k2:
            for s in range(2):
                act.wait_ge(rel_out[s], k2 * 16)
                rel_evac(k2 * 2 + s, s)
        act.wait_ge(rel_out[0], (TILES // 2) * 16)
        rel_evac(TILES - 1, 0)
        with act.Fori(0, CHUNKS) as c:
            copy_sums(3, c)
            ln_sqrt(3, c)
            for u in range(CHUNK):
                k = c * CHUNK + u
                act.wait_ge(ln_row[3], k + 1)
                act.activation(rows[:, u, :], xn[:, k, :], ACT.Copy).then_inc(rows_copied, 1)
            evacuate(5, c, into_xt)
            act.wait_ge(mean_mm, c + 1)
        for i in range(2):
            act.wait_ge(exp_in, i + 1)
            act.activation(small[:, 1, :], small[:, 1, :], ACT.Exp).then_inc(exp_out, 1)
        act.wait_ge(exp_in, 3)
        act.activation(small[:, 9, 0:1], small[:, 9, 0:1], ACT.Exp).then_inc(exp_out, 1)
        act.wait_ge(sel_ev, 1)

        def hidden(c, with_sqrt):
            for s in range(TOP_K):
                for f in range(FT):
                    q = s * FT + f
                    if with_sqrt and q == FT:
                        ln_sqrt(4, c - 1)
                    act.wait_ge(hid_mm, c * (TOP_K * FT) + q + 1)
                    act.activation(hh[:, s, f, :].rearrange("p (n w) -> p n w", n=2),
                                   ps[:, 2 * (q % 2):2 * (q % 2) + 2, 0:NH], ACT.Gelu,
                                   bias=b1c[:, s, f:f + 1]).then_inc(hid_ev, 1)

        hidden(0, False)
        with act.Fori(1, CHUNKS) as c:
            hidden(c, True)
        ln_sqrt(4, CHUNKS - 1)

    @block.vector
    def _(v):
        once = Steps(v, once_steps)
        v.sem_inc(y_ev, CHUNK)
        for i in range(AGGS):
            v.sem_inc(agg_added[i], 2)
        v.sem_inc(yo_ev, CHUNK)
        v.sem_inc(rel_ev_v, 4)
        v.sem_inc(fo_ev, CHUNK)

        v.wait_ge(consts, 12)
        v.wait_ge(ld_edges, 16 * 8)
        for k in range(3):
            v.tensor_copy(edge_f[0:GROUPS, k, :], edge_i[0:GROUPS, k, :]).then_inc(edges_f, 1)
        v.wait_ge(edges_f, 3)
        dst_rows = edge_f[0:GROUPS, 0, :]
        once.done(v.tensor_scalar(tmpe[0:GROUPS, 0, :], dst_rows, 0.0, BIG, ALU.is_lt, ALU.mult))
        once.done(v.tensor_tensor(tmpe[0:GROUPS, 1, :], tmpe[0:GROUPS, 0, :], dst_rows, ALU.add))
        once.done(v.tensor_reduce(gstat[0:GROUPS, 0:1], tmpe[0:GROUPS, 1, :], AX_X, ALU.min))
        once.done(v.tensor_reduce(gstat[0:GROUPS, 1:2], dst_rows, AX_X, ALU.max))
        once.done(v.tensor_tensor(gstat[0:GROUPS, 2:3], gstat[0:GROUPS, 1:2], gstat[0:GROUPS, 0:1], ALU.subtract))
        v.tensor_scalar(gspread[0:GROUPS, 0, :], ones[0:GROUPS, :], gstat[0:GROUPS, 0:1], None, ALU.mult)
        v.tensor_scalar(gspread[0:GROUPS, 1, :], ones[0:GROUPS, :], gstat[0:GROUPS, 2:3], None,
                        ALU.mult).then_inc(gstat_ready, 1)

        def column(k):
            return ps[:, k, 0:GROUPS * GE].rearrange("p (j g) -> p g j", j=GE)

        v.wait_ge(edges_tr, 4)
        once.done(v.tensor_copy(dstc[:, :, :], column(0)))
        once.done(v.tensor_copy(tmpci[:, 2, :, :], dstc[:, :, :]))
        v.tensor_scalar(tmpci[:, 0, :, :], tmpci[:, 2, :, :], P - 1, None, ALU.bitwise_and)
        once.done(v.tensor_scalar(tmpci[:, 1, :, :], tmpci[:, 2, :, :], 7, None, ALU.arith_shift_right))
        v.tensor_copy(tmpc[:, 0, :, :], tmpci[:, 0, :, :])
        v.tensor_copy(iota_bf[:, :], iota_w[:, :])
        v.tensor_copy(tmpc[:, 1, :, :], tmpci[:, 1, :, :]).then_inc(digits_ready, 1)
        v.wait_ge(digits_ready, 1)

        with v.Fori(0, GROUPS // 2) as i:
            for s in range(2):
                n = i * 2 + s
                v.wait_ge(hist_mm, n + 1)
                for j in range(GE):
                    ins = v.tensor_scalar(lo1h[:, s, j, :], iota_bf[:, :], tmpc[:, 0, n, j:j + 1], None, ALU.is_equal)
                ins.then_inc(lo_1h, 1)
                v.tensor_tensor(hi1h[:, s, :, :], tmpc[:, 1, n, :].unsqueeze(2).to_broadcast([P, GE, TILES]),
                                iota_w[:, 0:TILES].unsqueeze(1).to_broadcast([P, GE, TILES]),
                                ALU.is_equal).then_inc(hi_1h, 1)

        v.tensor_copy(tmpc[:, 2, :, :], column(1))
        v.tensor_copy(tmpc[:, 3, :, :], column(2))
        once.done(v.tensor_copy(wgtc[:, :, :], column(3)))
        once.done(v.tensor_copy(idx_src[:, 0:GROUPS, :], tmpc[:, 2, :, :]))
        once.done(v.scalar_tensor_tensor(out=idx_rel[:, 0:GROUPS, :], in0=tmpc[:, 2, :, :], scalar=float(RELS),
                                         in1=tmpc[:, 3, :, :], op0=ALU.mult, op1=ALU.add))
        v.tensor_copy(idx_src[:, GROUPS, :], idx_src[:, 0, :])
        v.tensor_copy(idx_rel[:, GROUPS, :], idx_rel[:, 0, :])
        v.wait_ge(gspread_mm, 1)
        v.tensor_copy(base0[:, :], ps[:, 4, 0:GROUPS])
        once.done(v.tensor_copy(span_i[:, :], ps[:, 5, 0:GROUPS]))
        once.done(v.tensor_scalar(base_i[:, :], span_i[:, :], 7, None, ALU.arith_shift_right))
        once.done(v.tensor_copy(base_f[:, :], base_i[:, :]))
        once.done(v.tensor_reduce(npass_f[:, 0:1], base_f[:, :], AX_X, ALU.max))
        v.tensor_scalar(npass_f[:, 1:2], npass_f[:, 0:1], 0.0, None, ALU.is_equal)
        for c in range(CHUNKS - 1):
            once.done(v.tensor_reduce(npass_f[:, 2:3], base0[:, PROLOGUE * (c + 1):GROUPS], AX_X, ALU.min))
            once.done(v.tensor_scalar(npass_f[:, 2:3], npass_f[:, 2:3], float(CROWS * (c + 1)), None, ALU.is_ge))
            once.done(v.tensor_tensor(npass_f[:, 1:2], npass_f[:, 1:2], npass_f[:, 2:3], ALU.mult))
        v.tensor_copy(npass[:, 1:2], npass_f[:, 1:2])
        once.done(v.tensor_scalar(npass[:, 0:1], npass_f[:, 0:1], 1.0, None, ALU.add))
        v.sem_inc(plan_ready, 1)

        def row_stats(steps, src, i, c, st=stats[:, :, :], mn=mean[:, :], var=rstd[:, :], hf=half[:, :]):
            v.memset(hf, 0.0)
            for u in range(CHUNK):
                ins = v.bn_stats(st[:, u, :], src[:, c * CHUNK + u, :])
            steps.done(ins)
            v.tensor_tensor(mn, st[:, :, 1], st[:, :, 4], ALU.add)
            v.tensor_tensor(var, st[:, :, 2], st[:, :, 5], ALU.add)
            steps.done(v.tensor_tensor(hf, st[:, :, 1], st[:, :, 4], ALU.subtract))
            v.tensor_scalar(mn, mn, 0.5, None, ALU.mult)
            v.tensor_scalar(var, var, 1.0 / D, LN_EPS, ALU.mult, ALU.add)
            steps.done(v.scalar_tensor_tensor(out=hf, in0=hf, scalar=0.25, in1=hf, op0=ALU.mult, op1=ALU.mult))
            v.tensor_tensor(var, var, hf, ALU.add).then_inc(ln_var[i], 1)

        def one_over_sd(steps, i, c):
            v.wait_ge(ln_sd[i], c + 1)
            steps.done(v.reciprocal(rstd[:, :], rstd[:, :]))

        def normalise(i, c, dst):
            for u in range(CHUNK):
                k = c * CHUNK + u
                v.tensor_scalar(dst(k, u), x_res[:, k, :], mean[:, u:u + 1], rstd[:, u:u + 1],
                                ALU.subtract, ALU.mult).then_inc(ln_row[i], 1)

        def into_xn(k, u):
            return xn[:, k, :]

        def into_rows(k, u):
            return rows[:, u, :]

        v.wait_ge(ld_x, 32)
        for c in range(CHUNKS):
            at = slice(c * CHUNK, (c + 1) * CHUNK)
            row_stats(once, x_res, 0, c, stats0[:, at, :], mean0[:, at], rstd0[:, at], half0[:, at])
        v.wait_ge(hist_done, 1)
        v.tensor_scalar(dinv[:, :], ps[:, 6, 0:TILES], 1.0, None, ALU.add).then_inc(deg_in, 1)
        v.wait_ge(deg_sd, 1)
        once.done(v.reciprocal(dinv[:, :], dinv[:, :]))
        v.wait_ge(ln_sd[0], 1)
        once.done(v.reciprocal(rstd0[:, :], rstd0[:, :]))
        once.done(v.tensor_tensor(rstd0[:, :], rstd0[:, :], dinv[:, :], ALU.mult))
        for k in range(TILES):
            v.tensor_scalar(xn[:, k, :], x_res[:, k, :], mean0[:, k:k + 1], rstd0[:, k:k + 1],
                            ALU.subtract, ALU.mult).then_inc(ln_row[0], 1)

        v.wait_ge(bn_tr, 1)
        once.done(v.tensor_copy(bnc[:, :, :, :].rearrange("p q n e -> p (q n e)"), ps[:, 5, 0:160]))
        v.tensor_scalar(bn_s[:, :, :], bnc[:, :, 4, :], BN_EPS, None, ALU.add).then_inc(bn_var, 1)
        v.wait_ge(bn_sd, 1)
        once.done(v.reciprocal(bn_s[:, :, :], bn_s[:, :, :]))
        once.done(v.tensor_tensor(bn_s[:, :, :], bn_s[:, :, :], bnc[:, :, 1, :], ALU.mult))
        once.done(v.tensor_tensor(bn_t[:, :, :], bnc[:, :, 0, :], bnc[:, :, 3, :], ALU.subtract))
        once.done(v.tensor_tensor(bn_t[:, :, :], bn_t[:, :, :], bn_s[:, :, :], ALU.mult))
        v.tensor_tensor(bn_t[:, :, :], bn_t[:, :, :], bnc[:, :, 2, :], ALU.add).then_inc(bn_ready, 1)

        passes = v.value_load(npass[0:1, 0:1], min_val=1, max_val=26)
        ordered = v.value_load(npass[0:1, 1:2], min_val=0, max_val=1)

        def onehots(l, n, t, s):
            v.wait_ge(group_mm[l], t + 2)
            for j in range(GE):
                scalar = rel_dst[:, n, j:j + 1]
                if l < 3:
                    ins = v.tensor_scalar(onehot[:, s % 2, j, :], iota_w[:, :], scalar, None, ALU.is_equal)
                else:
                    ins = v.tensor_scalar(onehot[:, s % 2, j, :], iota_w[:, :], scalar,
                                          wgtc[:, n, j:j + 1], ALU.is_equal, ALU.mult)
            ins.then_inc(onehot_ready[l], 1)

        def add(l, n, t):
            first = v.value_load(base_i[0:1, bass.ds(n, 1)], min_val=0, max_val=ROWS)
            v.wait_ge(group_mm[l], t + 4)
            v.wait_ge(agg_added[l], t + 2)
            window = xt[:, :, bass.ds(first, P)]
            v.tensor_tensor(window, ps[:, 7, 0:D].rearrange("p (h n) -> p h n", h=HALVES),
                            window, ALU.add).then_inc(agg_added[l], 1)

        def set_window(l, m):
            v.wait_ge(pass_base[l], m * 3 + 1)
            v.tensor_copy(base_i[:, :], base_f[:, :]).then_inc(pass_base[l], 1)
            v.tensor_tensor(rel_dst[:, :, :], dstc[:, :, :],
                            base_f[:, :].unsqueeze(2).to_broadcast([P, GROUPS, GE]),
                            ALU.subtract).then_inc(pass_base[l], 1)

        def groups(l, n0, t0, turns, m):
            with v.Fori(0, turns) as i:
                for s in range(RING):
                    v.wait_ge(pass_base[l], m * 3 + 3)
                    onehots(l, n0 + i * RING + s, t0 + i * RING + s, s)
                    add(l, n0 + i * RING + s, t0 + i * RING + s)

        def gcn_chunk(l, c, _):
            for u in range(CHUNK):
                k = c * CHUNK + u
                v.wait_ge(y_mm, c * UNITS + (l * CHUNKS * UNITS + u // 2 + 1))
                v.wait_ge(tr_ev[l + 1], c * CHUNK + CHUNK)
                v.wait_ge(rows_free, c + (l * CHUNKS + 1))
                v.scalar_tensor_tensor(out=rows[:, u, :], in0=ps[:, 4 + u // 2, (u % 2) * D:(u % 2 + 1) * D],
                                       scalar=dinv[:, bass.ds(k, 1)], in1=gb[:, l, :],
                                       op0=ALU.mult, op1=ALU.add).then_inc(y_ev, 1)

        def mix_chunk(l, c, t0):
            before, between, after = mix_plan(t0)
            steps = Steps(v, mix_steps, c, 11)
            for n in range(min(before, 2)):
                onehots(l, t0[0] + n, t0[0] + n, n)
            for u in range(CHUNK):
                k = c * CHUNK + u
                v.wait_ge(y_mm, c * UNITS + (l * CHUNKS * UNITS + u // 2 + 1))
                v.wait_ge(tr_ev[4], c * CHUNK + CHUNK)
                v.scalar_tensor_tensor(out=rows[:, u, :], in0=ps[:, 4 + u // 2, (u % 2) * D:(u % 2 + 1) * D],
                                       scalar=dinv[:, bass.ds(k, 1)], in1=gb[:, l, :],
                                       op0=ALU.mult, op1=ALU.add).then_inc(y_ev, 1)
            for u in range(CHUNK):
                k = c * CHUNK + u
                v.wait_ge(y_ev, k + (l * TILES + CHUNK + 1))
                v.tensor_tensor(x_res[:, k, :], x_res[:, k, :], rows[:, u, :], ALU.add).then_inc(gcn_added, 1)
            v.wait_ge(gcn_added, c * CHUNK + CHUNK)
            row_stats(steps, x_res, 1, c)
            for n in range(min(before, 1)):
                add(l, t0[0] + n, t0[0] + n)
            one_over_sd(steps, 1, c)
            normalise(1, c, into_rows)
            for n in range(1, before):
                add(l, t0[0] + n, t0[0] + n)
            v.wait_ge(rout_mm, c + 1)
            logits = ps[:, 5, 0:CHUNK * E0].rearrange("p (t e) -> p t e", e=E0)
            prob, top = rout[:, :, :], rtmp[:, :]
            over = top.unsqueeze(2).to_broadcast([P, CHUNK, E0])
            steps.done(v.tensor_reduce(top, logits, AX_X, ALU.max))
            v.tensor_tensor(prob, logits, over, ALU.subtract).then_inc(rout_max, 1)
            v.wait_ge(rout_exp, c + 1)
            steps.done(v.tensor_reduce(top, prob, AX_X, ALU.add))
            steps.done(v.reciprocal(top, top))
            v.tensor_tensor(prob, prob, over, ALU.mult).then_inc(rout_ready, 1)
            v.wait_ge(rout_ready, c + 1)
            for e in range(E0):
                t = c * E0 + e
                n = before + e
                if between and e < E0 - 1:
                    onehots(l, t0[0] + n, t0[0] + n, n)
                elif after and e == E0 - 1:
                    n = before + between
                    onehots(l, t0[0] + n, t0[0] + n, n)
                for u in range(CHUNK):
                    k = c * CHUNK + u
                    v.wait_ge(yo_ev, t * CHUNK + u + 1)
                    v.scalar_tensor_tensor(out=x_res[:, k, :], in0=bob[:, e, :], scalar=rout[:, u, e:e + 1],
                                           in1=x_res[:, k, :], op0=ALU.mult, op1=ALU.add).then_inc(bo_added, 1)
                for u in range(CHUNK):
                    k = c * CHUNK + u
                    v.wait_ge(bo_added, t * CHUNK + u + 1)
                    v.wait_ge(yo_mm, t * UNITS + u // 2 + 1)
                    v.scalar_tensor_tensor(out=x_res[:, k, :], in0=ps[:, 4 + u // 2, (u % 2) * D:(u % 2 + 1) * D],
                                           scalar=rout[:, u, e:e + 1], in1=x_res[:, k, :],
                                           op0=ALU.mult, op1=ALU.add).then_inc(yo_ev, 1)
                if between and e < E0 - 1:
                    add(l, t0[0] + n, t0[0] + n)
            v.wait_ge(yo_ev, (c * E0 + E0) * CHUNK + CHUNK)
            row_stats(steps, x_res, 2, c)
            n0 = before + between
            for n in range(n0, n0 + after):
                if n + 1 < n0 + after:
                    onehots(l, t0[0] + n + 1, t0[0] + n + 1, n + 1)
                add(l, t0[0] + n, t0[0] + n)
                if n == n0:
                    one_over_sd(steps, 2, c)
                    normalise(2, c, into_rows)
            if not after:
                one_over_sd(steps, 2, c)
                normalise(2, c, into_rows)
            steps.end()

        def back_chunk(l, c, _):
            steps = Steps(v, back_steps, c, 4)
            for u in range(CHUNK):
                k = c * CHUNK + u
                v.wait_ge(back_mm, k + 1)
                v.scalar_tensor_tensor(out=x_res[:, k, :], in0=ps[:, u, 0:D], scalar=0.0, in1=x_res[:, k, :],
                                       op0=ALU.max, op1=ALU.add).then_inc(back_ev, 1)
            v.wait_ge(back_ev, c * CHUNK + CHUNK)
            row_stats(steps, x_res, 3, c)
            one_over_sd(steps, 3, c)
            normalise(3, c, into_xn)
            steps.end()

        def stage_of(l, chunk):
            def summed(added):
                v.wait_ge(agg_added[l], added + 2)
                v.sem_inc(chunk_summed, 1)

            v.tensor_copy(base_f[:, :], base0[:, :]).then_inc(pass_base[l], 1)
            with v.If_eq(v.to_reg(ordered), 1):
                set_window(l, 0)
                groups(l, 0, 0, PROLOGUE // RING, 0)
                with v.Fori(0, 3) as c:
                    t0 = c * PROLOGUE + PROLOGUE
                    summed(t0)
                    chunk(l, c, (t0, 0, FOLLOW[0]))
                    if chunk is not mix_chunk:
                        groups(l, t0, t0, FOLLOW[0] // RING, 0)
                for c in (3, 4):
                    t0 = PROLOGUE * (c + 1) if c == 3 else GROUPS
                    summed(t0)
                    chunk(l, c, (t0, 0, FOLLOW[c]))
                    if chunk is not mix_chunk and FOLLOW[c]:
                        groups(l, t0, t0, FOLLOW[c] // RING, 0)
                v.sem_inc(agg_done, 1)
            with v.Else():
                with v.Fori(0, passes) as m:
                    set_window(l, m)
                    groups(l, 0, m * GROUPS, GROUPS // RING, m)
                    v.tensor_scalar(base_f[:, :], base_f[:, :], float(P), float(ROWS), ALU.add,
                                    ALU.min).then_inc(pass_base[l], 1)
                with v.Fori(0, CHUNKS) as c:
                    summed(passes * GROUPS)
                    chunk(l, c, (0, 0, 0))
                v.wait_ge(pass_base[l], passes * 3 + 1)
                v.sem_inc(agg_done, 1)

        v.wait_ge(tr_ev[0], CHUNK + TILES)
        stage_of(0, gcn_chunk)
        v.wait_ge(tr_ev[1], CHUNK + TILES)
        stage_of(1, gcn_chunk)
        v.wait_ge(tr_ev[2], CHUNK + TILES)
        v.wait_ge(ld_bo, 16)
        stage_of(2, mix_chunk)

        v.wait_ge(gate_ready, 1)

        def rel_evac(k, s):
            for r in range(1, RELS // 2, 2):
                v.wait_ge(rel_mm, k * 8 + r + 1)
                for q in range(2):
                    rel = 2 * r + q
                    ins = v.tensor_scalar(stage[:, s, rel, :], ps[:, 4 + r // 2, q * D:(q + 1) * D],
                                          gates[:, k, rel:rel + 1], None, ALU.mult)
                ins.then_inc(rel_ev_v, 1)

        rel_evac(0, 0)
        rel_evac(1, 1)
        with v.Fori(1, TILES // 2) as k2:
            for s in range(2):
                v.wait_ge(rel_out[s], k2 * 16)
                rel_evac(k2 * 2 + s, s)
        v.wait_ge(rel_out[0], (TILES // 2) * 16)
        rel_evac(TILES - 1, 0)
        v.wait_ge(xr_copied, TILES)
        once.done(v.memset(xt[:, :, :], 0.0))
        v.wait_ge(rel_out[0], 16 * (TILES // 2 + 1))
        v.wait_ge(rel_out[1], 16 * (TILES // 2))
        stage_of(3, back_chunk)

        v.wait_ge(mean_mm, CHUNKS + 1)
        v.tensor_scalar(mean_t[:, :], ps[:, 5:5 + HALVES, 0], 1.0 / N_NODES, None, ALU.mult).then_inc(mean_ev, 1)
        v.wait_ge(log_mm, 1)

        def row(i, n=E0, at=0):
            return small[:, i, at:at + n]

        def softmax(i):
            once.done(v.tensor_reduce(row(2, 1), row(1), AX_X, ALU.max))
            v.tensor_scalar(row(1), row(1), row(2, 1), None, ALU.subtract).then_inc(exp_in, 1)
            v.wait_ge(exp_out, i + 1)
            once.done(v.tensor_reduce(row(2, 1), row(1), AX_X, ALU.add))
            once.done(v.reciprocal(row(2, 1), row(2, 1)))
            once.done(v.tensor_scalar(row(1), row(1), row(2, 1), None, ALU.mult))

        once.done(v.tensor_tensor(row(1), ps[0:1, 6, 0:E0], row(0), ALU.add))
        softmax(0)
        once.done(v.tensor_scalar(row(3), row(1), float(N_NODES), CAPACITY, ALU.mult, ALU.max))
        once.done(v.reciprocal(row(3), row(3)))
        once.done(v.tensor_scalar(row(3), row(3), CAPACITY, None, ALU.mult))
        once.done(v.tensor_tensor(row(1), row(1), row(3), ALU.mult))
        softmax(1)
        v.tensor_scalar(row(6), iota8[:, :], -1.0, float(E0), ALU.mult, ALU.add)
        for s in range(TOP_K):
            once.done(v.tensor_reduce(row(4, 1, s), row(1), AX_X, ALU.max))
            once.done(v.tensor_scalar(row(5), row(1), row(4, 1, s), None, ALU.is_equal))
            once.done(v.tensor_tensor(row(5), row(5), row(6), ALU.mult))
            once.done(v.tensor_reduce(row(7, 1), row(5), AX_X, ALU.max))
            once.done(v.tensor_scalar(row(7, 1, 1 + s), row(7, 1), -1.0, float(E0), ALU.mult, ALU.add))
            once.done(v.tensor_scalar(row(5), iota8[:, :], row(7, 1, 1 + s), -2.0, ALU.is_equal, ALU.mult))
            once.done(v.tensor_tensor(row(1), row(1), row(5), ALU.add))
        v.tensor_copy(sel_i[:, 0:TOP_K], row(7, TOP_K, 1)).then_inc(sel_ready, 1)
        v.tensor_tensor(row(9, 1), row(4, 1, 1), row(4, 1, 0), ALU.subtract).then_inc(exp_in, 1)
        v.wait_ge(exp_out, 3)
        once.done(v.tensor_scalar(row(10, 1), row(9, 1), 1.0, None, ALU.add))
        once.done(v.reciprocal(row(8, 1), row(10, 1)))
        v.tensor_tensor(row(8, 1, 1), row(8, 1), row(9, 1), ALU.mult).then_inc(wsel_in, 1)
        v.wait_ge(wsel_in, 1)
        v.wait_ge(wsel_mm, 1)
        once.done(v.tensor_copy(wsel[:, :], ps[:, 6, 16:16 + TOP_K]))
        v.wait_ge(sel_ld, 16 * 4 * TOP_K)
        v.wait_ge(sel_tr, 1)
        v.tensor_copy(b1c[:, :, :].rearrange("p s f -> p (s f)"), ps[:, 7, 0:TOP_K * FT]).then_inc(sel_ev, 1)
        for s in range(TOP_K):
            w = s2[:, s, :, :].rearrange("p k f -> p (k f)")
            v.tensor_scalar(w, w, wsel[:, s:s + 1], None, ALU.mult).then_inc(w2_scaled, 1)
        once.done(v.tensor_scalar(b2m[:, 0, :], b2s[:, 0, :], wsel[0:1, 0:1], None, ALU.mult))
        v.scalar_tensor_tensor(out=b2m[:, 1, :], in0=b2s[:, 1, :], scalar=wsel[0:1, 1:2], in1=b2m[:, 0, :],
                               op0=ALU.mult, op1=ALU.add).then_inc(b2_ready, 1)
        with v.Fori(0, CHUNKS) as c:
            steps = Steps(v, out_steps, c, 4)
            for u in range(CHUNK):
                k = c * CHUNK + u
                v.wait_ge(fo_mm, c * UNITS + u // 2 + 1)
                v.tensor_tensor(xn[:, k, :], ps[:, 4 + u // 2, (u % 2) * D:(u % 2 + 1) * D], xn[:, k, :],
                                ALU.add).then_inc(fo_ev, 1)
            v.wait_ge(fo_ev, c * CHUNK + 2 * CHUNK)
            row_stats(steps, xn, 4, c)
            one_over_sd(steps, 4, c)
            v.wait_ge(beta_added, c * CHUNK + CHUNK)
            for u in range(CHUNK):
                k = c * CHUNK + u
                v.scalar_tensor_tensor(out=xn[:, k, :], in0=xn[:, k, :], scalar=mean[:, u:u + 1],
                                       in1=gam[:, :], op0=ALU.subtract, op1=ALU.mult).then_inc(fin_scaled, 1)
            for u in range(CHUNK):
                k = c * CHUNK + u
                v.wait_ge(fin_scaled, k + 1)
                v.scalar_tensor_tensor(out=x_res[:, k, :], in0=xn[:, k, :], scalar=rstd[:, u:u + 1],
                                       in1=x_res[:, k, :], op0=ALU.mult, op1=ALU.add).then_inc(fin_ready, 1)
            steps.end()


_INS = ["x", "src", "dst", "edge_type_16", "edge_weight1",
        "L0_gnn_W1", "L0_gnn_b1", "L0_gnn_W2", "L0_gnn_b2", "L0_gnn_W3", "L0_gnn_b3",
        "L0_ffn_Wr", "L0_ffn_br", "L0_ffn_W1", "L0_ffn_b1", "L0_ffn_g1", "L0_ffn_be1", "L0_ffn_m1", "L0_ffn_v1",
        "L0_ffn_W2", "L0_ffn_b2", "L0_ffn_g2", "L0_ffn_be2", "L0_ffn_m2", "L0_ffn_v2", "L0_ffn_Wo", "L0_ffn_bo",
        "L1_gnn_weight", "L1_gnn_gate_weight",
        "L1_ffn_Wr", "L1_ffn_br", "L1_ffn_W1", "L1_ffn_b1", "L1_ffn_W2", "L1_ffn_b2", "L1_ffn_gamma", "L1_ffn_beta"]


def kernel(**inputs):
    import numpy as np
    import concourse.bacc as bacc
    from concourse.bass_utils import run_bass_kernel_spmd

    nc = bacc.Bacc("TRN2", target_bir_lowering=False, num_devices=1)
    arrays, aps = {}, {}
    for name in _INS:
        arr = np.ascontiguousarray(inputs[name])
        arrays["in_" + name] = arr
        aps[name] = nc.dram_tensor("in_" + name, arr.shape, mybir.dt.from_np(arr.dtype), kind="ExternalInput").ap()
    result = nc.dram_tensor("result", (N_NODES, D), F32, kind="ExternalOutput").ap()
    build(nc, aps, result)
    r = run_bass_kernel_spmd(nc, [arrays], core_ids=[0])
    return r.results[0]["result"]
```

```python
from contextlib import ExitStack

import concourse.bass as bass
from concourse import mybir
from concourse.alu_op_type import AluOpType as ALU

F32 = mybir.dt.float32
BF16 = mybir.dt.bfloat16
I32 = mybir.dt.int32
ACT = mybir.ActivationFunctionType
AX_X = mybir.AxisListType.X

P = 128
N_NODES = 3125
N_EDGES = 53125
D = 256
HALVES = D // P
TILES = -(-N_NODES // P)
ROWS = TILES * P
TAIL = N_NODES - (TILES - 1) * P
CHUNK = 5
CHUNKS = TILES // CHUNK
UNITS = -(-CHUNK // 2)
CROWS = CHUNK * P
NH = CROWS // 2
GE = 8
GROUP = GE * P
GROUPS = -(-N_EDGES // GROUP)
GTAIL = N_EDGES - (GROUPS - 1) * GROUP
RING = 4
RELS = 16
E0 = 8
F1 = 512
FT = F1 // P
TOP_K = 2
LN_EPS = 1e-5
BN_EPS = 1e-3
PROLOGUE = 12
FOLLOW = [12, 12, 12, 4, 0]
AGGS = 4
BIG = 4096.0
CAPACITY = float(-(-(N_NODES * 5) // (4 * E0)))


class Steps:

    def __init__(self, eng, sem, turn=0, per_turn=0):
        self.eng, self.sem, self.n, self.base, self.per_turn = eng, sem, 0, turn * per_turn, per_turn

    def done(self, ins):
        ins.then_inc(self.sem, 1)
        self.n += 1
        self.eng.wait_ge(self.sem, self.base + self.n)

    def end(self):
        assert self.n == self.per_turn, self.n


def mix_plan(follow):
    if follow == PROLOGUE:
        return 3, (0, 2, 3, 4, 5, 6, 7), 2
    return (3, (), follow - 3) if follow else (0, (), 0)


def streamed(c, n):
    real = N_NODES - (CHUNKS - 1) * CROWS if isinstance(c, int) and c == CHUNKS - 1 else CROWS
    return min(NH, real - n * NH)


def build(nc, a, out):
    with ExitStack() as ctx:
        _build(nc, a, out, ctx)


def _build(nc, a, out, ctx):
    def sb(name, shape, dt=F32):
        return ctx.enter_context(nc.sbuf_tensor(name, shape, dt))

    def sem(name):
        return ctx.enter_context(nc.semaphore(name))

    gcn_table = [nc.dram_tensor(f"gcn_table{l}", (ROWS, D), F32).ap() for l in range(3)]
    rel_table = nc.dram_tensor("rel_table", (N_NODES * RELS, D), F32).ap()

    x_res = sb("x_res", [P, TILES, D])
    xn = sb("xn", [P, TILES, D])
    xt = sb("xt", [P, HALVES, ROWS + P])
    union = sb("union", [P, 10240])
    ring = union[:, 0:8192].rearrange("p (s j f) -> p s j f", s=RING, j=GE)
    onehot = union[:, 8192:10240].rearrange("p (s j w) -> p s j w", s=2, j=GE)
    rows = sb("rows", [P, CHUNK, D])
    xs = sb("xs", [P, HALVES, CROWS])
    stage = union[:, 0:8192].rearrange("p (s r f) -> p s r f", s=2, r=RELS)
    hh = union[:, 0:5120].rearrange("p (s m n) -> p s m n", s=2, m=FT)
    lo1h = union[:, 0:1024].bitcast(BF16).rearrange("p (s w j) -> p s w j", s=2, j=GE)
    hi1h = union[:, 1024:1024 + GE * TILES].bitcast(BF16).rearrange("p (s w j) -> p s w j", s=2, j=GE)
    values = rows[:, 0:2, :].bitcast(BF16).rearrange("p u (w j) -> p (u w) j", j=GE)
    gspread = union[:, 1536:1792].rearrange("p (k q) -> p k q", k=2)
    edge_i = union[:, 2048:5120].bitcast(I32).rearrange("p (k e) -> p k e", k=3)
    edge_f = union[:, 6144:10240].rearrange("p (k e) -> p k e", k=4)

    gw = sb("gw", [P, 3, HALVES, D])
    gb = sb("gb", [P, 3, D])
    weights = sb("weights", [P, 3, E0 * HALVES * D])
    wa, wb, wc = (weights[:, i, :].rearrange("p (e k f) -> p e k f", e=E0, k=HALVES) for i in range(3))
    rw = weights[:, 0:2, :].rearrange("p k (r f) -> p k r f", r=RELS)
    rg = sb("rg", [P, HALVES, RELS])
    s1 = weights[:, 2, 0:2048].rearrange("p (s k f) -> p s k f", s=TOP_K, k=HALVES)
    s2 = weights[:, 2, 2048:4096].rearrange("p (s k f) -> p s k f", s=TOP_K, k=FT)

    ident = sb("ident", [P, P])
    ones = sb("ones", [P, P])
    iota_w = sb("iota_w", [P, P])
    digits = sb("digits", [P, 2, GROUPS, GE], BF16)
    zero_bf = sb("zero_bf", [P, P], BF16)
    row_mask = sb("row_mask", [P, TILES])
    zero_f = sb("zero_f", [P, 2])
    dstc = sb("dstc", [P, GROUPS, GE])
    wgtc = sb("wgtc", [P, GROUPS, GE])
    scratch = xn[:, :, :].rearrange("p t f -> p (t f)")
    tmpci = scratch[:, 1664:1664 + 3 * GROUPS * GE].bitcast(I32).rearrange("p (k g j) -> p k g j", k=3, j=GE)
    h1 = scratch[:, 0:1280].rearrange("p (m n) -> p m n", m=2)
    h2 = scratch[:, 1280:2560].rearrange("p (m n) -> p m n", m=2)
    bob = scratch[:, 2560:4608].rearrange("p (e f) -> p e f", e=E0)
    tmpe = scratch[:, 4096:6144].rearrange("p (k e) -> p k e", k=2)
    rel_dst = sb("rel_dst", [P, GROUPS, GE])
    idx_src = sb("idx_src", [P, GROUPS + RING, GE], I32)
    idx_rel = sb("idx_rel", [P, GROUPS + RING, GE], I32)
    src_f = sb("src_f", [P, GROUPS, GE])
    idx_ring = sb("idx_ring", [P, AGGS, RING, GE], I32)
    base0 = sb("base0", [P, GROUPS])
    base_f = sb("base_f", [P, GROUPS])
    base_i = sb("base_i", [P, GROUPS], I32)
    gstat = sb("gstat", [P, 4])
    span_i = sb("span_i", [P, GROUPS], I32)
    npass_f = sb("npass_f", [P, 3])
    npass = sb("npass", [P, 2], I32)
    dinv = sb("dinv", [P, TILES])
    xr = sb("xr", [P, 2, HALVES, P])
    stats0 = sb("stats0", [P, TILES, 6])
    mean0, rstd0, half0 = (sb(n, [P, TILES]) for n in ("mean0", "rstd0", "half0"))
    stats = sb("stats", [P, CHUNK, 6])
    mean, rstd, half = (sb(n, [P, CHUNK]) for n in ("mean", "rstd", "half"))
    wr0 = sb("wr0", [P, HALVES, E0])
    br0 = sb("br0", [1, E0])
    rout = sb("rout", [P, CHUNK, E0])
    rtmp = sb("rtmp", [P, CHUNK])
    bnp = sb("bnp", [80, 2, P])
    bnc = sb("bnc", [P, 2, 5, 16])
    bn_s = sb("bn_s", [P, 2, 16])
    bn_t = sb("bn_t", [P, 2, 16])
    gates = sb("gates", [P, TILES, RELS])
    wr1 = sb("wr1", [P, HALVES, E0])
    small = sb("small", [1, 12, E0])
    iota8 = sb("iota8", [1, E0])
    sel_i = sb("sel_i", [1, 4], I32)
    mean_t = sb("mean_t", [P, HALVES])
    b1s = union[0:FT, 5120:5376].rearrange("p (s f) -> p s f", s=TOP_K)
    b1c = sb("b1c", [P, TOP_K, FT])
    b2s = union[0:1, 5376:5888].rearrange("p (s f) -> p s f", s=TOP_K)
    wsel = sb("wsel", [P, TOP_K])
    b2m = union[0:1, 5888:6400].rearrange("p (s f) -> p s f", s=2)
    b2_all = gb[:, 0, :]
    gam = sb("gam", [P, D])
    bet = sb("bet", [P, D])

    ps = ctx.enter_context(nc.psum_tensor("ps", [P, 8, 512], F32))

    ld_dst, ld_edges, ld_x, ld_gcn, ld_mix, ld_rel, ld_mix2 = (
        sem("ld_" + n) for n in ("dst", "edges", "x", "gcn", "mix", "rel", "mix2"))
    consts = sem("consts")
    once_steps, mix_steps, back_steps, out_steps = (
        sem(n) for n in ("once_steps", "mix_steps", "back_steps", "out_steps"))
    dst_f, edges_f = sem("dst_f"), sem("edges_f")
    edges_tr = sem("edges_tr")
    gstat_ready = sem("gstat_ready")
    cols_copied, idx_made, rel_idx = sem("cols_copied"), sem("idx_made"), sem("rel_idx")
    gspread_mm = sem("gspread_mm")
    plan_ready = sem("plan_ready")
    deg_in, deg_sd, gcn_added, bo_added = sem("deg_in"), sem("deg_sd"), sem("gcn_added"), sem("bo_added")
    hist_1h, hist_mm, hist_done = sem("hist_1h"), sem("hist_mm"), sem("hist_done")
    ln_var = [sem(f"ln_var{i}") for i in range(5)]
    ln_sd = [sem(f"ln_sd{i}") for i in range(5)]
    ln_row = [sem(f"ln_row{i}") for i in range(4)]
    tr_mm = [sem(f"tr_mm{i}") for i in range(6)]
    tr_ev = [sem(f"tr_ev{i}") for i in range(6)]
    table_out = [sem(f"table_out{i}") for i in range(3)]
    idx_copied = [sem(f"idx_copied{i}") for i in range(AGGS)]
    gathered = [[sem(f"gathered{i}_{s}") for s in range(RING)] for i in range(AGGS)]
    onehot_ready = [sem(f"onehot_ready{i}") for i in range(AGGS)]
    group_mm = [sem(f"group_mm{i}") for i in range(AGGS)]
    agg_added = [sem(f"agg_added{i}") for i in range(AGGS)]
    pass_base = [sem(f"pass_base{i}") for i in range(AGGS)]
    groups_issued = sem("groups_issued")
    xs_copied, agg_done = sem("xs_copied"), sem("agg_done")
    y_mm, y_ev = sem("y_mm"), sem("y_ev")
    gelu_done, row_ready, rows_free = sem("gelu_done"), sem("row_ready"), sem("rows_free")
    rout_mm, rout_max, rout_exp, rout_ready = (sem("rout_" + n) for n in ("mm", "max", "exp", "ready"))
    ld_bo = sem("ld_bo")
    bn_tr, bn_var, bn_sd, bn_ready = (sem("bn_" + n) for n in ("tr", "var", "sd", "ready"))
    l1_mm, l1_ev, l2_mm, l2_ev, yo_mm, yo_ev = (sem(n) for n in ("l1_mm", "l1_ev", "l2_mm", "l2_ev", "yo_mm", "yo_ev"))
    xr_copied = sem("xr_copied")
    gate_mm, gate_ready = sem("gate_mm"), sem("gate_ready")
    rel_mm, rel_ev_a, rel_ev_v = sem("rel_mm"), sem("rel_ev_a"), sem("rel_ev_v")
    rel_out = [sem("rel_out0"), sem("rel_out1")]
    back_mm, back_ev = sem("back_mm"), sem("back_ev")
    rows_copied, beta_added, fin_scaled = sem("rows_copied"), sem("beta_added"), sem("fin_scaled")
    mean_mm, mean_ev, log_mm, exp_in, exp_out = (sem(n) for n in ("mean_mm", "mean_ev", "log_mm", "exp_in", "exp_out"))
    sel_ready, sel_ld1, sel_ld2, sel_tr, sel_ev, wsel_in, wsel_mm = (
        sem(n) for n in ("sel_ready", "sel_ld1", "sel_ld2", "sel_tr", "sel_ev", "wsel_in", "wsel_mm"))
    b2_ready, b2_mm, b2_copied, b2_added, w2_scaled = (
        sem(n) for n in ("b2_ready", "b2_mm", "b2_copied", "b2_added", "w2_scaled"))
    hid_mm, hid_ev, fo_mm, fo_ev, fin_ready, out_done = (
        sem(n) for n in ("hid_mm", "hid_ev", "fo_mm", "fo_ev", "fin_ready", "out_done"))

    block = ctx.enter_context(nc.Block())

    @block.sync
    def _(sp):
        sp.wait_ge(consts, 4)
        for k, name in enumerate(("dst", "src", "edge_type_16")):
            loaded = ld_edges if k else ld_dst
            sp.dma_start(edge_i[0:GROUPS - 1, k, :],
                         a[name][0:(GROUPS - 1) * GROUP].rearrange("(g e) -> g e", g=GROUPS - 1)).then_inc(loaded, 16)
            sp.dma_start(edge_i[GROUPS - 1:GROUPS, k, 0:GTAIL],
                         a[name][(GROUPS - 1) * GROUP:N_EDGES].rearrange("(g e) -> g e", g=1)).then_inc(loaded, 16)
        sp.dma_start(edge_f[0:GROUPS - 1, 3, :], a["edge_weight1"][0:(GROUPS - 1) * GROUP, :]
                     .rearrange("(g e) o -> g (e o)", g=GROUPS - 1)).then_inc(ld_edges, 16)
        sp.dma_start(edge_f[GROUPS - 1:GROUPS, 3, 0:GTAIL], a["edge_weight1"][(GROUPS - 1) * GROUP:N_EDGES, :]
                     .rearrange("(g e) o -> g (e o)", g=1)).then_inc(ld_edges, 16)
        sp.dma_start(x_res[:, 0:TILES - 1, :],
                     a["x"][0:(TILES - 1) * P, :].rearrange("(t p) f -> p t f", p=P)).then_inc(ld_x, 16)
        sp.dma_start(x_res[0:TAIL, TILES - 1, :], a["x"][(TILES - 1) * P:N_NODES, :]).then_inc(ld_x, 16)
        for l in range(3):
            sp.dma_start(gw[:, l, :, :], a[f"L0_gnn_W{l + 1}"].rearrange("(k p) f -> p k f", p=P)).then_inc(ld_gcn, 16)
            sp.dma_start(gb[:, l, :], a[f"L0_gnn_b{l + 1}"].partition_broadcast(P)).then_inc(ld_gcn, 16)
        for w, name in ((wa, "L0_ffn_W1"), (wb, "L0_ffn_W2"), (wc, "L0_ffn_Wo")):
            for e in range(E0):
                sp.dma_start(w[:, e, :, :], a[name][e].rearrange("(k p) f -> p k f", p=P)).then_inc(ld_mix, 16)
        for q, names in enumerate((("b1", "g1", "be1", "m1", "v1"), ("b2", "g2", "be2", "m2", "v2"))):
            for n, name in enumerate(names):
                sp.dma_start(bnp[n * 16:(n + 1) * 16, q, :],
                             a["L0_ffn_" + name].rearrange("e (h p) -> (e h) p", p=P)).then_inc(ld_mix, 16)
        sp.dma_start(wr0[:, :, :], a["L0_ffn_Wr"].rearrange("(k p) e -> p k e", p=P)).then_inc(ld_mix, 16)
        sp.dma_start(br0[:, :], a["L0_ffn_br"].rearrange("(o e) -> o e", o=1)).then_inc(ld_mix, 16)
        for k in range(HALVES):
            sp.dma_start(rg[:, k, :], a["L1_gnn_gate_weight"][:, k * P:(k + 1) * P, :].rearrange("r p o -> p (r o)"),
                         allow_slow_non_contiguous=True).then_inc(ld_rel, 16)
        sp.dma_start(wr1[:, :, :], a["L1_ffn_Wr"].rearrange("(k p) e -> p k e", p=P)).then_inc(ld_mix2, 16)
        sp.dma_start(small[:, 0, :], a["L1_ffn_br"].rearrange("(o e) -> o e", o=1)).then_inc(ld_mix2, 16)
        sp.dma_start(gam[:, :], a["L1_ffn_gamma"].partition_broadcast(P)).then_inc(ld_mix2, 16)
        sp.dma_start(bet[:, :], a["L1_ffn_beta"].partition_broadcast(P)).then_inc(ld_mix2, 16)

        def chunk_out(table, c, src, done):
            sp.dma_start(table[bass.ds(c * CROWS, CROWS), :].rearrange("(u p) f -> p u f", p=P), src).then_inc(done, 16)

        for c in range(CHUNKS):
            sp.wait_ge(ln_row[0], (c + 1) * CHUNK)
            chunk_out(gcn_table[0], c, xn[:, c * CHUNK:(c + 1) * CHUNK, :], table_out[0])
        sp.wait_ge(table_out[0], 16 * CHUNKS)
        sp.wait_ge(tr_mm[0], TILES)
        sp.dma_start(bob[:, :, :], a["L0_ffn_bo"].partition_broadcast(P)).then_inc(ld_bo, 16)
        sp.sem_inc(rows_free, 1)
        for l in range(2):
            with sp.Fori(0, CHUNKS) as c:
                sp.wait_ge(row_ready, c * CHUNK + (l * TILES + CHUNK))
                chunk_out(gcn_table[l + 1], c, rows[:, :, :], table_out[l + 1])
                sp.wait_ge(table_out[l + 1], c * 16 + 16)
                sp.sem_inc(rows_free, 1)
        last = (CHUNKS - 1) * E0
        for e in range(E0):
            for i, used in enumerate((l1_mm, l2_mm)):
                sp.wait_ge(used, (last + e + 1) * 2)
                sp.dma_start(rw[:, i, 2 * e:2 * e + 2, :], a["L1_gnn_weight"][2 * e:2 * e + 2, i * P:(i + 1) * P, :]
                             .rearrange("r p f -> p r f")).then_inc(ld_rel, 16)
        def rel_rows(k, s, real=P):
            sp.wait_ge(rel_ev_a, k * 4 + 8)
            sp.wait_ge(rel_ev_v, k * 4 + 8)
            sp.dma_start(rel_table[bass.ds(k * P * RELS, real * RELS), :].rearrange("(p r) f -> p r f", r=RELS),
                         stage[0:real, s, :, :]).then_inc(rel_out[s], 16)
        with sp.Fori(0, TILES // 2) as k2:
            rel_rows(k2 * 2, 0)
            rel_rows(k2 * 2 + 1, 1)
        rel_rows(TILES - 1, 0, TAIL)

        sp.wait_ge(sel_ready, 1)
        chosen = [sp.value_load(sel_i[0:1, s:s + 1], min_val=0, max_val=E0 - 1) for s in range(TOP_K)]
        for s, e in enumerate(chosen):
            sp.dma_start(s1[:, s, :, :], a["L1_ffn_W1"][bass.ds(e, 1), :, :]
                         .rearrange("o (k p) f -> p (o k) f", p=P)).then_inc(sel_ld1, 16)
            sp.dma_start(b1s[:, s, :], a["L1_ffn_b1"][bass.ds(e, 1), :]
                         .rearrange("o (k p) -> (o k) p", p=P)).then_inc(sel_ld1, 16)
        for s, e in enumerate(chosen):
            sp.dma_start(s2[:, s, :, :], a["L1_ffn_W2"][bass.ds(e, 1), :, :]
                         .rearrange("o (k p) f -> p (o k) f", p=P)).then_inc(sel_ld2, 16)
            sp.dma_start(b2s[:, s, :], a["L1_ffn_b2"][bass.ds(e, 1), :]).then_inc(sel_ld2, 16)
        for c in range(CHUNKS):
            first, full = c * CHUNK, CHUNK if c < CHUNKS - 1 else CHUNK - 1
            sp.wait_ge(fin_ready, first + full)
            sp.dma_start(out[first * P:(first + full) * P, :].rearrange("(u p) f -> p u f", p=P),
                         x_res[:, first:first + full, :]).then_inc(out_done, 16)
        sp.wait_ge(fin_ready, TILES)
        sp.dma_start(out[(TILES - 1) * P:N_NODES, :], x_res[0:TAIL, TILES - 1, :]).then_inc(out_done, 16)
        sp.wait_ge(out_done, 16 * (CHUNKS + 1))

    @block.gpsimd
    def _(g):
        g.memset(edge_i[32:64, 0, GTAIL:], -1).then_inc(consts, 1)
        g.memset(edge_i[32:64, 1:3, GTAIL:], 0).then_inc(consts, 1)
        g.memset(edge_f[32:64, 3, GTAIL:], 0.0).then_inc(consts, 1)
        g.wait_ge(consts, 3)
        g.memset(x_res[:, TILES - 1, :], 0.0).then_inc(consts, 1)
        g.memset(xt[:, :, ROWS:], 0.0).then_inc(consts, 1)
        g.iota(iota_w[:, :], [[1, P]], base=0, channel_multiplier=0,
               allow_small_or_imprecise_dtypes=True).then_inc(consts, 1)
        g.iota(iota8[:, :], [[1, E0]], base=0, channel_multiplier=0,
               allow_small_or_imprecise_dtypes=True).then_inc(consts, 1)
        g.memset(ones[:, :], 1.0).then_inc(consts, 1)
        g.memset(zero_bf[:, :], 0.0).then_inc(consts, 1)
        g.wait_ge(consts, 8)
        g.affine_select(out=ident[:, :], in_=ones[:, :], compare_op=ALU.is_equal, fill=0.0,
                        base=0, pattern=[[-1, P]], channel_multiplier=1).then_inc(consts, 1)
        g.affine_select(out=row_mask[:, :], in_=ones[:, 0:TILES], compare_op=ALU.is_ge, fill=0.0,
                        base=N_NODES - 1, pattern=[[-P, TILES]], channel_multiplier=-1).then_inc(consts, 1)
        g.memset(zero_f[:, :], 0.0).then_inc(consts, 1)
        g.wait_ge(cols_copied, 2)
        g.tensor_copy(idx_src[:, 0:GROUPS, :], src_f[:, :, :]).then_inc(idx_made, 1)
        g.wait_ge(idx_made, 1)
        g.tensor_copy(idx_src[:, GROUPS:, :], idx_src[:, 0:RING, :]).then_inc(idx_made, 1)
        for l in range(3):
            g.tensor_copy(idx_ring[:, l, :, :], idx_src[:, 0:RING, :]).then_inc(idx_copied[l], RING)

        for l in range(AGGS):
            table = gcn_table[l] if l < 3 else rel_table
            if l == 0:
                g.wait_ge(plan_ready, 1)
                passes = g.value_load(npass[0:1, 0:1], min_val=1, max_val=26)
            if l == 3:
                g.wait_ge(tr_ev[4], CHUNK + TILES)
                for s in range(2):
                    g.tensor_copy(xr[:, s, :, :], xt[:, :, s * P:(s + 1) * P]).then_inc(xr_copied, 1)
                with g.Fori(1, TILES // 2) as k2:
                    for s in range(2):
                        k = k2 * 2 + s
                        g.wait_ge(rel_mm, (k - 1) * 8)
                        g.tensor_copy(xr[:, s, :, :], xt[:, :, bass.ds(k * P, P)]).then_inc(xr_copied, 1)
                g.wait_ge(rel_mm, (TILES - 2) * 8)
                g.tensor_copy(xr[:, 0, :, :], xt[:, :, ROWS - P:ROWS]).then_inc(xr_copied, 1)
                g.wait_ge(rel_out[0], 16 * (TILES // 2 + 1))
                g.wait_ge(rel_out[1], 16 * (TILES // 2))
            else:
                g.wait_ge(table_out[l], 16 * CHUNKS)
            if l > 0:
                g.wait_ge(agg_done, l)
            with g.Fori(0, passes) as m:
                with g.Fori(0, GROUPS // RING) as i:
                    for s in range(RING):
                        g.wait_ge(idx_copied[l], m * GROUPS + i * RING + s + 1)
                        g.sem_inc(groups_issued, 1)
                        for j in range(GE):
                            g.indirect_dma_start(
                                out=ring[:, s, j, :], out_offset=None, in_=table[:, :],
                                in_offset=bass.IndirectOffsetOnAxis(ap=idx_ring[:, l, s, j:j + 1], axis=0),
                            ).then_inc(gathered[l][s], 16)
        g.wait_ge(ld_mix2, 64)
        with g.Fori(0, CHUNKS) as c:
            for u in range(CHUNK):
                k = c * CHUNK + u
                g.wait_ge(ln_row[3], k + 1)
                g.tensor_tensor(x_res[:, k, :], x_res[:, k, :], bet[:, :], ALU.add).then_inc(beta_added, 1)
        g.wait_ge(b2_copied, 1)
        with g.Fori(0, CHUNKS) as c:
            for u in range(CHUNK):
                k = c * CHUNK + u
                g.wait_ge(rows_copied, k + 1)
                g.tensor_tensor(xn[:, k, :], xn[:, k, :], b2_all[:, :], ALU.add).then_inc(b2_added, 1)

    @block.tensor
    def _(pe):
        pe.wait_ge(consts, 12)
        for l in range(AGGS):
            pe.sem_inc(group_mm[l], 2)
        for k in range(4):
            if k == 0:
                pe.wait_ge(dst_f, 1)
            elif k < 3:
                pe.wait_ge(edges_f, k)
            if k == 3:
                pe.wait_ge(ld_edges, 16 * 6)
            for j in range(GE):
                mm = pe.transpose(ps[:, k, j * GROUPS:(j + 1) * GROUPS],
                                  edge_f[0:GROUPS, k, j * P:(j + 1) * P], ident[0:GROUPS, 0:GROUPS])
            mm.then_inc(edges_tr, 1)
        pe.wait_ge(gstat_ready, 1)
        pe.matmul(ps[:, 4, 0:GROUPS], gspread[0:GROUPS, 0, :], ident[0:GROUPS, 0:GROUPS], start=True, stop=True)
        pe.matmul(ps[:, 5, 0:GROUPS], gspread[0:GROUPS, 1, :], ident[0:GROUPS, 0:GROUPS],
                  start=True, stop=True).then_inc(gspread_mm, 1)
        deg = ps[:, 6, 0:TILES]
        pe.sem_inc(hist_mm, 2)
        pe.matmul(deg, zero_bf[:, :], zero_bf[:, 0:TILES], start=True, stop=False, skip_group_check=True)
        with pe.Fori(0, GROUPS // 2) as i:
            for s in range(2):
                pe.wait_ge(hist_1h, i * 2 + s + 1)
                for j in range(GE):
                    mm = pe.matmul(deg, lo1h[:, s, :, j], hi1h[:, s, :, j], start=False, stop=False,
                                   skip_group_check=True)
                mm.then_inc(hist_mm, 1)
        pe.matmul(deg, zero_bf[:, :], zero_bf[:, 0:TILES], start=False, stop=True,
                  skip_group_check=True).then_inc(hist_done, 1)

        def transposes(tile, ready, which, c, first=0):
            for u in range(CHUNK):
                k = c * CHUNK + u
                pe.wait_ge(ready, k + (first + 1))
                pe.wait_ge(tr_ev[which], k + 1)
                for h in range(HALVES):
                    mm = pe.transpose(ps[:, u, h * P:(h + 1) * P], tile(u)[:, h * P:(h + 1) * P], ident[:, :])
                mm.then_inc(tr_mm[which], 1)

        def chunk_row(u):
            return rows[:, u, :]

        pe.wait_ge(plan_ready, 1)
        pe.wait_ge(rel_idx, 1)
        pe.wait_ge(cols_copied, 2)
        for c in range(CHUNKS):
            transposes(lambda u: xn[:, c * CHUNK + u, :], ln_row[0], 0, c)
        pe.wait_ge(ld_mix, 16 * (3 * E0 + 12))
        for q in range(2):
            mm = pe.transpose(ps[:, 5, q * 80:(q + 1) * 80], bnp[:, q, :], ident[0:80, 0:80])
        mm.then_inc(bn_tr, 1)
        passes = pe.value_load(npass[0:1, 0:1], min_val=1, max_val=26)
        ordered = pe.value_load(npass[0:1, 1:2], min_val=0, max_val=1)
        pe.wait_ge(ld_gcn, 16 * 6)
        pe.wait_ge(bn_ready, 1)

        def group(l, t, turn, s):
            pe.wait_ge(gathered[l][s], (turn + 1) * (16 * GE))
            pe.wait_ge(onehot_ready[l], t + 1)
            pe.wait_ge(agg_added[l], t + 2)
            for h in range(HALVES):
                for j in range(GE):
                    mm = pe.matmul(ps[:, 7, h * P:(h + 1) * P], ring[:, s, j, h * P:(h + 1) * P],
                                   onehot[:, s % 2, j, :], start=(j == 0), stop=(j == GE - 1))
            mm.then_inc(group_mm[l], 1)

        def groups(l, t0, n):
            with pe.Fori(0, n // RING) as i:
                for s in range(RING):
                    group(l, t0 + i * RING + s, t0 // RING + i, s)

        def y_products(l, c):
            pe.wait_ge(xs_copied, l * CHUNKS + 1 + c)
            pe.wait_ge(tr_ev[l + 1 if l < 2 else 4], c * CHUNK + CHUNK)
            for u in range(CHUNK):
                if u % 2 == 0:
                    pe.wait_ge(y_ev, c * CHUNK + (l * TILES + min(u + 2, CHUNK)))
                for h in range(HALVES):
                    mm = pe.matmul(ps[:, 4 + u // 2, (u % 2) * D:(u % 2 + 1) * D], xs[:, h, u * P:(u + 1) * P],
                                   gw[:, l, h, :], start=(h == 0), stop=(h == 1))
                if u % 2 == 1 or u == CHUNK - 1:
                    mm.then_inc(y_mm, 1)

        def gcn_chunk(l, c, _):
            y_products(l, c)
            transposes(chunk_row, row_ready, l + 1, c, l * TILES)

        def experts_out(t, e):
            pe.wait_ge(l2_ev, t * 2 + 4)
            for u in range(CHUNK):
                if u % 2 == 0:
                    pe.wait_ge(yo_ev, t * CHUNK + min(u + 2, CHUNK))
                for h in range(HALVES):
                    mm = pe.matmul(ps[:, 4 + u // 2, (u % 2) * D:(u % 2 + 1) * D], h2[:, h, u * P:(u + 1) * P],
                                   wc[:, e, h, :], start=(h == 0), stop=(h == 1))
                if u % 2 == 1 or u == CHUNK - 1:
                    mm.then_inc(yo_mm, 1)

        def mix_chunk(l, c, t0):
            before, steps_with, after = mix_plan(t0[2])
            if before:
                group(l, t0[0], t0[1], 0)
            y_products(l, c)
            for n in range(1, before):
                group(l, t0[0] + n, t0[1], n % RING)
            transposes(chunk_row, ln_row[1], 3, c)
            pe.wait_ge(tr_ev[3], c * CHUNK + 2 * CHUNK)
            for u in range(CHUNK):
                at = ps[:, 5, u * E0:(u + 1) * E0]
                pe.matmul(at, ones[0:1, :], br0[:, :], start=True, stop=False)
                for h in range(HALVES):
                    mm = pe.matmul(at, xs[:, h, u * P:(u + 1) * P], wr0[:, h, :], start=False, stop=(h == 1))
            mm.then_inc(rout_mm, 1)
            for e in range(E0):
                t = c * E0 + e
                for m in range(2):
                    pe.wait_ge(l2_ev, t * 2 + m + 1)
                    for n in range(2):
                        for h in range(HALVES):
                            mm = pe.matmul(ps[:, 2 * m + n, 0:streamed(c, n)], wa[:, e, h, m * P:(m + 1) * P],
                                           xs[:, h, n * NH:n * NH + streamed(c, n)], start=(h == 0), stop=(h == 1))
                    mm.then_inc(l1_mm, 1)
                if e == 1:
                    pe.wait_ge(rout_max, c + 1)
                if e > 0:
                    experts_out(t - 1, e - 1)
                if e in steps_with and e < E0 - 1:
                    n = before + steps_with.index(e)
                    group(l, t0[0] + n, t0[1] + n // RING, n % RING)
                pe.wait_ge(l1_ev, t * 2 + 2)
                for m in range(2):
                    for n in range(2):
                        for h in range(HALVES):
                            mm = pe.matmul(ps[:, 2 * m + n, 0:streamed(c, n)], wb[:, e, h, m * P:(m + 1) * P],
                                           h1[:, h, n * NH:n * NH + streamed(c, n)], start=(h == 0), stop=(h == 1))
                    mm.then_inc(l2_mm, 1)
            n0 = before + len(steps_with)
            if E0 - 1 in steps_with:
                group(l, t0[0] + n0 - 1, t0[1] + (n0 - 1) // RING, (n0 - 1) % RING)
            experts_out(c * E0 + (E0 - 1), E0 - 1)
            for n in range(n0, n0 + after):
                group(l, t0[0] + n, t0[1] + n // RING, n % RING)
            transposes(chunk_row, ln_row[2], 4, c)

        def back_chunk(l, c, t0):
            follows = t0[2] > 0
            if follows:
                group(l, t0[0], t0[1], 0)
            pe.wait_ge(xs_copied, l * CHUNKS + 1 + c)
            for u in range(CHUNK):
                pe.wait_ge(tr_ev[5], c * CHUNK + u + 1)
                for h in range(HALVES):
                    mm = pe.transpose(ps[:, u, h * P:(h + 1) * P], xs[:, h, u * P:(u + 1) * P], ident[:, :])
                mm.then_inc(back_mm, 1)
            if follows:
                group(l, t0[0] + 1, t0[1], 1)
                group(l, t0[0] + 2, t0[1], 2)
            transposes(chunk_row, ln_row[3], 5, c)
            for u in range(CHUNK):
                for h in range(HALVES):
                    mm = pe.matmul(ps[:, 5 + h, 0:1], rows[:, u, h * P:(h + 1) * P],
                                   row_mask[:, bass.ds(c * CHUNK + u, 1)], start=False, stop=False,
                                   skip_group_check=True)
            mm.then_inc(mean_mm, 1)
            if follows:
                group(l, t0[0] + 3, t0[1], 3)

        def stage_of(l, chunk):
            with pe.If_eq(pe.to_reg(ordered), 1):
                groups(l, 0, PROLOGUE)
                with pe.Fori(0, 3) as c:
                    t0, turn = c * PROLOGUE + PROLOGUE, (c + 1) * (PROLOGUE // RING)
                    chunk(l, c, (t0, turn, FOLLOW[0]))
                    if chunk is not mix_chunk:
                        done = RING if chunk is back_chunk else 0
                        with pe.Fori(0, (FOLLOW[0] - done) // RING) as i:
                            for s in range(RING):
                                group(l, t0 + done + i * RING + s, turn + done // RING + i, s)
                for c in (3, 4):
                    t0 = PROLOGUE * (c + 1) if c == 3 else GROUPS
                    chunk(l, c, (t0, t0 // RING, FOLLOW[c]))
                    if chunk is gcn_chunk:
                        for s in range(FOLLOW[c]):
                            group(l, t0 + s, t0 // RING, s)
            with pe.Else():
                with pe.Fori(0, passes) as m:
                    with pe.Fori(0, GROUPS // RING) as i:
                        for s in range(RING):
                            group(l, m * GROUPS + i * RING + s, m * (GROUPS // RING) + i, s)
                with pe.Fori(0, CHUNKS) as c:
                    chunk(l, c, (0, 0, 0))

        stage_of(0, gcn_chunk)
        stage_of(1, gcn_chunk)
        stage_of(2, mix_chunk)

        pe.wait_ge(ld_rel, 16 * (2 * E0 + HALVES))
        pe.wait_ge(tr_ev[4], CHUNK + TILES)
        for k in range(TILES):
            for h in range(HALVES):
                mm = pe.matmul(ps[:, 7, k * RELS:(k + 1) * RELS], xt[:, h, k * P:(k + 1) * P], rg[:, h, :],
                               start=(h == 0), stop=(h == 1))
        mm.then_inc(gate_mm, 1)
        pe.wait_ge(gate_ready, 1)

        def rel_products(k, s):
            pe.wait_ge(xr_copied, k + 1)
            for r in range(RELS // 2):
                pe.wait_ge(rel_ev_v if r % 2 else rel_ev_a, k * 4 + r // 2 + 1)
                for h in range(HALVES):
                    mm = pe.matmul(ps[:, (r % 2) * 4 + r // 2, :], xr[:, s, h, :],
                                   rw[:, h, 2 * r:2 * r + 2, :].rearrange("p r f -> p (r f)"),
                                   start=(h == 0), stop=(h == 1))
                mm.then_inc(rel_mm, 1)

        with pe.Fori(0, TILES // 2) as k2:
            for s in range(2):
                rel_products(k2 * 2 + s, s)
        rel_products(TILES - 1, 0)

        pe.wait_ge(rel_ev_v, 4 * TILES + 4)
        for h in range(HALVES):
            pe.matmul(ps[:, 5 + h, 0:1], ident[:, :], zero_f[:, 0:1], start=True, stop=False, skip_group_check=True)
        stage_of(3, back_chunk)
        for h in range(HALVES):
            mm = pe.matmul(ps[:, 5 + h, 0:1], ident[:, :], zero_f[:, 0:1], start=False, stop=True,
                           skip_group_check=True)
        mm.then_inc(mean_mm, 1)

        pe.wait_ge(mean_ev, 1)
        pe.wait_ge(ld_mix2, 64)
        for h in range(HALVES):
            mm = pe.matmul(ps[0:1, 6, 0:E0], mean_t[:, h:h + 1], wr1[:, h, :], start=(h == 0), stop=(h == 1))
        mm.then_inc(log_mm, 1)
        pe.wait_ge(wsel_in, 1)
        pe.matmul(ps[:, 6, 16:16 + TOP_K], ones[0:1, :], small[:, 8, 0:TOP_K],
                  start=True, stop=True).then_inc(wsel_mm, 1)
        pe.wait_ge(sel_ld1, 16 * 2 * TOP_K)
        for s in range(TOP_K):
            mm = pe.transpose(ps[:, 7, s * FT:(s + 1) * FT], b1s[:, s, :], ident[0:FT, 0:FT])
        mm.then_inc(sel_tr, 1)
        pe.wait_ge(tr_ev[5], CHUNK + TILES)
        def experts_chunk(c):
            for s in range(TOP_K):
                for f in range(FT):
                    q = s * FT + f
                    pe.wait_ge(hid_ev, (c * TOP_K * FT) + q + 1)
                    for n in range(2):
                        for h in range(HALVES):
                            mm = pe.matmul(ps[:, 2 * (q % 2) + n, 0:streamed(c, n)], s1[:, s, h, f * P:(f + 1) * P],
                                           xt[:, h, bass.ds(c * CROWS + n * NH, streamed(c, n))],
                                           start=(h == 0), stop=(h == 1))
                    mm.then_inc(hid_mm, 1)
            pe.wait_ge(w2_scaled, TOP_K)
            if isinstance(c, int) and c == 0:
                pe.wait_ge(b2_ready, 1)
                pe.matmul(ps[:, 7, 0:D], ones[0:1, :], b2m[:, 1, :], start=True, stop=True).then_inc(b2_mm, 1)
            pe.wait_ge(hid_ev, (c + 1) * TOP_K * FT + 2)
            for u in range(CHUNK):
                if u % 2 == 0:
                    pe.wait_ge(fo_ev, c * CHUNK + min(u + 2, CHUNK))
                acc = ps[:, 4 + u // 2, (u % 2) * D:(u % 2 + 1) * D]
                for s in range(TOP_K):
                    for f in range(FT):
                        mm = pe.matmul(acc, hh[:, s, f, u * P:(u + 1) * P], s2[:, s, f, :],
                                       start=(s == 0 and f == 0), stop=(s == TOP_K - 1 and f == FT - 1))
                if u % 2 == 1 or u == CHUNK - 1:
                    mm.then_inc(fo_mm, 1)

        experts_chunk(0)
        with pe.Fori(1, CHUNKS - 1) as c:
            experts_chunk(c)
        experts_chunk(CHUNKS - 1)

    @block.scalar
    def _(act):
        for i in range(6):
            act.sem_inc(tr_ev[i], CHUNK)
        act.sem_inc(l2_ev, 2)
        act.sem_inc(hid_ev, 2)
        act.sem_inc(rel_ev_a, 4)

        def evacuate(which, c, dst):
            for u in range(CHUNK):
                k = c * CHUNK + u
                act.wait_ge(tr_mm[which], k + 1)
                act.activation(dst(k, u), ps[:, u, 0:D].rearrange("p (h n) -> p h n", h=HALVES),
                               ACT.Copy).then_inc(tr_ev[which], 1)

        def into_xt(k, u):
            return xt[:, :, bass.ds(k * P, P)]

        def into_xs(k, u):
            return xs[:, :, u * P:(u + 1) * P]

        def ln_sqrt(i, c):
            act.wait_ge(ln_var[i], c + 1)
            act.activation(rstd[:, :], rstd[:, :], ACT.Sqrt).then_inc(ln_sd[i], 1)

        act.wait_ge(ld_edges, 16 * 6)
        for k in (1, 2):
            act.activation(edge_f[0:GROUPS, k, :], edge_i[0:GROUPS, k, :], ACT.Copy).then_inc(edges_f, 1)
        act.wait_ge(edges_tr, 4)
        for k, dst in ((1, src_f), (3, wgtc)):
            act.activation(dst[:, :, :], ps[:, k, 0:GROUPS * GE].rearrange("p (j g) -> p g j", j=GE),
                           ACT.Copy).then_inc(cols_copied, 1)
        act.wait_ge(ln_var[0], 1)
        act.activation(rstd0[:, :], rstd0[:, :], ACT.Sqrt).then_inc(ln_sd[0], 1)
        act.wait_ge(deg_in, 1)
        act.activation(dinv[:, :], dinv[:, :], ACT.Sqrt).then_inc(deg_sd, 1)
        with act.Fori(0, CHUNKS) as c:
            evacuate(0, c, into_xt)
        act.wait_ge(bn_var, 1)
        act.activation(bn_s[:, :, :], bn_s[:, :, :], ACT.Sqrt).then_inc(bn_sd, 1)
        for l in range(2):
            with act.Fori(0, CHUNKS) as c:
                for u in range(CHUNK):
                    k = c * CHUNK + u
                    act.wait_ge(y_ev, k + (l * TILES + CHUNK + 1))
                    act.activation(rows[:, u, :], rows[:, u, :], ACT.Gelu_apprx_tanh).then_inc(gelu_done, 1)
                evacuate(l + 1, c, into_xt)
        with act.Fori(0, CHUNKS) as c:
            ln_sqrt(1, c)
            evacuate(3, c, into_xs)
            act.wait_ge(rout_max, c + 1)
            act.activation(rout[:, :, :], rout[:, :, :], ACT.Exp).then_inc(rout_exp, 1)
            for e in range(E0):
                t = c * E0 + e
                for layer, (mm, ev, h) in enumerate(((l1_mm, l1_ev, h1), (l2_mm, l2_ev, h2))):
                    for m in range(2):
                        act.wait_ge(mm, t * 2 + m + 1)
                        col = 2 * e + m
                        act.activation(h[:, m, :].rearrange("p (n w) -> p n w", n=2), ps[:, 2 * m:2 * m + 2, 0:NH],
                                       ACT.Relu, bias=bn_t[:, layer, col:col + 1],
                                       scale=bn_s[:, layer, col:col + 1]).then_inc(ev, 1)
            ln_sqrt(2, c)
            evacuate(4, c, into_xt)
        act.wait_ge(gate_mm, 1)
        act.activation(gates[:, :, :].rearrange("p t r -> p (t r)"), ps[:, 7, 0:TILES * RELS],
                       ACT.Sigmoid).then_inc(gate_ready, 1)
        act.wait_ge(gate_ready, 1)

        def rel_evac(k, s):
            for r in range(0, RELS // 2, 2):
                act.wait_ge(rel_mm, k * 8 + r + 1)
                for q in range(2):
                    rel = 2 * r + q
                    ins = act.activation(stage[:, s, rel, :], ps[:, r // 2, q * D:(q + 1) * D], ACT.Copy,
                                         scale=gates[:, k, rel:rel + 1])
                ins.then_inc(rel_ev_a, 1)

        rel_evac(0, 0)
        rel_evac(1, 1)
        with act.Fori(1, TILES // 2) as k2:
            for s in range(2):
                act.wait_ge(rel_out[s], k2 * 16)
                rel_evac(k2 * 2 + s, s)
        act.wait_ge(rel_out[0], (TILES // 2) * 16)
        rel_evac(TILES - 1, 0)
        with act.Fori(0, CHUNKS) as c:
            ln_sqrt(3, c)
            for u in range(CHUNK):
                k = c * CHUNK + u
                act.wait_ge(ln_row[3], k + 1)
                act.activation(xn[:, k, :], rows[:, u, :], ACT.Copy).then_inc(rows_copied, 1)
            evacuate(5, c, into_xt)
        for i in range(2):
            act.wait_ge(exp_in, i + 1)
            act.activation(small[:, 1, :], small[:, 1, :], ACT.Exp).then_inc(exp_out, 1)
        act.wait_ge(exp_in, 3)
        act.activation(small[:, 9, 0:1], small[:, 9, 0:1], ACT.Exp).then_inc(exp_out, 1)
        act.wait_ge(sel_ev, 1)

        def hidden(c, with_sqrt):
            for s in range(TOP_K):
                for f in range(FT):
                    q = s * FT + f
                    if with_sqrt and q == FT:
                        ln_sqrt(4, c - 1)
                    act.wait_ge(hid_mm, c * (TOP_K * FT) + q + 1)
                    act.activation(hh[:, s, f, :].rearrange("p (n w) -> p n w", n=2),
                                   ps[:, 2 * (q % 2):2 * (q % 2) + 2, 0:NH], ACT.Gelu,
                                   bias=b1c[:, s, f:f + 1]).then_inc(hid_ev, 1)

        hidden(0, False)
        with act.Fori(1, CHUNKS) as c:
            hidden(c, True)
        ln_sqrt(4, CHUNKS - 1)

    @block.vector
    def _(v):
        once = Steps(v, once_steps)
        v.sem_inc(y_ev, CHUNK)
        for i in range(AGGS):
            v.sem_inc(agg_added[i], 2)
        v.sem_inc(yo_ev, CHUNK)
        v.sem_inc(rel_ev_v, 4)
        v.sem_inc(fo_ev, CHUNK)

        v.wait_ge(consts, 12)
        v.wait_ge(ld_dst, 32)
        v.tensor_copy(edge_f[0:GROUPS, 0, :], edge_i[0:GROUPS, 0, :]).then_inc(dst_f, 1)
        v.wait_ge(dst_f, 1)
        dst_rows = edge_f[0:GROUPS, 0, :]
        once.done(v.tensor_scalar(tmpe[0:GROUPS, 0, :], dst_rows, 0.0, BIG, ALU.is_lt, ALU.mult))
        once.done(v.tensor_tensor(tmpe[0:GROUPS, 1, :], tmpe[0:GROUPS, 0, :], dst_rows, ALU.add))
        once.done(v.tensor_reduce(gstat[0:GROUPS, 0:1], tmpe[0:GROUPS, 1, :], AX_X, ALU.min))
        once.done(v.tensor_reduce(gstat[0:GROUPS, 1:2], dst_rows, AX_X, ALU.max))
        once.done(v.tensor_tensor(gstat[0:GROUPS, 2:3], gstat[0:GROUPS, 1:2], gstat[0:GROUPS, 0:1], ALU.subtract))
        v.tensor_scalar(gspread[0:GROUPS, 0, :], ones[0:GROUPS, :], gstat[0:GROUPS, 0:1], None, ALU.mult)
        v.tensor_scalar(gspread[0:GROUPS, 1, :], ones[0:GROUPS, :], gstat[0:GROUPS, 2:3], None,
                        ALU.mult).then_inc(gstat_ready, 1)

        def column(k):
            return ps[:, k, 0:GROUPS * GE].rearrange("p (j g) -> p g j", j=GE)

        v.wait_ge(edges_tr, 1)
        once.done(v.tensor_copy(dstc[:, :, :], column(0)))
        once.done(v.tensor_copy(tmpci[:, 2, :, :], dstc[:, :, :]))
        v.tensor_scalar(tmpci[:, 0, :, :], tmpci[:, 2, :, :], P - 1, None, ALU.bitwise_and)
        once.done(v.tensor_scalar(tmpci[:, 1, :, :], tmpci[:, 2, :, :], 7, None, ALU.arith_shift_right))
        v.tensor_copy(values[:, :, :], iota_w[:, :].unsqueeze(2).to_broadcast([P, P, GE]))
        once.done(v.tensor_copy(digits[:, :, :, :], tmpci[:, 0:2, :, :]))

        with v.Fori(0, GROUPS // 2) as i:
            for s in range(2):
                n = i * 2 + s
                v.wait_ge(hist_mm, n + 1)
                v.tensor_tensor(lo1h[:, s, :, :], digits[:, 0, n, :].unsqueeze(1).to_broadcast([P, P, GE]),
                                values[:, :, :], ALU.is_equal)
                v.tensor_tensor(hi1h[:, s, :, :], digits[:, 1, n, :].unsqueeze(1).to_broadcast([P, TILES, GE]),
                                values[:, 0:TILES, :], ALU.is_equal).then_inc(hist_1h, 1)

        def row_moments(steps, src, c):
            v.memset(half[:, :], 0.0)
            for u in range(CHUNK):
                ins = v.bn_stats(stats[:, u, :], src[:, c * CHUNK + u, :])
            steps.done(ins)

        def row_variance(steps, i, st=stats[:, :, :], mn=mean[:, :], var=rstd[:, :], hf=half[:, :]):
            v.tensor_tensor(mn, st[:, :, 1], st[:, :, 4], ALU.add)
            v.tensor_tensor(var, st[:, :, 2], st[:, :, 5], ALU.add)
            steps.done(v.tensor_tensor(hf, st[:, :, 1], st[:, :, 4], ALU.subtract))
            v.tensor_scalar(mn, mn, 0.5, None, ALU.mult)
            v.tensor_scalar(var, var, 1.0 / D, LN_EPS, ALU.mult, ALU.add)
            steps.done(v.scalar_tensor_tensor(out=hf, in0=hf, scalar=0.25, in1=hf, op0=ALU.mult, op1=ALU.mult))
            v.tensor_tensor(var, var, hf, ALU.add).then_inc(ln_var[i], 1)

        def one_over_sd(steps, i, c):
            v.wait_ge(ln_sd[i], c + 1)
            steps.done(v.reciprocal(rstd[:, :], rstd[:, :]))

        def normalise(i, c):
            for u in range(CHUNK):
                k = c * CHUNK + u
                v.tensor_scalar(rows[:, u, :], x_res[:, k, :], mean[:, u:u + 1], rstd[:, u:u + 1],
                                ALU.subtract, ALU.mult).then_inc(ln_row[i], 1)

        v.wait_ge(ld_x, 32)
        for k in range(TILES):
            ins = v.bn_stats(stats0[:, k, :], x_res[:, k, :])
        once.done(ins)
        row_variance(once, 0, stats0[:, :, :], mean0[:, :], rstd0[:, :], half0[:, :])
        v.wait_ge(hist_done, 1)
        v.tensor_scalar(dinv[:, :], ps[:, 6, 0:TILES], 1.0, None, ALU.add).then_inc(deg_in, 1)
        v.wait_ge(ln_sd[0], 1)
        v.reciprocal(rstd0[:, :], rstd0[:, :])
        v.wait_ge(deg_sd, 1)
        once.done(v.reciprocal(dinv[:, :], dinv[:, :]))
        once.done(v.tensor_tensor(rstd0[:, :], rstd0[:, :], dinv[:, :], ALU.mult))
        for k in range(TILES):
            v.tensor_scalar(xn[:, k, :], x_res[:, k, :], mean0[:, k:k + 1], rstd0[:, k:k + 1],
                            ALU.subtract, ALU.mult).then_inc(ln_row[0], 1)

        v.wait_ge(gspread_mm, 1)
        v.tensor_copy(base0[:, :], ps[:, 4, 0:GROUPS])
        once.done(v.tensor_copy(span_i[:, :], ps[:, 5, 0:GROUPS]))
        once.done(v.tensor_scalar(base_i[:, :], span_i[:, :], 7, None, ALU.arith_shift_right))
        once.done(v.tensor_copy(base_f[:, :], base_i[:, :]))
        once.done(v.tensor_reduce(npass_f[:, 0:1], base_f[:, :], AX_X, ALU.max))
        v.tensor_scalar(npass_f[:, 1:2], npass_f[:, 0:1], 0.0, None, ALU.is_equal)
        for c in range(CHUNKS - 1):
            once.done(v.tensor_reduce(npass_f[:, 2:3], base0[:, PROLOGUE * (c + 1):GROUPS], AX_X, ALU.min))
            once.done(v.tensor_scalar(npass_f[:, 2:3], npass_f[:, 2:3], float(CROWS * (c + 1)), None, ALU.is_ge))
            once.done(v.tensor_tensor(npass_f[:, 1:2], npass_f[:, 1:2], npass_f[:, 2:3], ALU.mult))
        v.tensor_copy(npass[:, 1:2], npass_f[:, 1:2])
        once.done(v.tensor_scalar(npass[:, 0:1], npass_f[:, 0:1], 1.0, None, ALU.add))
        v.sem_inc(plan_ready, 1)
        v.wait_ge(cols_copied, 2)
        v.scalar_tensor_tensor(out=idx_rel[:, 0:GROUPS, :], in0=src_f[:, :, :], scalar=float(RELS),
                               in1=column(2), op0=ALU.mult, op1=ALU.add).then_inc(rel_idx, 1)
        v.wait_ge(rel_idx, 1)
        v.tensor_copy(idx_ring[:, 3, :, :], idx_rel[:, 0:RING, :]).then_inc(idx_copied[3], RING)
        v.tensor_copy(idx_rel[:, GROUPS:, :], idx_rel[:, 0:RING, :])
        v.wait_ge(idx_made, 2)

        v.wait_ge(bn_tr, 1)
        once.done(v.tensor_copy(bnc[:, :, :, :].rearrange("p q n e -> p (q n e)"), ps[:, 5, 0:160]))
        v.tensor_scalar(bn_s[:, :, :], bnc[:, :, 4, :], BN_EPS, None, ALU.add).then_inc(bn_var, 1)
        v.wait_ge(bn_sd, 1)
        once.done(v.reciprocal(bn_s[:, :, :], bn_s[:, :, :]))
        once.done(v.tensor_tensor(bn_s[:, :, :], bn_s[:, :, :], bnc[:, :, 1, :], ALU.mult))
        once.done(v.tensor_tensor(bn_t[:, :, :], bnc[:, :, 0, :], bnc[:, :, 3, :], ALU.subtract))
        once.done(v.tensor_tensor(bn_t[:, :, :], bn_t[:, :, :], bn_s[:, :, :], ALU.mult))
        v.tensor_tensor(bn_t[:, :, :], bn_t[:, :, :], bnc[:, :, 2, :], ALU.add).then_inc(bn_ready, 1)

        passes = v.value_load(npass[0:1, 0:1], min_val=1, max_val=26)
        ordered = v.value_load(npass[0:1, 1:2], min_val=0, max_val=1)

        def onehots(l, n, t, s):
            v.wait_ge(group_mm[l], t + 1)
            if l < 3:
                ins = v.tensor_tensor(onehot[:, s % 2, :, :], rel_dst[:, n, :].unsqueeze(2).to_broadcast([P, GE, P]),
                                      iota_w[:, :].unsqueeze(1).to_broadcast([P, GE, P]), ALU.is_equal)
            else:
                for j in range(GE):
                    ins = v.tensor_scalar(onehot[:, s % 2, j, :], iota_w[:, :], rel_dst[:, n, j:j + 1],
                                          wgtc[:, n, j:j + 1], ALU.is_equal, ALU.mult)
            ins.then_inc(onehot_ready[l], 1)

        def add(l, n, t, s):
            first = v.value_load(base_i[0:1, bass.ds(n, 1)], min_val=0, max_val=ROWS)
            v.wait_ge(group_mm[l], t + 3)
            v.wait_ge(agg_added[l], t + 2)
            window = xt[:, :, bass.ds(first, P)]
            v.tensor_tensor(window, ps[:, 7, 0:D].rearrange("p (h n) -> p h n", h=HALVES),
                            window, ALU.add).then_inc(agg_added[l], 1)
            idx = idx_src if l < 3 else idx_rel
            v.tensor_copy(idx_ring[:, l, s % RING, :], idx[:, n + RING, :]).then_inc(idx_copied[l], 1)

        def set_window(l, m):
            v.wait_ge(pass_base[l], m * 3 + 1)
            v.tensor_copy(base_i[:, :], base_f[:, :]).then_inc(pass_base[l], 1)
            v.tensor_tensor(rel_dst[:, :, :], dstc[:, :, :],
                            base_f[:, :].unsqueeze(2).to_broadcast([P, GROUPS, GE]),
                            ALU.subtract).then_inc(pass_base[l], 1)

        def groups(l, turns, m):
            with v.Fori(0, turns) as i:
                for s in range(RING):
                    v.wait_ge(pass_base[l], m * 3 + 3)
                    onehots(l, i * RING + s, m * GROUPS + i * RING + s, s)
                    add(l, i * RING + s, m * GROUPS + i * RING + s, s)

        def prepare(l, t0, n):
            if not isinstance(t0, int) or t0 + n < GROUPS:
                onehots(l, t0 + n, t0 + n, n)

        def one_group(l, t0, n):
            prepare(l, t0, n + 1)
            add(l, t0 + n, t0 + n, n)

        def copy_sums(l, c):
            v.tensor_copy(xs[:, :, :], xt[:, :, bass.ds(c * CROWS, CROWS)]).then_inc(xs_copied, 1)

        def layer_row(l, c, u):
            k = c * CHUNK + u
            v.wait_ge(y_mm, c * UNITS + (l * CHUNKS * UNITS + u // 2 + 1))
            v.scalar_tensor_tensor(out=rows[:, u, :], in0=ps[:, 4 + u // 2, (u % 2) * D:(u % 2 + 1) * D],
                                   scalar=dinv[:, bass.ds(k, 1)], in1=gb[:, l, :],
                                   op0=ALU.mult, op1=ALU.add).then_inc(y_ev, 1)

        def gcn_chunk(l, c, _):
            v.wait_ge(tr_ev[l + 1], c * CHUNK + CHUNK)
            v.wait_ge(rows_free, c + (l * CHUNKS + 1))
            copy_sums(l, c)
            for u in range(CHUNK):
                layer_row(l, c, u)
            for u in range(CHUNK):
                k = c * CHUNK + u
                v.wait_ge(gelu_done, k + (l * TILES + 1))
                v.tensor_scalar(rows[:, u, :], rows[:, u, :], dinv[:, bass.ds(k, 1)], None,
                                ALU.mult).then_inc(row_ready, 1)

        def mix_chunk(l, c, first):
            before, steps_with, after = mix_plan(first[2])
            t0 = first[0]
            steps = Steps(v, mix_steps, c, 11)
            v.wait_ge(tr_ev[4], c * CHUNK + CHUNK)
            copy_sums(l, c)
            if before:
                one_group(l, t0, 0)
                prepare(l, t0, 2)
            for u in range(CHUNK):
                layer_row(l, c, u)
            for u in range(CHUNK):
                k = c * CHUNK + u
                v.wait_ge(y_ev, k + (l * TILES + CHUNK + 1))
                v.tensor_tensor(x_res[:, k, :], x_res[:, k, :], rows[:, u, :], ALU.add).then_inc(gcn_added, 1)
            if before:
                add(l, t0 + 1, t0 + 1, 1)
            v.wait_ge(gcn_added, c * CHUNK + CHUNK)
            row_moments(steps, x_res, c)
            row_variance(steps, 1)
            one_over_sd(steps, 1, c)
            normalise(1, c)
            if before:
                one_group(l, t0, 2)
            v.wait_ge(rout_mm, c + 1)
            logits = ps[:, 5, 0:CHUNK * E0].rearrange("p (t e) -> p t e", e=E0)
            prob, top = rout[:, :, :], rtmp[:, :]
            over = top.unsqueeze(2).to_broadcast([P, CHUNK, E0])
            steps.done(v.tensor_reduce(top, logits, AX_X, ALU.max))
            v.tensor_tensor(prob, logits, over, ALU.subtract).then_inc(rout_max, 1)
            v.wait_ge(rout_exp, c + 1)
            steps.done(v.tensor_reduce(top, prob, AX_X, ALU.add))
            steps.done(v.reciprocal(top, top))
            v.tensor_tensor(prob, prob, over, ALU.mult).then_inc(rout_ready, 1)
            v.wait_ge(rout_ready, c + 1)
            n0 = before + len(steps_with)
            for e in range(E0):
                t = c * E0 + e
                for u in range(CHUNK):
                    k = c * CHUNK + u
                    v.wait_ge(yo_ev, t * CHUNK + u + 1)
                    v.scalar_tensor_tensor(out=x_res[:, k, :], in0=bob[:, e, :], scalar=rout[:, u, e:e + 1],
                                           in1=x_res[:, k, :], op0=ALU.mult, op1=ALU.add).then_inc(bo_added, 1)
                if e in steps_with:
                    one_group(l, t0, before + steps_with.index(e))
                for u in range(CHUNK):
                    k = c * CHUNK + u
                    v.wait_ge(bo_added, t * CHUNK + u + 1)
                    v.wait_ge(yo_mm, t * UNITS + u // 2 + 1)
                    v.scalar_tensor_tensor(out=x_res[:, k, :], in0=ps[:, 4 + u // 2, (u % 2) * D:(u % 2 + 1) * D],
                                           scalar=rout[:, u, e:e + 1], in1=x_res[:, k, :],
                                           op0=ALU.mult, op1=ALU.add).then_inc(yo_ev, 1)
            v.wait_ge(yo_ev, (c * E0 + E0) * CHUNK + CHUNK)
            row_moments(steps, x_res, c)
            if after > 1:
                one_group(l, t0, n0)
            row_variance(steps, 2)
            if after > 1:
                prepare(l, t0, n0 + 2)
            one_over_sd(steps, 2, c)
            normalise(2, c)
            for n in range(n0 + 1 if after > 1 else n0, n0 + after):
                if n > n0 + 1:
                    prepare(l, t0, n + 1)
                add(l, t0 + n, t0 + n, n)
            steps.end()

        def back_chunk(l, c, first):
            t0, follows = first[0], first[2] > 0
            steps = Steps(v, back_steps, c, 4)
            copy_sums(l, c)
            if follows:
                one_group(l, t0, 0)
                prepare(l, t0, 2)
            for u in range(CHUNK):
                k = c * CHUNK + u
                v.wait_ge(back_mm, k + 1)
                v.scalar_tensor_tensor(out=x_res[:, k, :], in0=ps[:, u, 0:D], scalar=0.0, in1=x_res[:, k, :],
                                       op0=ALU.max, op1=ALU.add).then_inc(back_ev, 1)
            if follows:
                add(l, t0 + 1, t0 + 1, 1)
            v.wait_ge(back_ev, c * CHUNK + CHUNK)
            row_moments(steps, x_res, c)
            row_variance(steps, 3)
            if follows:
                one_group(l, t0, 2)
            one_over_sd(steps, 3, c)
            normalise(3, c)
            if follows:
                one_group(l, t0, 3)
            steps.end()

        def stage_of(l, chunk):
            v.tensor_copy(base_f[:, :], base0[:, :]).then_inc(pass_base[l], 1)
            with v.If_eq(v.to_reg(ordered), 1):
                set_window(l, 0)
                v.wait_ge(pass_base[l], 3)
                prepare(l, 0, 0)
                with v.Fori(0, PROLOGUE // RING) as i:
                    for s in range(RING):
                        one_group(l, i * RING, s)
                inside = {gcn_chunk: 0, mix_chunk: PROLOGUE, back_chunk: RING}[chunk]
                with v.Fori(0, 3) as c:
                    t0 = c * PROLOGUE + PROLOGUE
                    v.wait_ge(agg_added[l], t0 + 2)
                    chunk(l, c, (t0, 0, FOLLOW[0]))
                    if inside < PROLOGUE:
                        with v.Fori(0, (FOLLOW[0] - inside) // RING) as i:
                            for s in range(RING):
                                one_group(l, t0 + inside + i * RING, s)
                for c in (3, 4):
                    t0 = PROLOGUE * (c + 1) if c == 3 else GROUPS
                    v.wait_ge(agg_added[l], t0 + 2)
                    chunk(l, c, (t0, 0, FOLLOW[c]))
                    if not inside:
                        for s in range(FOLLOW[c]):
                            one_group(l, t0, s)
                v.sem_inc(agg_done, 1)
            with v.Else():
                with v.Fori(0, passes) as m:
                    set_window(l, m)
                    groups(l, GROUPS // RING, m)
                    v.tensor_scalar(base_f[:, :], base_f[:, :], float(P), float(ROWS), ALU.add,
                                    ALU.min).then_inc(pass_base[l], 1)
                with v.Fori(0, CHUNKS) as c:
                    v.wait_ge(agg_added[l], passes * GROUPS + 2)
                    chunk(l, c, (0, 0, 0))
                v.wait_ge(pass_base[l], passes * 3 + 1)
                v.sem_inc(agg_done, 1)

        v.wait_ge(tr_ev[0], CHUNK + TILES)
        stage_of(0, gcn_chunk)
        v.wait_ge(tr_ev[1], CHUNK + TILES)
        stage_of(1, gcn_chunk)
        v.wait_ge(tr_ev[2], CHUNK + TILES)
        v.wait_ge(ld_bo, 16)
        stage_of(2, mix_chunk)

        v.wait_ge(gate_ready, 1)

        def rel_evac(k, s):
            for r in range(1, RELS // 2, 2):
                v.wait_ge(rel_mm, k * 8 + r + 1)
                for q in range(2):
                    rel = 2 * r + q
                    ins = v.tensor_scalar(stage[:, s, rel, :], ps[:, 4 + r // 2, q * D:(q + 1) * D],
                                          gates[:, k, rel:rel + 1], None, ALU.mult)
                ins.then_inc(rel_ev_v, 1)

        rel_evac(0, 0)
        rel_evac(1, 1)
        with v.Fori(1, TILES // 2) as k2:
            for s in range(2):
                v.wait_ge(rel_out[s], k2 * 16)
                rel_evac(k2 * 2 + s, s)
        v.wait_ge(rel_out[0], (TILES // 2) * 16)
        rel_evac(TILES - 1, 0)
        v.wait_ge(xr_copied, TILES)
        once.done(v.memset(xt[:, :, :], 0.0))
        v.wait_ge(rel_out[0], 16 * (TILES // 2 + 1))
        v.wait_ge(rel_out[1], 16 * (TILES // 2))
        stage_of(3, back_chunk)

        v.wait_ge(mean_mm, CHUNKS + 1)
        v.tensor_scalar(mean_t[:, :], ps[:, 5:5 + HALVES, 0], 1.0 / N_NODES, None, ALU.mult).then_inc(mean_ev, 1)
        v.wait_ge(log_mm, 1)

        def row(i, n=E0, at=0):
            return small[:, i, at:at + n]

        def softmax(i):
            once.done(v.tensor_reduce(row(2, 1), row(1), AX_X, ALU.max))
            v.tensor_scalar(row(1), row(1), row(2, 1), None, ALU.subtract).then_inc(exp_in, 1)
            v.wait_ge(exp_out, i + 1)
            once.done(v.tensor_reduce(row(2, 1), row(1), AX_X, ALU.add))
            once.done(v.reciprocal(row(2, 1), row(2, 1)))
            once.done(v.tensor_scalar(row(1), row(1), row(2, 1), None, ALU.mult))

        once.done(v.tensor_tensor(row(1), ps[0:1, 6, 0:E0], row(0), ALU.add))
        softmax(0)
        once.done(v.tensor_scalar(row(3), row(1), float(N_NODES), CAPACITY, ALU.mult, ALU.max))
        once.done(v.reciprocal(row(3), row(3)))
        once.done(v.tensor_scalar(row(3), row(3), CAPACITY, None, ALU.mult))
        once.done(v.tensor_tensor(row(1), row(1), row(3), ALU.mult))
        softmax(1)
        v.tensor_scalar(row(6), iota8[:, :], -1.0, float(E0), ALU.mult, ALU.add)
        for s in range(TOP_K):
            once.done(v.tensor_reduce(row(4, 1, s), row(1), AX_X, ALU.max))
            once.done(v.tensor_scalar(row(5), row(1), row(4, 1, s), None, ALU.is_equal))
            once.done(v.tensor_tensor(row(5), row(5), row(6), ALU.mult))
            once.done(v.tensor_reduce(row(7, 1), row(5), AX_X, ALU.max))
            once.done(v.tensor_scalar(row(7, 1, 1 + s), row(7, 1), -1.0, float(E0), ALU.mult, ALU.add))
            once.done(v.tensor_scalar(row(5), iota8[:, :], row(7, 1, 1 + s), -2.0, ALU.is_equal, ALU.mult))
            once.done(v.tensor_tensor(row(1), row(1), row(5), ALU.add))
        v.tensor_copy(sel_i[:, 0:TOP_K], row(7, TOP_K, 1)).then_inc(sel_ready, 1)
        v.tensor_tensor(row(9, 1), row(4, 1, 1), row(4, 1, 0), ALU.subtract).then_inc(exp_in, 1)
        v.wait_ge(exp_out, 3)
        once.done(v.tensor_scalar(row(10, 1), row(9, 1), 1.0, None, ALU.add))
        once.done(v.reciprocal(row(8, 1), row(10, 1)))
        v.tensor_tensor(row(8, 1, 1), row(8, 1), row(9, 1), ALU.mult).then_inc(wsel_in, 1)
        v.wait_ge(wsel_in, 1)
        v.wait_ge(wsel_mm, 1)
        once.done(v.tensor_copy(wsel[:, :], ps[:, 6, 16:16 + TOP_K]))
        v.wait_ge(sel_tr, 1)
        v.tensor_copy(b1c[:, :, :].rearrange("p s f -> p (s f)"), ps[:, 7, 0:TOP_K * FT]).then_inc(sel_ev, 1)
        v.wait_ge(sel_ld2, 16 * 2 * TOP_K)
        for s in range(TOP_K):
            w = s2[:, s, :, :].rearrange("p k f -> p (k f)")
            v.tensor_scalar(w, w, wsel[:, s:s + 1], None, ALU.mult).then_inc(w2_scaled, 1)
        once.done(v.tensor_scalar(b2m[:, 0, :], b2s[:, 0, :], wsel[0:1, 0:1], None, ALU.mult))
        v.scalar_tensor_tensor(out=b2m[:, 1, :], in0=b2s[:, 1, :], scalar=wsel[0:1, 1:2], in1=b2m[:, 0, :],
                               op0=ALU.mult, op1=ALU.add).then_inc(b2_ready, 1)
        v.wait_ge(b2_mm, 1)
        v.tensor_copy(b2_all[:, :], ps[:, 7, 0:D]).then_inc(b2_copied, 1)
        with v.Fori(0, CHUNKS) as c:
            steps = Steps(v, out_steps, c, 4)
            for u in range(CHUNK):
                k = c * CHUNK + u
                v.wait_ge(fo_mm, c * UNITS + u // 2 + 1)
                v.wait_ge(b2_added, k + 1)
                v.tensor_tensor(xn[:, k, :], ps[:, 4 + u // 2, (u % 2) * D:(u % 2 + 1) * D], xn[:, k, :],
                                ALU.add).then_inc(fo_ev, 1)
            v.wait_ge(fo_ev, c * CHUNK + 2 * CHUNK)
            row_moments(steps, xn, c)
            row_variance(steps, 4)
            one_over_sd(steps, 4, c)
            v.wait_ge(beta_added, c * CHUNK + CHUNK)
            for u in range(CHUNK):
                k = c * CHUNK + u
                v.scalar_tensor_tensor(out=xn[:, k, :], in0=xn[:, k, :], scalar=mean[:, u:u + 1],
                                       in1=gam[:, :], op0=ALU.subtract, op1=ALU.mult).then_inc(fin_scaled, 1)
            for u in range(CHUNK):
                k = c * CHUNK + u
                v.wait_ge(fin_scaled, k + 1)
                v.scalar_tensor_tensor(out=x_res[:, k, :], in0=xn[:, k, :], scalar=rstd[:, u:u + 1],
                                       in1=x_res[:, k, :], op0=ALU.mult, op1=ALU.add).then_inc(fin_ready, 1)
            steps.end()


_INS = ["x", "src", "dst", "edge_type_16", "edge_weight1",
        "L0_gnn_W1", "L0_gnn_b1", "L0_gnn_W2", "L0_gnn_b2", "L0_gnn_W3", "L0_gnn_b3",
        "L0_ffn_Wr", "L0_ffn_br", "L0_ffn_W1", "L0_ffn_b1", "L0_ffn_g1", "L0_ffn_be1", "L0_ffn_m1", "L0_ffn_v1",
        "L0_ffn_W2", "L0_ffn_b2", "L0_ffn_g2", "L0_ffn_be2", "L0_ffn_m2", "L0_ffn_v2", "L0_ffn_Wo", "L0_ffn_bo",
        "L1_gnn_weight", "L1_gnn_gate_weight",
        "L1_ffn_Wr", "L1_ffn_br", "L1_ffn_W1", "L1_ffn_b1", "L1_ffn_W2", "L1_ffn_b2", "L1_ffn_gamma", "L1_ffn_beta"]


def kernel(**inputs):
    import numpy as np
    import concourse.bacc as bacc
    from concourse.bass_utils import run_bass_kernel_spmd

    nc = bacc.Bacc("TRN2", target_bir_lowering=False, num_devices=1)
    arrays, aps = {}, {}
    for name in _INS:
        arr = np.ascontiguousarray(inputs[name])
        arrays["in_" + name] = arr
        aps[name] = nc.dram_tensor("in_" + name, arr.shape, mybir.dt.from_np(arr.dtype), kind="ExternalInput").ap()
    result = nc.dram_tensor("result", (N_NODES, D), F32, kind="ExternalOutput").ap()
    build(nc, aps, result)
    r = run_bass_kernel_spmd(nc, [arrays], core_ids=[0])
    return r.results[0]["result"]
```
